# Optimizing a Trainium2 kernel written in Bass

```python
import numpy as np
import jax
import jax.numpy as jnp

def _softmax(x, axis=-1):
    return jax.nn.softmax(x, axis=axis)
def _gelu(x):
    return jax.nn.gelu(x, approximate=True)
def _silu(x):
    return jax.nn.silu(x)
def _sigmoid(x):
    return jax.nn.sigmoid(x)
def _layernorm(x, axis=-1, eps=1e-5):
    m = jnp.mean(x, axis=axis, keepdims=True)
    v = jnp.var(x, axis=axis, keepdims=True)
    return (x - m) / jnp.sqrt(v + eps)
def _scatter_add(tgt, idx, src, axis=0):
    return tgt.at[idx].add(src)
def _segment_sum(src, seg, n):
    return jax.ops.segment_sum(src, seg, n)

kernel_name = 'mk_conv_attn_hybrid_d4_conv_nchw256_880e36'

def setup_inputs(seed: int = 0):
    np.random.seed(seed)
    _w = jnp.asarray
    def _rec_inputs():
        import jax
        import jax.numpy as jnp
        _gk = jax.random.key(seed)
        x = -0.0009438 + 1 * jax.random.normal(jax.random.fold_in(_gk, 1), (2, 256, 48, 48), jnp.float32)
        return x
    x = _rec_inputs()
    def _L0_conv_setup():
        import jax, jax.numpy as jnp
        from jax import lax
        import numpy as np
        D_STATE = 16
        D_CONV = 4
        EXPAND = 2
        DT_RANK = 16
        LN_EPS = 1e-05

        def _layernorm(x, g, b):
            m = jnp.mean(x, axis=-1, keepdims=True)
            v = jnp.mean(jnp.square(x - m), axis=-1, keepdims=True)
            return (x - m) * lax.rsqrt(v + LN_EPS) * g + b

        def _selective_scan(u, delta, A, Bm, Cm, D):
            Bsz, L, d = u.shape
            h0 = jnp.zeros((Bsz, d, A.shape[1]), u.dtype)

            def step(h, xs):
                d_t, B_t, C_t, u_t = xs
                dA = jnp.exp(d_t[..., None] * A)
                h = dA * h + (d_t * u_t)[..., None] * B_t[:, None, :]
                y = jnp.einsum('bdn,bn->bd', h, C_t)
                return (h, y)
            xs = (delta.transpose(1, 0, 2), Bm.transpose(1, 0, 2), Cm.transpose(1, 0, 2), u.transpose(1, 0, 2))
            _, ys = lax.scan(step, h0, xs)
            return ys.transpose(1, 0, 2) + u * D

        def _mamba_branch(xi, z, conv_w, conv_b, xproj_w, dtproj_w, dtproj_b, A_log, D):
            Bsz, L, d = xi.shape
            xt = jnp.pad(xi.transpose(0, 2, 1), ((0, 0), (0, 0), (D_CONV - 1, 0)))
            xc = lax.conv_general_dilated(xt, conv_w[:, None, :], (1,), 'VALID', feature_group_count=d, dimension_numbers=('NCH', 'OIH', 'NCH'))
            xs = jax.nn.silu(xc + conv_b[None, :, None]).transpose(0, 2, 1)
            proj = xs @ xproj_w.T
            dt = jax.nn.softplus(proj[..., :DT_RANK] @ dtproj_w.T + dtproj_b)
            Bm = proj[..., DT_RANK:DT_RANK + D_STATE]
            Cm = proj[..., DT_RANK + D_STATE:]
            A = -jnp.exp(A_log)
            y = _selective_scan(xs, dt, A, Bm, Cm, D)
            return y * jax.nn.silu(z)
        key = jax.random.key(seed)
        ks = jax.random.split(key, 24)
        B, C, H, W = (2, 256, 48, 48)
        d_inner = EXPAND * C

        def nrm(k, shape, s=0.02):
            return jax.random.normal(k, shape, jnp.float32) * s
        inp = {'x': jax.random.normal(ks[0], (B, C, H, W), jnp.float32), 'ln_g': jnp.ones((C,), jnp.float32), 'ln_b': jnp.zeros((C,), jnp.float32), 'pos_scale': jnp.ones((1,), jnp.float32), 'in_proj_w': nrm(ks[1], (2 * d_inner, C)), 'out_proj_w': nrm(ks[2], (C, d_inner))}
        for i, s in enumerate(['f', 'b']):
            base = 3 + i * 7
            inp[f'conv_w_{s}'] = nrm(ks[base], (d_inner, D_CONV), 0.1)
            inp[f'conv_b_{s}'] = nrm(ks[base + 1], (d_inner,), 0.1)
            inp[f'xproj_w_{s}'] = nrm(ks[base + 2], (DT_RANK + 2 * D_STATE, d_inner))
            inp[f'dtproj_w_{s}'] = nrm(ks[base + 3], (d_inner, DT_RANK), 0.1)
            inp[f'dtproj_b_{s}'] = jax.random.uniform(ks[base + 4], (d_inner,), jnp.float32, -4.0, -2.0)
            inp[f'A_log_{s}'] = jnp.log(jnp.tile(jnp.arange(1, D_STATE + 1, dtype=jnp.float32), (d_inner, 1)))
            inp[f'D_{s}'] = jnp.ones((d_inner,), jnp.float32)
        return inp
    _L0_conv_all = _L0_conv_setup()
    _L0_conv_in = {k: v for k, v in _L0_conv_all.items() if k in ('ln_g', 'ln_b', 'pos_scale', 'in_proj_w', 'out_proj_w', 'conv_w_f', 'conv_b_f', 'xproj_w_f', 'dtproj_w_f', 'dtproj_b_f', 'A_log_f', 'D_f', 'conv_w_b', 'conv_b_b', 'xproj_w_b', 'dtproj_w_b', 'dtproj_b_b', 'A_log_b', 'D_b', )}
    del _L0_conv_all

    def _L1_conv_setup():
        import jax, jax.numpy as jnp
        import numpy as np
        B, C, H, W = (8, 256, 64, 64)
        NH = 8
        CM = 2048
        EPS = 1e-05

        def _repbn(x, g, b, m, v, alpha):
            bn = (x - m) * jax.lax.rsqrt(v + EPS) * g + b
            return bn + alpha * x
        key = jax.random.key(seed)
        ks = jax.random.split(key, 16)
        n = lambda k, s: jax.random.normal(k, s, dtype=jnp.float32) * 0.02
        return {'x': jax.random.normal(ks[0], (B, C, H, W), dtype=jnp.float32), 'Wqkv': n(ks[1], (C, 3 * C)), 'bqkv': n(ks[2], (3 * C,)), 'dw_w': n(ks[3], (C, 1, 3, 3)), 'dw_b': n(ks[4], (C,)), 'Wproj': n(ks[5], (C, C)), 'bproj': n(ks[6], (C,)), 'bn1_g': jnp.ones((C,), jnp.float32), 'bn1_b': jnp.zeros((C,), jnp.float32), 'bn1_m': n(ks[7], (C,)), 'bn1_v': jax.random.uniform(ks[8], (C,), dtype=jnp.float32) + 0.5, 'alpha1': jnp.ones((1,), jnp.float32), 'Wfc1': n(ks[9], (C, CM)), 'bfc1': n(ks[10], (CM,)), 'Wfc2': n(ks[11], (CM, C)), 'bfc2': n(ks[12], (C,)), 'bn2_g': jnp.ones((C,), jnp.float32), 'bn2_b': jnp.zeros((C,), jnp.float32), 'bn2_m': n(ks[13], (C,)), 'bn2_v': jax.random.uniform(ks[14], (C,), dtype=jnp.float32) + 0.5, 'alpha2': jnp.ones((1,), jnp.float32)}
    _L1_conv_all = _L1_conv_setup()
    _L1_conv_in = {k: v for k, v in _L1_conv_all.items() if k in ('Wqkv', 'bqkv', 'dw_w', 'dw_b', 'Wproj', 'bproj', 'bn1_g', 'bn1_b', 'bn1_m', 'bn1_v', 'alpha1', 'Wfc1', 'bfc1', 'Wfc2', 'bfc2', 'bn2_g', 'bn2_b', 'bn2_m', 'bn2_v', 'alpha2', )}
    del _L1_conv_all

    def _L2_attn_setup():
        import jax, jax.numpy as jnp
        import numpy as np
        IN_CHANNELS = 256
        SCALE = IN_CHANNELS ** (-0.5)
        key = jax.random.key(seed)
        k_x, k_we, k_wo = jax.random.split(key, 3)
        B, M, C, H3, NH = (4, 12288, 256, 768, 3)
        x = jax.random.normal(k_x, (B, M, C), dtype=jnp.float32)
        W_embed = jax.random.normal(k_we, (NH, H3, C), dtype=jnp.float32) * 0.01
        b_embed = jnp.zeros((NH, H3), dtype=jnp.float32)
        W_out = jax.random.normal(k_wo, (C, H3), dtype=jnp.float32) * 0.01
        b_out = jnp.zeros((C,), dtype=jnp.float32)
        return {'x': x, 'W_embed': W_embed, 'b_embed': b_embed, 'W_out': W_out, 'b_out': b_out}
    _L2_attn_all = _L2_attn_setup()
    _L2_attn_in = {k: v for k, v in _L2_attn_all.items() if k in ('W_embed', 'b_embed', 'W_out', 'b_out', )}
    del _L2_attn_all

    def _L2_ffn_setup():
        import jax, jax.numpy as jnp
        import numpy as np
        B, N, D = (16, 4096, 256)
        NUM_EXPERTS, TOP_K, HEADS = (4, 2, 4)
        N_EDGES = 1048576
        LN_EPS = 1e-05

        def _layernorm(x, g, b):
            mu = x.mean(-1, keepdims=True)
            var = ((x - mu) ** 2).mean(-1, keepdims=True)
            return (x - mu) * jax.lax.rsqrt(var + LN_EPS) * g + b

        def _forward(x, edge_index, W_gat, att_src, att_dst, b_gat, ln_gamma, ln_beta, W1, b1, W2, b2):
            Bc, Nc, Dc = x.shape
            M = Bc * Nc
            x_flat = x.reshape(M, Dc)
            h = (x_flat @ W_gat).reshape(M, HEADS, NUM_EXPERTS)
            loops = jnp.arange(M, dtype=edge_index.dtype)
            src = jnp.concatenate([edge_index[0], loops])
            dst = jnp.concatenate([edge_index[1], loops])
            a_src = (h * att_src).sum(-1)
            a_dst = (h * att_dst).sum(-1)
            e = jax.nn.leaky_relu(a_src[src] + a_dst[dst], negative_slope=0.2)
            e_max = jax.ops.segment_max(e, dst, num_segments=M)
            ee = jnp.exp(e - e_max[dst])
            denom = jax.ops.segment_sum(ee, dst, num_segments=M)
            alpha = ee / (denom[dst] + 1e-16)
            msg = h[src] * alpha[:, :, None]
            agg = jax.ops.segment_sum(msg, dst, num_segments=M).reshape(M, HEADS * NUM_EXPERTS) + b_gat
            scores = _layernorm(agg, ln_gamma, ln_beta).reshape(M, HEADS, NUM_EXPERTS).mean(1)
            scores = scores.reshape(Bc, Nc, NUM_EXPERTS)
            topk_s, topk_i = jax.lax.top_k(scores, TOP_K)
            w = jax.nn.softmax(topk_s, axis=-1)
            out = jnp.zeros_like(x)
            for ei in range(NUM_EXPERTS):
                g = jnp.where(topk_i == ei, w, 0.0).sum(-1)
                hh = jax.nn.gelu(x @ W1[ei] + b1[ei], approximate=False)
                out = out + g[..., None] * (hh @ W2[ei] + b2[ei])
            return out
        key = jax.random.key(seed)
        ks = jax.random.split(key, 8)
        s = 0.05
        return {'x': jax.random.normal(ks[0], (B, N, D), jnp.float32), 'W_gat': jax.random.normal(ks[1], (D, HEADS * NUM_EXPERTS), jnp.float32) * s, 'att_src': jax.random.normal(ks[2], (HEADS, NUM_EXPERTS), jnp.float32) * s, 'att_dst': jax.random.normal(ks[3], (HEADS, NUM_EXPERTS), jnp.float32) * s, 'b_gat': jnp.zeros((HEADS * NUM_EXPERTS,), jnp.float32), 'ln_gamma': jnp.ones((HEADS * NUM_EXPERTS,), jnp.float32), 'ln_beta': jnp.zeros((HEADS * NUM_EXPERTS,), jnp.float32), 'W1': jax.random.normal(ks[4], (NUM_EXPERTS, D, 2 * D), jnp.float32) * s, 'b1': jnp.zeros((NUM_EXPERTS, 2 * D), jnp.float32), 'W2': jax.random.normal(ks[5], (NUM_EXPERTS, 2 * D, D), jnp.float32) * s, 'b2': jnp.zeros((NUM_EXPERTS, D), jnp.float32), 'edge_index': jax.random.randint(ks[6], (2, N_EDGES), 0, B * N, jnp.int32)}
    _L2_ffn_all = _L2_ffn_setup()
    _L2_ffn_in = {k: v for k, v in _L2_ffn_all.items() if k in ('W_gat', 'att_src', 'att_dst', 'b_gat', 'ln_gamma', 'ln_beta', 'W1', 'b1', 'W2', 'b2', 'edge_index', )}
    del _L2_ffn_all

    def _L3_attn_setup():
        import jax, jax.numpy as jnp
        import numpy as np
        key = jax.random.key(seed)
        k1, k2 = jax.random.split(key)
        B, N, D = (4, 4096, 256)
        inp = jax.random.normal(k1, (B, N, D), dtype=jnp.float32)
        q_weight = jax.random.normal(k2, (D, D), dtype=jnp.float32)
        return {'input': inp, 'q_weight': q_weight}
    _L3_attn_all = _L3_attn_setup()
    _L3_attn_in = {k: v for k, v in _L3_attn_all.items() if k in ('q_weight', )}
    del _L3_attn_all

    def _L3_ffn_setup():
        import math
        import jax, jax.numpy as jnp
        import numpy as np
        CAPACITY_FACTOR = 1.25
        key = jax.random.key(seed)
        ks = jax.random.split(key, 5)
        B, L, D, F, E = (8, 8192, 256, 1024, 8)
        h = jax.random.normal(ks[0], (B, L, D), dtype=jnp.float32)
        gate_w = jax.random.normal(ks[1], (D, E), dtype=jnp.float32) * 0.02
        gate_b = jnp.zeros((E,), dtype=jnp.float32)
        w1 = jax.random.normal(ks[2], (E, D, F), dtype=jnp.float32) * (1.0 / math.sqrt(D))
        b1 = jnp.zeros((E, F), dtype=jnp.float32)
        w2 = jax.random.normal(ks[3], (E, F, D), dtype=jnp.float32) * (1.0 / math.sqrt(F))
        b2 = jnp.zeros((E, D), dtype=jnp.float32)
        return {'h': h, 'gate_w': gate_w, 'gate_b': gate_b, 'w1': w1, 'b1': b1, 'w2': w2, 'b2': b2}
    _L3_ffn_all = _L3_ffn_setup()
    _L3_ffn_in = {k: v for k, v in _L3_ffn_all.items() if k in ('gate_w', 'gate_b', 'w1', 'b1', 'w2', 'b2', )}
    del _L3_ffn_all

    return {
        "x": x,
        "L0_conv_ln_g": _L0_conv_in["ln_g"],
        "L0_conv_ln_b": _L0_conv_in["ln_b"],
        "L0_conv_pos_scale": _L0_conv_in["pos_scale"],
        "L0_conv_in_proj_w": _L0_conv_in["in_proj_w"],
        "L0_conv_out_proj_w": _L0_conv_in["out_proj_w"],
        "L0_conv_conv_w_f": _L0_conv_in["conv_w_f"],
        "L0_conv_conv_b_f": _L0_conv_in["conv_b_f"],
        "L0_conv_xproj_w_f": _L0_conv_in["xproj_w_f"],
        "L0_conv_dtproj_w_f": _L0_conv_in["dtproj_w_f"],
        "L0_conv_dtproj_b_f": _L0_conv_in["dtproj_b_f"],
        "L0_conv_A_log_f": _L0_conv_in["A_log_f"],
        "L0_conv_D_f": _L0_conv_in["D_f"],
        "L0_conv_conv_w_b": _L0_conv_in["conv_w_b"],
        "L0_conv_conv_b_b": _L0_conv_in["conv_b_b"],
        "L0_conv_xproj_w_b": _L0_conv_in["xproj_w_b"],
        "L0_conv_dtproj_w_b": _L0_conv_in["dtproj_w_b"],
        "L0_conv_dtproj_b_b": _L0_conv_in["dtproj_b_b"],
        "L0_conv_A_log_b": _L0_conv_in["A_log_b"],
        "L0_conv_D_b": _L0_conv_in["D_b"],
        "L1_conv_Wqkv": _L1_conv_in["Wqkv"],
        "L1_conv_bqkv": _L1_conv_in["bqkv"],
        "L1_conv_dw_w": _L1_conv_in["dw_w"],
        "L1_conv_dw_b": _L1_conv_in["dw_b"],
        "L1_conv_Wproj": _L1_conv_in["Wproj"],
        "L1_conv_bproj": _L1_conv_in["bproj"],
        "L1_conv_bn1_g": _L1_conv_in["bn1_g"],
        "L1_conv_bn1_b": _L1_conv_in["bn1_b"],
        "L1_conv_bn1_m": _L1_conv_in["bn1_m"],
        "L1_conv_bn1_v": _L1_conv_in["bn1_v"],
        "L1_conv_alpha1": _L1_conv_in["alpha1"],
        "L1_conv_Wfc1": _L1_conv_in["Wfc1"],
        "L1_conv_bfc1": _L1_conv_in["bfc1"],
        "L1_conv_Wfc2": _L1_conv_in["Wfc2"],
        "L1_conv_bfc2": _L1_conv_in["bfc2"],
        "L1_conv_bn2_g": _L1_conv_in["bn2_g"],
        "L1_conv_bn2_b": _L1_conv_in["bn2_b"],
        "L1_conv_bn2_m": _L1_conv_in["bn2_m"],
        "L1_conv_bn2_v": _L1_conv_in["bn2_v"],
        "L1_conv_alpha2": _L1_conv_in["alpha2"],
        "L2_attn_W_embed": _L2_attn_in["W_embed"],
        "L2_attn_b_embed": _L2_attn_in["b_embed"],
        "L2_attn_W_out": _L2_attn_in["W_out"],
        "L2_attn_b_out": _L2_attn_in["b_out"],
        "L2_ffn_W_gat": _L2_ffn_in["W_gat"],
        "L2_ffn_att_src": _L2_ffn_in["att_src"],
        "L2_ffn_att_dst": _L2_ffn_in["att_dst"],
        "L2_ffn_b_gat": _L2_ffn_in["b_gat"],
        "L2_ffn_ln_gamma": _L2_ffn_in["ln_gamma"],
        "L2_ffn_ln_beta": _L2_ffn_in["ln_beta"],
        "L2_ffn_W1": _L2_ffn_in["W1"],
        "L2_ffn_b1": _L2_ffn_in["b1"],
        "L2_ffn_W2": _L2_ffn_in["W2"],
        "L2_ffn_b2": _L2_ffn_in["b2"],
        "L2_ffn_edge_index": _L2_ffn_in["edge_index"],
        "L3_attn_q_weight": _L3_attn_in["q_weight"],
        "L3_ffn_gate_w": _L3_ffn_in["gate_w"],
        "L3_ffn_gate_b": _L3_ffn_in["gate_b"],
        "L3_ffn_w1": _L3_ffn_in["w1"],
        "L3_ffn_b1": _L3_ffn_in["b1"],
        "L3_ffn_w2": _L3_ffn_in["w2"],
        "L3_ffn_b2": _L3_ffn_in["b2"],
    }

def reference(x, L0_conv_ln_g, L0_conv_ln_b, L0_conv_pos_scale, L0_conv_in_proj_w, L0_conv_out_proj_w, L0_conv_conv_w_f, L0_conv_conv_b_f, L0_conv_xproj_w_f, L0_conv_dtproj_w_f, L0_conv_dtproj_b_f, L0_conv_A_log_f, L0_conv_D_f, L0_conv_conv_w_b, L0_conv_conv_b_b, L0_conv_xproj_w_b, L0_conv_dtproj_w_b, L0_conv_dtproj_b_b, L0_conv_A_log_b, L0_conv_D_b, L1_conv_Wqkv, L1_conv_bqkv, L1_conv_dw_w, L1_conv_dw_b, L1_conv_Wproj, L1_conv_bproj, L1_conv_bn1_g, L1_conv_bn1_b, L1_conv_bn1_m, L1_conv_bn1_v, L1_conv_alpha1, L1_conv_Wfc1, L1_conv_bfc1, L1_conv_Wfc2, L1_conv_bfc2, L1_conv_bn2_g, L1_conv_bn2_b, L1_conv_bn2_m, L1_conv_bn2_v, L1_conv_alpha2, L2_attn_W_embed, L2_attn_b_embed, L2_attn_W_out, L2_attn_b_out, L2_ffn_W_gat, L2_ffn_att_src, L2_ffn_att_dst, L2_ffn_b_gat, L2_ffn_ln_gamma, L2_ffn_ln_beta, L2_ffn_W1, L2_ffn_b1, L2_ffn_W2, L2_ffn_b2, L2_ffn_edge_index, L3_attn_q_weight, L3_ffn_gate_w, L3_ffn_gate_b, L3_ffn_w1, L3_ffn_b1, L3_ffn_w2, L3_ffn_b2):
    import jax
    import jax.numpy as jnp
    def _L0_conv_ref(x, ln_g, ln_b, pos_scale, in_proj_w, out_proj_w, conv_w_f, conv_b_f, xproj_w_f, dtproj_w_f, dtproj_b_f, A_log_f, D_f, conv_w_b, conv_b_b, xproj_w_b, dtproj_w_b, dtproj_b_b, A_log_b, D_b):
        import jax, jax.numpy as jnp
        from jax import lax
        import numpy as np
        D_STATE = 16
        D_CONV = 4
        EXPAND = 2
        DT_RANK = 16
        LN_EPS = 1e-05

        def _layernorm(x, g, b):
            m = jnp.mean(x, axis=-1, keepdims=True)
            v = jnp.mean(jnp.square(x - m), axis=-1, keepdims=True)
            return (x - m) * lax.rsqrt(v + LN_EPS) * g + b

        def _selective_scan(u, delta, A, Bm, Cm, D):
            Bsz, L, d = u.shape
            h0 = jnp.zeros((Bsz, d, A.shape[1]), u.dtype)

            def step(h, xs):
                d_t, B_t, C_t, u_t = xs
                dA = jnp.exp(d_t[..., None] * A)
                h = dA * h + (d_t * u_t)[..., None] * B_t[:, None, :]
                y = jnp.einsum('bdn,bn->bd', h, C_t)
                return (h, y)
            xs = (delta.transpose(1, 0, 2), Bm.transpose(1, 0, 2), Cm.transpose(1, 0, 2), u.transpose(1, 0, 2))
            _, ys = lax.scan(step, h0, xs)
            return ys.transpose(1, 0, 2) + u * D

        def _mamba_branch(xi, z, conv_w, conv_b, xproj_w, dtproj_w, dtproj_b, A_log, D):
            Bsz, L, d = xi.shape
            xt = jnp.pad(xi.transpose(0, 2, 1), ((0, 0), (0, 0), (D_CONV - 1, 0)))
            xc = lax.conv_general_dilated(xt, conv_w[:, None, :], (1,), 'VALID', feature_group_count=d, dimension_numbers=('NCH', 'OIH', 'NCH'))
            xs = jax.nn.silu(xc + conv_b[None, :, None]).transpose(0, 2, 1)
            proj = xs @ xproj_w.T
            dt = jax.nn.softplus(proj[..., :DT_RANK] @ dtproj_w.T + dtproj_b)
            Bm = proj[..., DT_RANK:DT_RANK + D_STATE]
            Cm = proj[..., DT_RANK + D_STATE:]
            A = -jnp.exp(A_log)
            y = _selective_scan(xs, dt, A, Bm, Cm, D)
            return y * jax.nn.silu(z)
        B, C, H, W = x.shape
        L = H * W
        seq = x.reshape(B, C, L).transpose(0, 2, 1)
        inv_freq = 1.0 / 10000.0 ** (jnp.arange(0, C, 2, dtype=jnp.float32) / C)
        t = jnp.arange(L, dtype=jnp.float32)
        sinu = t[:, None] * inv_freq[None, :]
        pos = jnp.concatenate([jnp.sin(sinu), jnp.cos(sinu)], axis=-1) * pos_scale
        h = _layernorm(seq, ln_g, ln_b) + pos
        xz = h @ in_proj_w.T
        d_inner = xz.shape[-1] // 2
        xi, z = (xz[..., :d_inner], xz[..., d_inner:])
        y_f = _mamba_branch(xi, z, conv_w_f, conv_b_f, xproj_w_f, dtproj_w_f, dtproj_b_f, A_log_f, D_f)
        y_b = _mamba_branch(xi[:, ::-1], z[:, ::-1], conv_w_b, conv_b_b, xproj_w_b, dtproj_w_b, dtproj_b_b, A_log_b, D_b)[:, ::-1]
        y = (y_f + y_b) @ out_proj_w.T
        out = seq + y
        return out.transpose(0, 2, 1).reshape(B, C, H, W)

    def _L1_conv_ref(x, Wqkv, bqkv, dw_w, dw_b, Wproj, bproj, bn1_g, bn1_b, bn1_m, bn1_v, alpha1, Wfc1, bfc1, Wfc2, bfc2, bn2_g, bn2_b, bn2_m, bn2_v, alpha2):
        import jax, jax.numpy as jnp
        import numpy as np
        B, C, H, W = (8, 256, 64, 64)
        NH = 8
        CM = 2048
        EPS = 1e-05

        def _repbn(x, g, b, m, v, alpha):
            bn = (x - m) * jax.lax.rsqrt(v + EPS) * g + b
            return bn + alpha * x
        b, c, h, w = x.shape
        n = h * w
        hd = c // NH
        scale = hd ** (-0.5)
        t = x.reshape(b, c, n).transpose(0, 2, 1)
        qkv = (t @ Wqkv + bqkv).reshape(b, n, 3, NH, hd).transpose(2, 0, 3, 1, 4)
        q, k, v = (qkv[0], qkv[1], qkv[2])
        q = jax.nn.relu(q) * scale
        k = jax.nn.relu(k)
        ctx = jnp.einsum('bhnd,bhne->bhde', k, v)
        out = jnp.einsum('bhnd,bhde->bhne', q, ctx)
        out = out.transpose(0, 2, 1, 3).reshape(b, n, c)
        img = out.transpose(0, 2, 1).reshape(b, c, h, w)
        img = jax.lax.conv_general_dilated(img, dw_w, (1, 1), 'SAME', feature_group_count=c)
        img = img + dw_b[None, :, None, None]
        out = img.reshape(b, c, n).transpose(0, 2, 1)
        out = out @ Wproj + bproj
        t = _repbn(t + out, bn1_g, bn1_b, bn1_m, bn1_v, alpha1)
        ff = jax.nn.gelu(t @ Wfc1 + bfc1, approximate=False) @ Wfc2 + bfc2
        t = _repbn(t + ff, bn2_g, bn2_b, bn2_m, bn2_v, alpha2)
        return t.transpose(0, 2, 1).reshape(b, c, h, w)

    def _L2_attn_ref(x, W_embed, b_embed, W_out, b_out):
        import jax, jax.numpy as jnp
        import numpy as np
        IN_CHANNELS = 256
        SCALE = IN_CHANNELS ** (-0.5)
        def head(W, b):
            e = jnp.einsum('bmc,hc->bmh', x, W) + b
            q, k, v = jnp.split(e, 3, axis=1)
            attn = jax.nn.softmax(jnp.einsum('bmd,bnd->bmn', q, k) * SCALE, axis=-1)
            return jnp.einsum('bmn,bnd->bmd', attn, v)
        outs = jax.vmap(head)(W_embed, b_embed)
        qkv = jnp.concatenate([outs[i] for i in range(outs.shape[0])], axis=1)
        out = jnp.einsum('bmd,cd->bmc', qkv, W_out) + b_out
        return out + x

    def _L2_ffn_ref(x, W_gat, att_src, att_dst, b_gat, ln_gamma, ln_beta, W1, b1, W2, b2, edge_index):
        import jax, jax.numpy as jnp
        import numpy as np
        B, N, D = (16, 4096, 256)
        NUM_EXPERTS, TOP_K, HEADS = (4, 2, 4)
        N_EDGES = 1048576
        LN_EPS = 1e-05

        def _layernorm(x, g, b):
            mu = x.mean(-1, keepdims=True)
            var = ((x - mu) ** 2).mean(-1, keepdims=True)
            return (x - mu) * jax.lax.rsqrt(var + LN_EPS) * g + b

        def _forward(x, edge_index, W_gat, att_src, att_dst, b_gat, ln_gamma, ln_beta, W1, b1, W2, b2):
            Bc, Nc, Dc = x.shape
            M = Bc * Nc
            x_flat = x.reshape(M, Dc)
            h = (x_flat @ W_gat).reshape(M, HEADS, NUM_EXPERTS)
            loops = jnp.arange(M, dtype=edge_index.dtype)
            src = jnp.concatenate([edge_index[0], loops])
            dst = jnp.concatenate([edge_index[1], loops])
            a_src = (h * att_src).sum(-1)
            a_dst = (h * att_dst).sum(-1)
            e = jax.nn.leaky_relu(a_src[src] + a_dst[dst], negative_slope=0.2)
            e_max = jax.ops.segment_max(e, dst, num_segments=M)
            ee = jnp.exp(e - e_max[dst])
            denom = jax.ops.segment_sum(ee, dst, num_segments=M)
            alpha = ee / (denom[dst] + 1e-16)
            msg = h[src] * alpha[:, :, None]
            agg = jax.ops.segment_sum(msg, dst, num_segments=M).reshape(M, HEADS * NUM_EXPERTS) + b_gat
            scores = _layernorm(agg, ln_gamma, ln_beta).reshape(M, HEADS, NUM_EXPERTS).mean(1)
            scores = scores.reshape(Bc, Nc, NUM_EXPERTS)
            topk_s, topk_i = jax.lax.top_k(scores, TOP_K)
            w = jax.nn.softmax(topk_s, axis=-1)
            out = jnp.zeros_like(x)
            for ei in range(NUM_EXPERTS):
                g = jnp.where(topk_i == ei, w, 0.0).sum(-1)
                hh = jax.nn.gelu(x @ W1[ei] + b1[ei], approximate=False)
                out = out + g[..., None] * (hh @ W2[ei] + b2[ei])
            return out
        return _forward(x, edge_index, W_gat, att_src, att_dst, b_gat, ln_gamma, ln_beta, W1, b1, W2, b2)

    def _L3_attn_ref(input, q_weight):
        import jax, jax.numpy as jnp
        import numpy as np
        query = jnp.einsum('bnd,de->bne', input, q_weight)
        att = jax.nn.sigmoid(jnp.einsum('bnd,bmd->bnm', query, input))
        value = jnp.einsum('bnm,bmd->bnd', att, input)
        return value

    def _L3_ffn_ref(h, gate_w, gate_b, w1, b1, w2, b2):
        import math
        import jax, jax.numpy as jnp
        import numpy as np
        CAPACITY_FACTOR = 1.25
        B, L, D = h.shape
        E = gate_w.shape[1]
        T = B * L
        C = max(1, math.ceil(CAPACITY_FACTOR * T / E))
        x = h.reshape(T, D)
        logits = x @ gate_w + gate_b
        probs = jax.nn.softmax(logits, axis=-1)
        idx = jnp.argmax(probs, axis=-1)
        prb = jnp.take_along_axis(probs, idx[:, None], axis=1)[:, 0]
        one_hot = jax.nn.one_hot(idx, E, dtype=jnp.float32)
        pos = (jnp.cumsum(one_hot, axis=0) * one_hot).sum(-1).astype(jnp.int32) - 1
        kept = pos < C
        pos_safe = jnp.where(kept, pos, C)
        buf = jnp.zeros((E, C, D), dtype=h.dtype).at[idx, pos_safe].set(x, mode='drop')
        hmid = jax.nn.relu(jnp.einsum('ecd,edf->ecf', buf, w1) + b1[:, None, :])
        ybuf = jnp.einsum('ecf,efd->ecd', hmid, w2) + b2[:, None, :]
        pos_g = jnp.minimum(pos, C - 1)
        y_tok = ybuf[idx, pos_g] * (prb * kept)[:, None]
        y = y_tok.reshape(B, L, D)
        y = jnp.nan_to_num(y, nan=0.0, posinf=10000.0, neginf=-10000.0)
        return y

    def _gn(v, G=32, eps=1e-5):
        B_, C_, H_, W_ = v.shape
        g = v.reshape(B_, G, C_ // G, H_, W_)
        m = jnp.mean(g, axis=(2, 3, 4), keepdims=True)
        s = jnp.var(g, axis=(2, 3, 4), keepdims=True)
        return ((g - m) / jnp.sqrt(s + eps)).reshape(v.shape)

    def _ln_c(v, eps=1e-6):
        m = jnp.mean(v, axis=1, keepdims=True)
        s = jnp.var(v, axis=1, keepdims=True)
        return (v - m) / jnp.sqrt(s + eps)

    def _ln_t(v, eps=1e-5):
        m = jnp.mean(v, axis=-1, keepdims=True)
        s = jnp.var(v, axis=-1, keepdims=True)
        return (v - m) / jnp.sqrt(s + eps)

    def _to_tokens(v):
        B_, C_, H_, W_ = v.shape
        return v.reshape(B_, C_, H_ * W_).transpose(0, 2, 1)
    def _from_tokens(t, like):
        B_, C_, H_, W_ = like.shape
        return t.transpose(0, 2, 1).reshape(B_, C_, H_, W_)

    x = _L0_conv_ref(x, L0_conv_ln_g, L0_conv_ln_b, L0_conv_pos_scale, L0_conv_in_proj_w, L0_conv_out_proj_w, L0_conv_conv_w_f, L0_conv_conv_b_f, L0_conv_xproj_w_f, L0_conv_dtproj_w_f, L0_conv_dtproj_b_f, L0_conv_A_log_f, L0_conv_D_f, L0_conv_conv_w_b, L0_conv_conv_b_b, L0_conv_xproj_w_b, L0_conv_dtproj_w_b, L0_conv_dtproj_b_b, L0_conv_A_log_b, L0_conv_D_b)
    x = x + _L1_conv_ref(_gn(x), L1_conv_Wqkv, L1_conv_bqkv, L1_conv_dw_w, L1_conv_dw_b, L1_conv_Wproj, L1_conv_bproj, L1_conv_bn1_g, L1_conv_bn1_b, L1_conv_bn1_m, L1_conv_bn1_v, L1_conv_alpha1, L1_conv_Wfc1, L1_conv_bfc1, L1_conv_Wfc2, L1_conv_bfc2, L1_conv_bn2_g, L1_conv_bn2_b, L1_conv_bn2_m, L1_conv_bn2_v, L1_conv_alpha2)
    t = _to_tokens(x)
    t = t + _L2_attn_ref(_ln_t(t), L2_attn_W_embed, L2_attn_b_embed, L2_attn_W_out, L2_attn_b_out)
    t = t + _L2_ffn_ref(_ln_t(t), L2_ffn_W_gat, L2_ffn_att_src, L2_ffn_att_dst, L2_ffn_b_gat, L2_ffn_ln_gamma, L2_ffn_ln_beta, L2_ffn_W1, L2_ffn_b1, L2_ffn_W2, L2_ffn_b2, L2_ffn_edge_index)
    t = t + _L3_attn_ref(_ln_t(t), L3_attn_q_weight)
    t = t + _L3_ffn_ref(_ln_t(t), L3_ffn_gate_w, L3_ffn_gate_b, L3_ffn_w1, L3_ffn_b1, L3_ffn_w2, L3_ffn_b2)
    x = _from_tokens(t, x)
    return x


_drawn_inputs = setup_inputs


def setup_inputs(seed=0):
    import zlib

    import numpy as np

    out = dict(_drawn_inputs(seed))
    spreads = {'L0_conv_ln_g': (1.0, 0.6),
     'L0_conv_ln_b': (0.0, 0.8),
     'L0_conv_D_f': (1.0, 0.6),
     'L0_conv_D_b': (1.0, 0.6),
     'L1_conv_bn1_g': (1.0, 0.2),
     'L1_conv_bn1_b': (0.0, 0.1),
     'L1_conv_bn2_g': (1.0, 0.2),
     'L1_conv_bn2_b': (0.0, 0.1),
     'L2_attn_b_embed': (0.0, 0.344),
     'L2_attn_b_out': (0.0, 0.1),
     'L2_ffn_b_gat': (0.0, 0.267),
     'L2_ffn_ln_gamma': (1.0, 0.6),
     'L2_ffn_ln_beta': (0.0, 0.8),
     'L2_ffn_b1': (0.0, 0.1),
     'L2_ffn_b2': (0.0, 0.1),
     'L3_ffn_gate_b': (0.0, 0.8),
     'L3_ffn_b1': (0.0, 2.0),
     'L3_ffn_b2': (0.0, 2.0)}
    factors = {'L0_conv_conv_w_f': 6.316,
     'L0_conv_conv_b_f': 2.815,
     'L0_conv_xproj_w_f': 8.0,
     'L0_conv_dtproj_w_f': 8.0,
     'L0_conv_dtproj_b_f': 8.0,
     'L0_conv_A_log_f': 8.0,
     'L0_conv_conv_w_b': 5.904,
     'L0_conv_conv_b_b': 2.699,
     'L0_conv_xproj_w_b': 8.0,
     'L0_conv_dtproj_w_b': 8.0,
     'L0_conv_dtproj_b_b': 8.0,
     'L0_conv_A_log_b': 8.0,
     'L2_attn_W_embed': 8.0,
     'L2_ffn_att_src': 22.17,
     'L2_ffn_att_dst': 51.802,
     'L3_ffn_gate_w': 8.0,
     'L3_ffn_w1': 8.0,
     'L3_ffn_w2': 8.0}
    for name, (base, spread) in spreads.items():
        noise = np.random.default_rng([zlib.crc32(name.encode()), seed]).standard_normal(out[name].shape)
        drawn = base * np.exp(spread * noise) if base else spread * noise
        out[name] = jnp.asarray(drawn.astype(out[name].dtype))
    for name, factor in factors.items():
        out[name] = (out[name] * factor).astype(out[name].dtype)
    return out
```

```python
import concourse.bass as bass
from concourse import mybir
from contextlib import ExitStack

import numpy as np

F32 = mybir.dt.float32
I32 = mybir.dt.int32
I16 = mybir.dt.int16
BF16 = mybir.dt.bfloat16
ALU = mybir.AluOpType
ACT = mybir.ActivationFunctionType
AX = mybir.AxisListType

P = 128
NB = 2
C = 256
KC = C // P
HW = 48
L = HW * HW
M = NB * L
T = 384
NT = L // T
BANK = 512

DI = 512
JD = DI // P
DS = 16
DR = 16
NQ = 3
Q = L // NQ


def sems(nc, ctx, *names):
    return [ctx.enter_context(nc.semaphore(n)) for n in names]


def fresh(nc, used):
    with nc.Block() as block:
        @block.sync
        def _(sp):
            for s in used:
                sp.sem_clear(s)


class Core:
    pass


def load_constants(nc, ctx, k, A):
    with ExitStack() as own:
        (loaded,) = sems(nc, own, "loaded")
        with nc.Block() as block:
            @block.sync
            def _(sp):
                n = 0
                for b in range(NB):
                    sp.dma_start(k.X[:, :, b * L:(b + 1) * L],
                                 A["x"][b].rearrange("(k p) n -> p k n", p=P)).then_inc(loaded, 16)
                    n += 16
                for dst, name in ((k.ident, "c_ident"), (k.mean_w, "c_mean"), (k.group_w, "c_group")):
                    sp.dma_start(dst[:], A[name]).then_inc(loaded, 16)
                    n += 16
                sp.wait_ge(loaded, n)
        fresh(nc, [loaded])


def norm_image(nc, k, b, eps):
    with ExitStack() as ctx:
        sq = ctx.enter_context(nc.sbuf_tensor(k.name("sq"), [P, 2, KC, T], F32))
        std = ctx.enter_context(nc.sbuf_tensor(k.name("std"), [P, 2, T], F32))
        used = sems(nc, ctx, "mean_ready", "centered", "squared", "var_ready", "rooted", "normalized")
        mean_ready, centered, squared, var_ready, rooted, normalized = used
        with nc.Block() as block:
            @block.tensor
            def _(pe):
                for s in range(NT + 1):
                    if s < NT:
                        if s >= 2:
                            pe.wait_ge(centered, s - 1)
                        for c in range(KC):
                            mm = pe.matmul(k.PS[:, s % 2, :T], k.mean_w[:], k.X[:, c, bass.ds(b * L + s * T, T)],
                                           start=(c == 0), stop=(c == KC - 1))
                        mm.then_inc(mean_ready, 1)
                    if s >= 1:
                        v = s - 1
                        pe.wait_ge(squared, v + 1)
                        if v >= 2:
                            pe.wait_ge(rooted, v - 1)
                        for c in range(KC):
                            mm = pe.matmul(k.PS[:, 2 + v % 2, :T], k.mean_w[:], sq[:, v % 2, c, :],
                                           start=(c == 0), stop=(c == KC - 1))
                        mm.then_inc(var_ready, 1)

            @block.vector
            def _(dve):
                for s in range(NT + 1):
                    if s < NT:
                        dve.wait_ge(mean_ready, s + 1)
                        for c in range(KC):
                            op = dve.tensor_tensor(k.N[:, c, s * T:(s + 1) * T], k.X[:, c, bass.ds(b * L + s * T, T)],
                                                   k.PS[:, s % 2, :T], ALU.subtract)
                        op.then_inc(centered, 1)
                    if s >= 1:
                        v = s - 1
                        dve.wait_ge(rooted, v + 1)
                        dve.reciprocal(std[:, v % 2, :], std[:, v % 2, :])
                        dve.drain()
                        for c in range(KC):
                            op = dve.tensor_tensor(k.N[:, c, v * T:(v + 1) * T], k.N[:, c, v * T:(v + 1) * T],
                                                   std[:, v % 2, :], ALU.mult)
                        op.then_inc(normalized, 1)

            @block.scalar
            def _(act):
                for s in range(NT + 1):
                    if s < NT:
                        act.wait_ge(centered, s + 1)
                        if s >= 2:
                            act.wait_ge(var_ready, s - 1)
                        act.activation(sq[:, s % 2, :, :], k.N[:, :, s * T:(s + 1) * T], ACT.Square)\
                           .then_inc(squared, 1)
                    if s >= 1:
                        v = s - 1
                        act.wait_ge(var_ready, v + 1)
                        if v >= 2:
                            act.wait_ge(normalized, v - 1)
                        act.activation(std[:, v % 2, :], k.PS[:, 2 + v % 2, :T], ACT.Sqrt, bias=eps[:])\
                           .then_inc(rooted, 1)
        fresh(nc, used)


def mamba(nc, k, A, b):
    norm_image(nc, k, b, k.eps5)
    with ExitStack() as ctx:
        def sb(name, shape, dt=F32):
            return ctx.enter_context(nc.sbuf_tensor(k.name(name), shape, dt))

        w_in = sb("w_in", [P, KC, 2 * DI])
        XS = sb("XS", [P, JD, L])
        Y = sb("Y", [P, JD, L])
        gb = sb("gb", [P, KC, 2])
        pscale = sb("pscale", [P, 1])
        used = sems(nc, ctx, "l0_loaded", "l0_scaled")
        l0_loaded, l0_scaled = used
        pos = Y[:, 0:KC, :]
        with nc.Block() as block:
            @block.sync
            def _(sp):
                sp.dma_start(pos, A["c_pos"]).then_inc(l0_loaded, 16)
                sp.dma_start(gb[:], A["l0_ln"]).then_inc(l0_loaded, 16)
                sp.dma_start(pscale[:], A["L0_conv_pos_scale"].rearrange("(o n) -> o n", o=1)
                             .broadcast_to([P, 1])).then_inc(l0_loaded, 16)
                sp.dma_start(w_in[:], A["l0_w_in"]).then_inc(l0_loaded, 16)
                sp.wait_ge(l0_loaded, 64)

            @block.vector
            def _(dve):
                dve.wait_ge(l0_loaded, 64)
                for c in range(KC):
                    dve.tensor_scalar(k.N[:, c, :], k.N[:, c, :], gb[:, c, 0:1], gb[:, c, 1:2], ALU.mult, ALU.add)
                dve.drain()
                for c in range(KC):
                    dve.scalar_tensor_tensor(k.N[:, c, :], pos[:, c, :], pscale[:], k.N[:, c, :], ALU.mult, ALU.add)
        fresh(nc, used)
        for rev in range(2):
            with ExitStack() as own:
                mamba_direction(nc, own, k, A, w_in, XS, Y, rev)
        mamba_output(nc, ctx, k, A, b, w_in, Y)


def mamba_direction(nc, ctx, k, A, w_in, XS, Y, rev):
    def sb(name, shape, dt=F32):
        return ctx.enter_context(nc.sbuf_tensor(k.name(name), shape, dt))

    d = "fb"[rev]
    PAD = 3
    region = sb("region", [P, 2 * JD * Q + 64])
    XP = region[:, 0:L + 2 * PAD]
    XC = region[:, L + 8:2 * L + 8]
    DT = region[:, 0:JD * Q].rearrange("p (j t) -> p j t", j=JD)
    DU = region[:, JD * Q:2 * JD * Q].rearrange("p (j t) -> p j t", j=JD)
    work = sb("work", [P, 8, Q])
    PJ = work[0:3 * DS, 0:3, :].rearrange("p a t -> p (a t)")
    DA, DBU, HS, G = (work[:, 2 * i:2 * i + 2, :] for i in range(4))
    dtr = sb("dtr", [DR, Q])
    BB = sb("BB", [P, 2, Q])
    CB = sb("CB", [P, 2, Q])
    conv_w = sb("conv_w", [P, JD, 4])
    vec = sb("vec", [P, JD, 3])
    alog = sb("alog", [P, JD, DS])
    w_x = sb("w_x", [P, JD, 3 * DS])
    w_dt = sb("w_dt", [DR, DI])
    HC = sb("HC", [P, JD, DS])

    used = sems(nc, ctx, "params", "xi_ready", "xi_copied", "conv_done", "xs_done", "pj_ready", "pj_copied",
                "pj_stored", "padded")
    params, xi_ready, xi_copied, conv_done, xs_done, pj_ready, pj_copied, pj_stored, padded = used
    with nc.Block() as block:
        @block.sync
        def _(sp):
            for dst, name in ((conv_w, "l0_conv_w_"), (vec, "l0_vec_"), (alog, "l0_alog_"), (w_x, "l0_w_x_"),
                              (w_dt, "l0_w_dt_")):
                sp.dma_start(dst[:], A[name + d]).then_inc(params, 16)
            sp.wait_ge(params, 80)
            sp.wait_ge(pj_copied, NT)
            sp.dma_start(k.proj_dram, PJ).then_inc(pj_stored, 16)
            sp.wait_ge(pj_stored, 16)

        @block.tensor
        def _(pe):
            for j in range(JD):
                for c in range(NT):
                    n = j * NT + c
                    if n >= 4:
                        pe.wait_ge(xi_copied, n - 3)
                    for i in range(KC):
                        mm = pe.matmul(k.PS[:, n % 4, :T], w_in[:, i, j * P:(j + 1) * P], k.N[:, i, c * T:(c + 1) * T],
                                       start=(i == 0), stop=(i == KC - 1))
                    mm.then_inc(xi_ready, 1)
            pe.wait_ge(params, 80)
            pe.wait_ge(xs_done, JD)
            for c in range(NT):
                if c >= 2:
                    pe.wait_ge(pj_copied, c - 1)
                for j in range(JD):
                    mm = pe.matmul(k.PS[0:3 * DS, 4 + c % 2, :T], w_x[:, j, :], XS[:, j, c * T:(c + 1) * T],
                                   start=(j == 0), stop=(j == JD - 1))
                mm.then_inc(pj_ready, 1)

        @block.scalar
        def _(act):
            act.wait_ge(params, 80)
            for j in range(JD):
                if j >= 1:
                    act.wait_ge(conv_done, j)
                for c in range(NT):
                    act.wait_ge(xi_ready, j * NT + c + 1)
                    act.activation(XP[:, PAD + c * T:PAD + (c + 1) * T], k.PS[:, (j * NT + c) % 4, :T], ACT.Copy)\
                       .then_inc(xi_copied, 1)
                act.wait_ge(conv_done, j + 1)
                act.activation(XS[:, j, :], XC, ACT.Silu, bias=vec[:, j, 0:1]).then_inc(xs_done, 1)
            for c in range(NT):
                act.wait_ge(pj_ready, c + 1)
                act.activation(PJ[:, c * T:(c + 1) * T], k.PS[0:3 * DS, 4 + c % 2, :T], ACT.Copy).then_inc(pj_copied, 1)

        @block.vector
        def _(dve):
            dve.memset(XP[:, 0:PAD], 0.0)
            dve.memset(XP[:, PAD + L:2 * PAD + L], 0.0)
            dve.memset(HC[:], 0.0)
            dve.drain()
            dve.wait_ge(params, 80)
            for j in range(JD):
                dve.wait_ge(xi_copied, (j + 1) * NT)
                if j >= 1:
                    dve.wait_ge(xs_done, j)
                for t in range(4):
                    at = 2 * PAD - t if rev else t
                    if t == 0:
                        dve.tensor_scalar(XC, XP[:, at:at + L], conv_w[:, j, 0:1], None, ALU.mult)
                    else:
                        dve.drain()
                        op = dve.scalar_tensor_tensor(XC, XP[:, at:at + L], conv_w[:, j, t:t + 1], XC, ALU.mult, ALU.add)
                op.then_inc(conv_done, 1)
    fresh(nc, used)

    with nc.Block() as block:
        @block.scalar
        def _(act):
            act.activation(alog[:], alog[:], ACT.Exp)
            act.drain()
            act.mul(alog[:], alog[:], -1.0)

    pieces = range(NQ - 1, -1, -1) if rev else range(NQ)
    H = Q // 2
    for q in pieces:
        t0 = q * Q
        used = sems(nc, ctx, "dtr_in", "dt_ready", "dt_pre", "dt_log", "dt_done",
                    "b_in0", "b_in1", "c_in0", "c_in1", "da_done", "dbu_done", "h_done", "g_done", "acc_done") \
            if q == pieces[0] else used
        (dtr_in, dt_ready, dt_pre, dt_log, dt_done,
         b_in0, b_in1, c_in0, c_in1, da_done, dbu_done, h_done, g_done, acc_done) = used
        b_in, c_in = (b_in0, b_in1), (c_in0, c_in1)
        with nc.Block() as block:
            @block.sync
            def _(sp):
                sp.dma_start(dtr[:], k.proj_dram[0:DR, t0:t0 + Q]).then_inc(dtr_in, 16)
                sp.wait_ge(dtr_in, 16)

            @block.tensor
            def _(pe):
                pe.wait_ge(dtr_in, 16)
                for j in range(JD):
                    for h in range(2):
                        mm = pe.matmul(k.PS[:, 2 * j + h, :H], w_dt[:, j * P:(j + 1) * P], dtr[:, h * H:(h + 1) * H],
                                       start=True, stop=True)
                    mm.then_inc(dt_ready, 1)

            @block.scalar
            def _(act):
                for j in range(JD):
                    act.wait_ge(dt_ready, j + 1)
                    if j >= 1:
                        act.wait_ge(dt_done, j)
                    act.activation(DT[:, j, :].rearrange("p (h t) -> p h t", h=2), k.PS[:, 2 * j:2 * j + 2, :H],
                                   ACT.Identity, bias=vec[:, j, 1:2])
                    act.drain()
                    act.activation(DA[:, 0, :], DT[:, j, :], ACT.Abs)
                    act.drain()
                    act.activation(DA[:, 1, :], DA[:, 0, :], ACT.Exp, scale=-1.0)
                    act.drain()
                    act.activation(HS[:, 0, :], DA[:, 1, :], ACT.Ln, bias=1.0).then_inc(dt_log, 1)

            @block.vector
            def _(dve):
                for j in range(JD):
                    dve.wait_ge(dt_log, j + 1)
                    e, ln, um, z = DA[:, 1, :], HS[:, 0, :], HS[:, 1, :], DBU[:, 0, :]
                    dve.tensor_scalar(um, e, 1.0, 1.0, ALU.add, ALU.subtract)
                    dve.drain()
                    dve.tensor_scalar(z, um, 0.0, None, ALU.is_equal)
                    dve.drain()
                    dve.tensor_tensor(um, um, z, ALU.add)
                    dve.tensor_tensor(ln, ln, z, ALU.add)
                    dve.drain()
                    dve.reciprocal(um, um)
                    dve.tensor_tensor(ln, ln, e, ALU.mult)
                    dve.drain()
                    dve.tensor_tensor(ln, ln, um, ALU.mult)
                    dve.drain()
                    dve.scalar_tensor_tensor(DT[:, j, :], DT[:, j, :], 0.0, ln, ALU.max, ALU.add)
                    dve.drain()
                    dve.tensor_tensor(DU[:, j, :], DT[:, j, :], XS[:, j, t0:t0 + Q], ALU.mult).then_inc(dt_done, 1)

        def flow(ap):
            return ap[:, ::-1] if rev else ap

        FREE, SPARE = 2, JD + 1
        with nc.Block() as block:
            @block.sync
            def _(sp):
                with sp.Fori(0, DS // 2) as n2:
                    for u in range(2):
                        sp.wait_ge(dbu_done, n2 * (2 * JD) + u * JD + 1)
                        sp.wait_ge(g_done, n2 * (2 * JD) + u * JD + 1)
                        for row, dst, s in ((DR, BB, b_in[u]), (DR + DS, CB, c_in[u])):
                            sp.dma_start(dst[:, u, :],
                                         k.proj_dram[bass.ds(row + u + n2 * 2, 1), t0:t0 + Q].broadcast_to([P, Q]))\
                              .then_inc(s, 16)

            @block.scalar
            def _(act):
                with act.Fori(0, DS // 2) as n2:
                    for u in range(2):
                        for j in range(JD):
                            s = u * JD + j
                            act.wait_ge(h_done, n2 * (2 * JD) + s + 1)
                            act.activation(DA[:, j % 2, :], DT[:, j, :], ACT.Exp,
                                           scale=alog[:, j, bass.ds(n2 * 2 + u, 1)]).then_inc(da_done, 1)

            @block.gpsimd
            def _(pool):
                pool.sem_inc(dbu_done, SPARE)
                with pool.Fori(0, DS // 2) as n2:
                    for u in range(2):
                        pool.wait_ge(b_in[u], n2 * 16 + 16)
                        for j in range(JD):
                            s = u * JD + j
                            pool.wait_ge(h_done, n2 * (2 * JD) + s + 1)
                            pool.tensor_tensor(DBU[:, j % 2, :], DU[:, j, :], BB[:, u, :], ALU.mult)\
                                .then_inc(dbu_done, 1)

            @block.vector
            def _(dve):
                dve.sem_inc(h_done, FREE)
                dve.sem_inc(g_done, SPARE)
                with dve.Fori(0, DS // 2) as n2:
                    for u in range(2):
                        dve.wait_ge(c_in[u], n2 * 16 + 16)
                        for j in range(JD):
                            s = u * JD + j
                            dve.wait_ge(da_done, n2 * (2 * JD) + s + 1)
                            dve.wait_ge(dbu_done, n2 * (2 * JD) + s + 1 + SPARE)
                            carry = HC[:, j, bass.ds(n2 * 2 + u, 1)]
                            dve.tensor_tensor_scan(flow(HS[:, j % 2, :]), flow(DA[:, j % 2, :]), flow(DBU[:, j % 2, :]),
                                                   carry, ALU.mult, ALU.add).then_inc(h_done, 1)
                            dve.drain()
                            last = 0 if rev else Q - 1
                            dve.tensor_copy(carry, HS[:, j % 2, last:last + 1])
                            dve.wait_ge(acc_done, n2 * (2 * JD) + s + 1)
                            dve.tensor_tensor(G[:, j % 2, :], HS[:, j % 2, :], CB[:, u, :], ALU.mult)\
                               .then_inc(g_done, 1)

            @block.tensor
            def _(pe):
                pe.sem_inc(acc_done, FREE)
                for j in range(JD):
                    for h in range(2):
                        pe.matmul(k.PS[:, 2 * j + h, :H], k.zero_w[:], DT[:, 0, 0:H], start=True, stop=False)
                with pe.Fori(0, DS // 2) as n2:
                    for u in range(2):
                        for j in range(JD):
                            pe.wait_ge(g_done, n2 * (2 * JD) + u * JD + j + 1 + SPARE)
                            for h in range(2):
                                mm = pe.matmul(k.PS[:, 2 * j + h, :H], k.ident[:], G[:, j % 2, h * H:(h + 1) * H],
                                               start=False, stop=False)
                            mm.then_inc(acc_done, 1)
                for j in range(JD):
                    for h in range(2):
                        pe.matmul(k.PS[:, 2 * j + h, :H], k.zero_w[:], DT[:, 0, 0:H], start=False, stop=True)
        with nc.Block() as block:
            @block.vector
            def _(dve):
                for j in range(JD):
                    y = Y[:, j, t0:t0 + Q]
                    y2 = y.rearrange("p (h t) -> p h t", h=2)
                    xs2 = XS[:, j, t0:t0 + Q].rearrange("p (h t) -> p h t", h=2)
                    if rev:
                        dve.tensor_tensor(y2, y2, k.PS[:, 2 * j:2 * j + 2, :H], ALU.add)
                        dve.drain()
                        dve.scalar_tensor_tensor(y, XS[:, j, t0:t0 + Q], vec[:, j, 2:3], y, ALU.mult, ALU.add)
                    else:
                        dve.scalar_tensor_tensor(y2, xs2, vec[:, j, 2:3], k.PS[:, 2 * j:2 * j + 2, :H], ALU.mult, ALU.add)
        fresh(nc, used)


def mamba_output(nc, ctx, k, A, b, w_in, Y):
    w_out = ctx.enter_context(nc.sbuf_tensor(k.name("w_out"), [P, JD, C], F32))
    Z = ctx.enter_context(nc.sbuf_tensor(k.name("Z"), [P, 2, T], F32))
    used = sems(nc, ctx, "wo_in", "z_ready", "z_done", "gated", "o_ready", "o_added")
    wo_in, z_ready, z_done, gated, o_ready, o_added = used
    with nc.Block() as block:
        @block.sync
        def _(sp):
            sp.dma_start(w_out[:], A["l0_w_out"]).then_inc(wo_in, 16)
            sp.wait_ge(wo_in, 16)

        @block.tensor
        def _(pe):
            pe.wait_ge(wo_in, 16)
            for c in range(NT):
                for j in range(JD):
                    n = c * JD + j
                    if n >= 2:
                        pe.wait_ge(z_done, n - 1)
                    for i in range(KC):
                        mm = pe.matmul(k.PS[:, n % 2, :T], w_in[:, i, DI + j * P:DI + (j + 1) * P],
                                       k.N[:, i, c * T:(c + 1) * T], start=(i == 0), stop=(i == KC - 1))
                    mm.then_inc(z_ready, 1)
                pe.wait_ge(gated, (c + 1) * JD)
                if c >= 1:
                    pe.wait_ge(o_added, c)
                for m in range(KC):
                    for j in range(JD):
                        mm = pe.matmul(k.PS[:, 2 + m, :T], w_out[:, j, m * P:(m + 1) * P], Y[:, j, c * T:(c + 1) * T],
                                       start=(j == 0), stop=(j == JD - 1))
                mm.then_inc(o_ready, 1)

        @block.scalar
        def _(act):
            for n in range(NT * JD):
                act.wait_ge(z_ready, n + 1)
                if n >= 2:
                    act.wait_ge(gated, n - 1)
                act.activation(Z[:, n % 2, :], k.PS[:, n % 2, :T], ACT.Silu).then_inc(z_done, 1)

        @block.vector
        def _(dve):
            for c in range(NT):
                for j in range(JD):
                    n = c * JD + j
                    dve.wait_ge(z_done, n + 1)
                    dve.tensor_tensor(Y[:, j, c * T:(c + 1) * T], Y[:, j, c * T:(c + 1) * T], Z[:, n % 2, :], ALU.mult)\
                       .then_inc(gated, 1)
                dve.wait_ge(o_ready, c + 1)
                x = k.X[:, :, bass.ds(b * L + c * T, T)]
                dve.tensor_tensor(x, x, k.PS[:, 2:2 + KC, :T], ALU.add).then_inc(o_added, 1)
    fresh(nc, used)


NHEAD = 8
CM = 2048
NM = CM // P
LT = L // P
ROWS = T // HW
TAPS = 3


def two_layer(nc, ctx, k, b, src, w1, b1, w2, banks_free, gate=None, first=None, last=None):
    H = ctx.enter_context(nc.sbuf_tensor(k.name("H"), [P, NM, T], F32))
    used = sems(nc, ctx, "hid_ready", "hid_done", "hid_gated", "hid_used", "sum_ready", "sum_used")
    hid_ready, hid_done, hid_gated, hid_used, sum_ready, sum_used = used
    feed = hid_gated if gate is not None else hid_done
    credit = 0 if gate is not None else 3
    with nc.Block() as block:
        @block.tensor
        def _(pe):
            pe.sem_inc(sum_ready, 1)
            with pe.Fori(0, NT) as c:
                for s in range(NM + 2):
                    if s < NM:
                        pe.wait_ge(hid_done, c * NM + s + 1)
                        for i in range(KC):
                            mm = pe.matmul(k.PS[:, (s % 3), :T], w1(i, s), src[:, i, bass.ds(c * T, T)],
                                           start=(i == 0), stop=(i == KC - 1))
                        mm.then_inc(hid_ready, 1)
                    if s >= 2:
                        m = s - 2
                        pe.wait_ge(feed, c * NM + m + 1 + credit)
                        if m == 0:
                            pe.wait_ge(sum_used, c + 1)
                            if first is not None:
                                first(pe, c)
                        for o in range(KC):
                            mm = pe.matmul(k.PS[:, 4 + o, :T], w2(m, o), H[:, m, :],
                                           start=(m == 0 and first is None), stop=(m == NM - 1))
                        mm.then_inc(hid_used if m < NM - 1 else sum_ready, 1)

        @block.scalar
        def _(act):
            act.sem_inc(hid_done, 3)
            with act.Fori(0, NT) as c:
                act.wait_ge(sum_ready, c + 1)
                for m in range(NM):
                    act.wait_ge(hid_ready, c * NM + m + 1)
                    act.activation(H[:, m, :], k.PS[:, m % 3, :T], ACT.Gelu, bias=b1(m)).then_inc(hid_done, 1)

        @block.vector
        def _(dve):
            dve.sem_inc(sum_used, 1)
            with dve.Fori(0, NT) as c:
                if gate is not None:
                    for m in range(NM):
                        dve.wait_ge(hid_done, c * NM + m + 1 + 3)
                        dve.tensor_tensor(H[:, m, :], H[:, m, :], gate(m, c), ALU.mult).then_inc(hid_gated, 1)
                dve.wait_ge(sum_ready, c + 2)
                last(dve, c).then_inc(sum_used, 1)
    fresh(nc, used)


def linear_attention_block(nc, k, A, b):
    with ExitStack() as ctx:
        def sb(name, shape, dt=F32):
            return ctx.enter_context(nc.sbuf_tensor(k.name(name), shape, dt))

        vec = sb("vec1", [P, KC, 12])
        alpha = sb("alpha", [P, 2])
        SB = sb("SB", [P, KC, 2, 2])
        TT = sb("TT", [P, KC, L])
        sq = sb("sq1", [P, KC, 4])
        (BQ, DWB, BPROJ, BN, BFC2) = (0, 1, 2, 3, 11)

        with ExitStack() as own:
            def sbo(name, shape, dt=F32):
                return own.enter_context(nc.sbuf_tensor(k.name(name), shape, dt))

            w_qkv = sbo("w_qkv", [P, KC, 3 * C])
            w_pr = sbo("w_pr", [P, KC, C])
            bkv = sbo("bkv", [P, 2 * C])
            dw = sbo("dw", [P, KC, TAPS * TAPS])
            hmask = sbo("hmask", [P, P])
            QT = sbo("QT", [P, KC, L])
            KV = sbo("KV", [P, LT, 2 * C])
            CTX = sbo("CTX", [P, KC, P])
            IMG = sbo("IMG", [P, KC, HW + 2, HW + 2])
            stats = sbo("stats", [P, KC, NT, 6])
            mv = sbo("mv", [P, KC, 2])
            g = sbo("g", [P, KC, 4])
            used = sems(nc, own, "l1_loaded", "mv_done", "mg_ready", "vg_done", "root_done")
            l1_loaded, mv_done, mg_ready, vg_done, root_done = used
            with nc.Block() as block:
                @block.sync
                def _(sp):
                    n = 0
                    for dst, name in ((vec, "l1_vec"), (w_qkv, "l1_w_qkv"), (w_pr, "l1_w_proj"), (dw, "l1_dw"),
                                      (hmask, "c_head")):
                        sp.dma_start(dst[:], A[name]).then_inc(l1_loaded, 16)
                        n += 16
                    for dst, src in ((bkv[:], A["l1_bkv"].broadcast_to([P, 2 * C])),
                                     (alpha[:], A["l1_alpha"].broadcast_to([P, 2]))):
                        sp.dma_start(dst, src).then_inc(l1_loaded, 16)
                        n += 16
                    assert n == 112
                    sp.wait_ge(l1_loaded, n)

                @block.vector
                def _(dve):
                    for i in range(KC):
                        for c in range(NT):
                            dve.bn_stats(stats[:, i, c, :], k.X[:, i, bass.ds(b * L + c * T, T)])
                    dve.drain()
                    for i in range(KC):
                        dve.bn_aggr(mv[:, i, :], stats[:, i, :, :].rearrange("p c s -> p (c s)"))
                    dve.drain()
                    dve.tensor_tensor(g[:, :, 0], mv[:, :, 0], mv[:, :, 0], ALU.mult)
                    dve.drain()
                    dve.tensor_tensor(mv[:, :, 1], mv[:, :, 1], g[:, :, 0], ALU.add).then_inc(mv_done, 1)
                    dve.wait_ge(mg_ready, 1)
                    gm = k.PS[:, 0, 0:2 * KC].rearrange("p (i s) -> p i s", i=KC)
                    dve.tensor_copy(g[:, :, 0:2], gm)
                    dve.drain()
                    dve.tensor_tensor(g[:, :, 2], g[:, :, 0], g[:, :, 0], ALU.mult)
                    dve.drain()
                    dve.tensor_tensor(g[:, :, 2], g[:, :, 1], g[:, :, 2], ALU.subtract).then_inc(vg_done, 1)
                    dve.wait_ge(root_done, 1)
                    dve.reciprocal(g[:, :, 3], g[:, :, 3])
                    dve.reciprocal(sq[:], sq[:])
                    dve.drain()
                    for i in range(KC):
                        dve.tensor_scalar(k.N[:, i, :], k.X[:, i, bass.ds(b * L, L)], g[:, i, 0:1], g[:, i, 3:4],
                                          ALU.subtract, ALU.mult)
                    for w in range(2):
                        bn = BN + 4 * w
                        dve.tensor_tensor(SB[:, :, w, 0], vec[:, :, bn], sq[:, :, w], ALU.mult)
                        dve.drain()
                        dve.tensor_tensor(SB[:, :, w, 1], vec[:, :, bn + 2], SB[:, :, w, 0], ALU.mult)
                        dve.drain()
                        dve.tensor_tensor(SB[:, :, w, 1], vec[:, :, bn + 1], SB[:, :, w, 1], ALU.subtract)
                        dve.tensor_scalar(SB[:, :, w, 0], SB[:, :, w, 0], alpha[:, w:w + 1], None, ALU.add)

                @block.tensor
                def _(pe):
                    pe.wait_ge(mv_done, 1)
                    pe.matmul(k.PS[:, 0, 0:2 * KC], k.group_w[:], mv[:].rearrange("p i s -> p (i s)"),
                              start=True, stop=True).then_inc(mg_ready, 1)

                @block.scalar
                def _(act):
                    act.wait_ge(l1_loaded, 112)
                    for w in range(2):
                        act.activation(sq[:, :, w], vec[:, :, BN + 4 * w + 3], ACT.Sqrt, bias=k.eps5[:])
                        act.activation(sq[:, :, 2 + w], vec[:, :, BN + 4 * w + 3], ACT.Sqrt, bias=k.eps5[:])
                    act.wait_ge(vg_done, 1)
                    act.activation(g[:, :, 3], g[:, :, 2], ACT.Sqrt, bias=k.eps5[:]).then_inc(root_done, 1)
            fresh(nc, used)

            used = sems(nc, own, "q_ready", "q_done", "kv_ready", "kv_added", "kv_done", "ctx_ready", "ctx_done",
                        "img_ready", "img_done", "img_zero", "conv1_done", "pr_ready", "tt_done")
            (q_ready, q_done, kv_ready, kv_added, kv_done, ctx_ready, ctx_done,
             img_ready, img_done, img_zero, conv1_done, pr_ready, tt_done) = used
            with nc.Block() as block:
                @block.tensor
                def _(pe):
                    for n in range(KC * NT):
                        m, c = n // NT, n % NT
                        if n >= 2:
                            pe.wait_ge(q_done, n - 1)
                        for i in range(KC):
                            mm = pe.matmul(k.PS[:, n % 2, :T], w_qkv[:, i, m * P:(m + 1) * P],
                                           k.N[:, i, c * T:(c + 1) * T], start=(i == 0), stop=(i == KC - 1))
                        mm.then_inc(q_ready, 1)
                    for t in range(LT + 1):
                        if t < LT:
                            if t >= 2:
                                pe.wait_ge(kv_added, t - 1)
                            for i in range(KC):
                                mm = pe.matmul(k.PS[:, 2 + t % 2, :], k.N[:, i, t * P:(t + 1) * P], w_qkv[:, i, C:3 * C],
                                               start=(i == 0), stop=(i == KC - 1))
                            mm.then_inc(kv_ready, 1)
                        if t >= 1:
                            pe.wait_ge(kv_done, t)
                            for i in range(KC):
                                mm = pe.matmul(k.PS[:, 4 + i, 0:P], KV[:, t - 1, i * P:(i + 1) * P],
                                               KV[:, t - 1, C + i * P:C + (i + 1) * P], start=(t == 1), stop=(t == LT))
                    mm.then_inc(ctx_ready, 1)
                    pe.wait_ge(ctx_done, 1)
                    pe.wait_ge(q_done, KC * NT)
                    for n in range(KC * NT):
                        i, c = n // NT, n % NT
                        if n >= 2:
                            pe.wait_ge(img_done, n - 1)
                        pe.matmul(k.PS[:, 6 + n % 2, :T], CTX[:, i, :], QT[:, i, c * T:(c + 1) * T],
                                  start=True, stop=True).then_inc(img_ready, 1)
                    pe.wait_ge(conv1_done, KC)
                    for n in range(KC * NT):
                        m, c = n // NT, n % NT
                        if n >= 2:
                            pe.wait_ge(tt_done, n - 1)
                        for i in range(KC):
                            mm = pe.matmul(k.PS[:, n % 2, :T], w_pr[:, i, m * P:(m + 1) * P],
                                           QT[:, i, c * T:(c + 1) * T], start=(i == 0), stop=(i == KC - 1))
                        mm.then_inc(pr_ready, 1)

                @block.scalar
                def _(act):
                    for n in range(KC * NT):
                        m, c = n // NT, n % NT
                        act.wait_ge(q_ready, n + 1)
                        act.activation(QT[:, m, c * T:(c + 1) * T], k.PS[:, n % 2, :T], ACT.Relu,
                                       bias=vec[:, m, BQ:BQ + 1]).then_inc(q_done, 1)
                    for t in range(LT):
                        act.wait_ge(kv_added, t + 1)
                        act.activation(KV[:, t, 0:C], KV[:, t, 0:C], ACT.Relu).then_inc(kv_done, 1)
                    act.wait_ge(img_zero, 1)
                    for n in range(KC * NT):
                        i, c = n // NT, n % NT
                        act.wait_ge(img_ready, n + 1)
                        act.activation(IMG[:, i, 1 + c * ROWS:1 + (c + 1) * ROWS, 1:1 + HW],
                                       k.PS[:, 6 + n % 2, :T].rearrange("p (r w) -> p r w", w=HW), ACT.Copy)\
                           .then_inc(img_done, 1)

                @block.gpsimd
                def _(pool):
                    pool.memset(IMG[:], 0.0).then_inc(img_zero, 1)

                @block.vector
                def _(dve):
                    for t in range(LT):
                        dve.wait_ge(kv_ready, t + 1)
                        dve.tensor_tensor(KV[:, t, :], k.PS[:, 2 + t % 2, :], bkv[:], ALU.add).then_inc(kv_added, 1)
                    dve.wait_ge(ctx_ready, 1)
                    for i in range(KC):
                        op = dve.tensor_tensor(CTX[:, i, :], k.PS[:, 4 + i, 0:P], hmask[:], ALU.mult)
                    op.then_inc(ctx_done, 1)
                    for i in range(KC):
                        dve.wait_ge(img_done, (i + 1) * NT)
                        acc = QT[:, i, :].rearrange("p (r w) -> p r w", w=HW)
                        for t in range(TAPS * TAPS):
                            y, x = t // TAPS, t % TAPS
                            win = IMG[:, i, y:y + HW, x:x + HW]
                            if t == 0:
                                dve.tensor_scalar(acc, win, dw[:, i, 0:1], vec[:, i, DWB:DWB + 1], ALU.mult, ALU.add)
                            else:
                                dve.drain()
                                op = dve.scalar_tensor_tensor(acc, win, dw[:, i, t:t + 1], acc, ALU.mult, ALU.add)
                        op.then_inc(conv1_done, 1)
                    for n in range(KC * NT):
                        m, c = n // NT, n % NT
                        dve.wait_ge(pr_ready, n + 1)
                        tt = TT[:, m, c * T:(c + 1) * T]
                        dve.scalar_tensor_tensor(tt, k.PS[:, n % 2, :T], vec[:, m, BPROJ:BPROJ + 1],
                                                 k.N[:, m, c * T:(c + 1) * T], ALU.add, ALU.add).then_inc(tt_done, 1)
                    dve.drain()
                    for m in range(KC):
                        dve.tensor_scalar(TT[:, m, :], TT[:, m, :], SB[:, m, 0, 0:1], SB[:, m, 0, 1:2], ALU.mult, ALU.add)
            fresh(nc, used)

        w1 = sb("w_fc1", [P, KC, CM])
        w2 = sb("w_fc2", [P, NM, C])
        b1 = sb("b_fc1", [P, NM])
        FF = sb("FF", [P, KC, T])
        used = sems(nc, ctx, "fc_loaded")
        with nc.Block() as block:
            @block.sync
            def _(sp):
                for dst, name in ((w1, "l1_w_fc1"), (w2, "l1_w_fc2"), (b1, "l1_b_fc1")):
                    sp.dma_start(dst[:], A[name]).then_inc(used[0], 16)
                sp.wait_ge(used[0], 48)
        fresh(nc, used)

        def add(dve, c):
            for o in range(KC):
                op = dve.scalar_tensor_tensor(FF[:, o, :], k.PS[:, 4 + o, :T], vec[:, o, BFC2:BFC2 + 1],
                                              TT[:, o, bass.ds(c * T, T)], ALU.add, ALU.add)
            dve.drain()
            for o in range(KC):
                dve.tensor_scalar(FF[:, o, :], FF[:, o, :], SB[:, o, 1, 0:1], SB[:, o, 1, 1:2], ALU.mult, ALU.add)
            dve.drain()
            x = k.X[:, :, bass.ds(b * L + c * T, T)]
            return dve.tensor_tensor(x, x, FF[:], ALU.add)

        two_layer(nc, ctx, k, b, TT, lambda i, m: w1[:, i, m * P:(m + 1) * P], lambda m: b1[:, m:m + 1],
                  lambda m, o: w2[:, m, o * P:(o + 1) * P], None, last=add)


H3 = 3 * C
FB = H3 // P
NH = 3
S = L // 3
ST = S // P
S2 = S // 2


def softmax_attention(nc, k, A, b):
    norm_image(nc, k, b, k.eps5)
    with ExitStack() as ctx:
        def sb(name, shape, dt=F32):
            return ctx.enter_context(nc.sbuf_tensor(k.name(name), shape, dt))

        w_e = sb("w_e", [P, FB, C])
        w_et = sb("w_et", [P, KC, H3])
        b_e = sb("b_e", [P, FB])
        w_o = sb("w_o2", [P, FB, C])
        b_o = sb("b_o2", [P, KC])
        XV = sb("XV", [P, ST, C])
        QE = sb("QE", [P, FB, S])
        R = sb("R", [P, KC, S])
        PR = sb("PR", [P, 2, S])
        PT = sb("PT", [P, ST, S])
        mx = sb("mx", [P, 2, 4])
        used = sems(nc, ctx, "l2_loaded", "xv_ready", "xv_done")
        l2_loaded, xv_ready, xv_done = used
        with nc.Block() as block:
            @block.sync
            def _(sp):
                sp.dma_start(w_o[:], A["l2_w_out"]).then_inc(l2_loaded, 16)
                sp.dma_start(b_o[:], A["l2_b_out"]).then_inc(l2_loaded, 16)
                sp.wait_ge(l2_loaded, 32)

            @block.tensor
            def _(pe):
                for t in range(ST):
                    if t >= 2:
                        pe.wait_ge(xv_done, t - 1)
                    for i in range(KC):
                        mm = pe.transpose(k.PS[:, t % 2, i * P:(i + 1) * P], k.N[:, i, 2 * S + t * P:2 * S + (t + 1) * P],
                                          k.ident[:])
                    mm.then_inc(xv_ready, 1)

            @block.vector
            def _(dve):
                for t in range(ST):
                    dve.wait_ge(xv_ready, t + 1)
                    dve.tensor_copy(XV[:, t, :], k.PS[:, t % 2, 0:C]).then_inc(xv_done, 1)
        fresh(nc, used)

        used = sems(nc, ctx, "head_loaded", "qe_ready", "qe_done", "r_ready", "r_done", "s_ready", "max_done",
                    "exp_done", "p_done", "pt_ready", "pt_done", "av_ready", "av_done", "ho_ready", "ho_done",
                    "out_ready", "out_done")
        (head_loaded, qe_ready, qe_done, r_ready, r_done, s_ready, max_done,
         exp_done, p_done, pt_ready, pt_done, av_ready, av_done, ho_ready, ho_done, out_ready, out_done) = used
        with nc.Fori(0, NH) as h:
            with nc.Block() as block:
                @block.sync
                def _(sp):
                    sp.dma_start(w_et[:], A["l2_w_et"][bass.ds(h, 1)].rearrange("o p i n -> (o p) i n")).then_inc(head_loaded, 16)
                    sp.dma_start(w_e[:], A["l2_w_e"][bass.ds(h, 1)].rearrange("o p i n -> (o p) i n")).then_inc(head_loaded, 16)
                    sp.dma_start(b_e[:], A["l2_b_e"][bass.ds(h, 1)].rearrange("o p i -> (o p) i")).then_inc(head_loaded, 16)
                    sp.wait_ge(head_loaded, 48)

                @block.tensor
                def _(pe):
                    pe.wait_ge(head_loaded, 48)
                    for n in range(FB * 2):
                        f, c = n // 2, n % 2
                        if n >= 2:
                            pe.wait_ge(qe_done, n - 1)
                        for i in range(KC):
                            mm = pe.matmul(k.PS[:, n % 2, :S2], w_et[:, i, f * P:(f + 1) * P],
                                           k.N[:, i, c * S2:(c + 1) * S2], start=(i == 0), stop=(i == KC - 1))
                        mm.then_inc(qe_ready, 1)
                    pe.wait_ge(qe_done, FB * 2)
                    for n in range(KC * 2):
                        o, c = n // 2, n % 2
                        for f in range(FB):
                            mm = pe.matmul(k.PS[:, 4 + n, :S2], w_e[:, f, o * P:(o + 1) * P],
                                           QE[:, f, c * S2:(c + 1) * S2], start=(f == 0), stop=(f == FB - 1))
                        mm.then_inc(r_ready, 1)
                    pe.wait_ge(r_done, KC * 2)
                    for t in range(ST + 1):
                        if t < ST:
                            if t >= 2:
                                pe.wait_ge(exp_done, t - 1)
                            for c in range(2):
                                for i in range(KC):
                                    mm = pe.matmul(k.PS[:, 2 * (t % 2) + c, :S2], R[:, i, t * P:(t + 1) * P],
                                                   k.N[:, i, S + c * S2:S + (c + 1) * S2],
                                                   start=(i == 0), stop=(i == KC - 1))
                            mm.then_inc(s_ready, 1)
                        if t >= 1:
                            v = t - 1
                            pe.wait_ge(p_done, v + 1)
                            for g in range(2):
                                if v >= 1:
                                    pe.wait_ge(pt_done, 2 * (v - 1) + g + 1)
                                for a in range(3):
                                    kt = 3 * g + a
                                    mm = pe.transpose(k.PS[:, 4 + g, a * P:(a + 1) * P], PR[:, v % 2, kt * P:(kt + 1) * P],
                                                      k.ident[:])
                                mm.then_inc(pt_ready, 1)
                    pe.wait_ge(pt_done, 2 * ST)
                    for n in range(KC * 2):
                        o, c = n // 2, n % 2
                        for kt in range(ST):
                            mm = pe.matmul(k.PS[:, n, :S2], XV[:, kt, o * P:(o + 1) * P],
                                           PT[:, kt, c * S2:(c + 1) * S2], start=(kt == 0), stop=(kt == ST - 1))
                        mm.then_inc(av_ready, 1)
                    pe.wait_ge(av_done, KC * 2)
                    for n in range(FB * 2):
                        f, c = n // 2, n % 2
                        if n >= 2:
                            pe.wait_ge(ho_done, n - 1)
                        for i in range(KC):
                            mm = pe.matmul(k.PS[:, 6 + n % 2, :S2], w_et[:, i, f * P:(f + 1) * P],
                                           R[:, i, c * S2:(c + 1) * S2], start=(i == 0), stop=(i == KC - 1))
                        mm.then_inc(ho_ready, 1)
                    pe.wait_ge(ho_done, FB * 2)
                    for n in range(KC * 2):
                        o, c = n // 2, n % 2
                        for f in range(FB):
                            mm = pe.matmul(k.PS[:, n, :S2], w_o[:, f, o * P:(o + 1) * P],
                                           QE[:, f, c * S2:(c + 1) * S2], start=(f == 0), stop=(f == FB - 1))
                        mm.then_inc(out_ready, 1)

                @block.scalar
                def _(act):
                    for n in range(FB * 2):
                        f, c = n // 2, n % 2
                        act.wait_ge(qe_ready, n + 1)
                        act.activation(QE[:, f, c * S2:(c + 1) * S2], k.PS[:, n % 2, :S2], ACT.Identity,
                                       bias=b_e[:, f:f + 1]).then_inc(qe_done, 1)
                    for t in range(ST):
                        act.wait_ge(max_done, t + 1)
                        act.activation(PR[:, t % 2, :].rearrange("p (c n) -> p c n", c=2),
                                       k.PS[:, 2 * (t % 2):2 * (t % 2) + 2, :S2], ACT.Exp, scale=C ** -0.5,
                                       bias=mx[:, t % 2, 1:2], accum_out=mx[:, t % 2, 2:3]).then_inc(exp_done, 1)
                        for g in range(2):
                            act.wait_ge(pt_ready, 2 * t + g + 1)
                            act.activation(PT[:, 3 * g:3 * g + 3, t * P:(t + 1) * P],
                                           k.PS[:, 4 + g, 0:3 * P].rearrange("p (a n) -> p a n", a=3), ACT.Copy)\
                               .then_inc(pt_done, 1)
                    for n in range(FB * 2):
                        f, c = n // 2, n % 2
                        act.wait_ge(ho_ready, n + 1)
                        act.activation(QE[:, f, c * S2:(c + 1) * S2], k.PS[:, 6 + n % 2, :S2], ACT.Identity,
                                       bias=b_e[:, f:f + 1]).then_inc(ho_done, 1)

                @block.vector
                def _(dve):
                    for n in range(KC * 2):
                        o, c = n // 2, n % 2
                        dve.wait_ge(r_ready, n + 1)
                        dve.tensor_copy(R[:, o, c * S2:(c + 1) * S2], k.PS[:, 4 + n, :S2]).then_inc(r_done, 1)
                    for t in range(ST):
                        m = mx[:, t % 2, :]
                        dve.wait_ge(s_ready, t + 1)
                        dve.tensor_reduce(m[:, 0:1], k.PS[:, 2 * (t % 2):2 * (t % 2) + 2, :S2], AX.XY, ALU.max)
                        dve.drain()
                        dve.tensor_scalar(m[:, 1:2], m[:, 0:1], -(C ** -0.5), None, ALU.mult).then_inc(max_done, 1)
                        dve.wait_ge(exp_done, t + 1)
                        dve.reciprocal(m[:, 3:4], m[:, 2:3])
                        dve.drain()
                        dve.tensor_scalar(PR[:, t % 2, :], PR[:, t % 2, :], m[:, 3:4], None, ALU.mult).then_inc(p_done, 1)
                    for n in range(KC * 2):
                        o, c = n // 2, n % 2
                        dve.wait_ge(av_ready, n + 1)
                        dve.tensor_copy(R[:, o, c * S2:(c + 1) * S2], k.PS[:, n, :S2]).then_inc(av_done, 1)
                    for n in range(KC * 2):
                        o, c = n // 2, n % 2
                        dve.wait_ge(out_ready, n + 1)
                        n_in = k.N[:, o, bass.ds(h * S + c * S2, S2)]
                        y = PR[:, 0, (n % 2) * S2:(n % 2 + 1) * S2]
                        dve.scalar_tensor_tensor(y, k.PS[:, n, :S2], b_o[:, o:o + 1], n_in, ALU.add, ALU.add)
                        dve.drain()
                        x = k.X[:, o, bass.ds(b * L + h * S + c * S2, S2)]
                        dve.tensor_tensor(x, x, y, ALU.add)
            fresh(nc, used)


E2 = 4
HE = E2 * E2
F2 = 2 * C
TM = M // P
EDGES = 1048576
EC = EDGES // P
SHIFT_BITS = 13
ROW = E2 + HE
TOP2 = 2
WINDOW = 60.0
GC = 8
HC_ = 16
BW = 1024
NBLK = EDGES // P // BW
NU = 2
HI = TM // 2
SLOPE = 0.2


def front(dve, V, D, D2, MV, width):
    cur, nxt = D, D2
    bits = width.bit_length() - 1
    for s in range(bits):
        w = width - (1 << s)
        dve.tensor_scalar(MV[:], cur[:], 1 << s, None, ALU.bitwise_and)
        dve.drain()
        if s < bits - 1:
            dve.scalar_tensor_tensor(nxt[:], MV[:], 0.0, cur[:], ALU.is_equal, ALU.mult)
            dve.drain()
            dve.copy_predicated(nxt[:, 0:w], MV[:, 1 << s:width], cur[:, 1 << s:width])
        dve.copy_predicated(V[:, 0:w], MV[:, 1 << s:width], V[:, 1 << s:width])
        dve.drain()
        cur, nxt = nxt, cur


def compact_edges(nc, k, A, g):
    with ExitStack() as ctx:
        def sb(name, shape, dt=I32):
            return ctx.enter_context(nc.sbuf_tensor(k.name(name), shape, dt))

        V, DSTS = sb("V", [P, EC]), sb("dsts", [P, EC])
        D, D2, MV = (sb(n, [P, EC], I16) for n in ("D", "D2", "MV"))
        used = sems(nc, ctx, "edges_in", "packed", "edges_out", "cnt_done", "cnt_row")
        edges_in, packed, edges_out, cnt_done, cnt_row = used
        with nc.Block() as block:
            @block.sync
            def _(sp):
                ei = A["edges"]
                sp.dma_start(V[:], ei[0].rearrange("(p c) -> p c", p=P)).then_inc(edges_in, 16)
                sp.dma_start(DSTS[:], ei[1].rearrange("(p c) -> p c", p=P)).then_inc(edges_in, 16)
                sp.wait_ge(packed, 1)
                sp.dma_start(k.edges_dram, V[:]).then_inc(edges_out, 16)
                sp.wait_ge(edges_out, 16)

            @block.vector
            def _(dve):
                dve.wait_ge(edges_in, 32)
                dve.tensor_scalar(MV[:], DSTS[:], float(M), None, ALU.is_ge)
                dve.tensor_scalar(V[:], V[:], float(M - 1), None, ALU.min)
                dve.drain()
                dve.tensor_tensor_scan(D[:], MV[:], MV[:], 0.0, ALU.add, ALU.max)
                dve.tensor_scalar(DSTS[:], DSTS[:], SHIFT_BITS, None, ALU.arith_shift_left)
                dve.drain()
                dve.tensor_tensor(V[:], V[:], DSTS[:], ALU.bitwise_or)
                dve.tensor_scalar(g.cnt[:], D[:, EC - 1:EC], -1.0, float(EC), ALU.mult, ALU.add).then_inc(cnt_done, 1)
                dve.drain()
                dve.scalar_tensor_tensor(D[:], MV[:], 0.0, D[:], ALU.is_equal, ALU.mult)
                dve.drain()
                front(dve, V, D, D2, MV, EC)
                dve.wait_ge(cnt_row, 1)
                dve.tensor_reduce(g.most[:, 0:1], k.PS[0:1, 0, 0:P], AX.X, ALU.max).then_inc(packed, 1)

            @block.tensor
            def _(pe):
                pe.wait_ge(cnt_done, 1)
                pe.matmul(k.PS[0:1, 0, 0:P], g.cnt[:], k.ident[:], start=True, stop=True).then_inc(cnt_row, 1)
        fresh(nc, used)


def split_block(nc, k, blk, held, g):
    with ExitStack() as ctx:
        def sb(name, shape, dt=I32):
            return ctx.enter_context(nc.sbuf_tensor(k.name(name), shape, dt))

        VB = sb("VB", [P, BW])
        S_, T_, X_ = (sb(n, [P, BW]) for n in ("S_", "T_", "X_"))
        LIVE, LAST, LOF, HIF, CH_ = (sb(n, [P, BW], F32) for n in ("LIVE", "LAST", "LOF", "HIFb", "CHb"))
        LOB, HIB = (sb(n, [P, BW], BF16) for n in ("LOB", "HIB"))
        OLB = sb("OLB", [P, NU, HC_, P], BF16)
        OHB = sb("OHB", [P, NU, HC_, TM], BF16)
        D, D2, MV = (sb(n, [P, BW], I16) for n in ("Db", "D2b", "MVb"))
        IDX = sb("IDX", [P, 2, BW])
        DIG = sb("DIG", [P, 2, BW], F32)
        lim = sb("lim", [P, 2], F32)
        used = sems(nc, ctx, "block_in", "hot_done", "hot_used", "count_done", "count_row", "lists_done", "lists_out")
        block_in, hot_done, hot_used, count_done, count_row, lists_done, lists_out = used

        def digits(dve, V, lo, hi):
            dve.tensor_scalar(T_[:], V[:], SHIFT_BITS, None, ALU.arith_shift_right)
            dve.drain()
            dve.tensor_scalar(X_[:], T_[:], P - 1, None, ALU.bitwise_and)
            dve.drain()
            dve.tensor_copy(lo, X_[:])
            dve.drain()
            dve.tensor_scalar(X_[:], T_[:], 7, None, ALU.arith_shift_right)
            dve.drain()
            dve.tensor_copy(hi, X_[:])
            dve.drain()

        with nc.Block() as block:
            @block.sync
            def _(sp):
                with sp.If(held > 0):
                    sp.dma_start(VB[:], k.edges_dram[:, bass.ds(blk * BW, BW)]).then_inc(block_in, 16)
                    sp.wait_ge(lists_done, 1)
                    for w in range(2):
                        sp.dma_start(k.idx_dram[w][:, bass.ds(blk * BW, BW)], IDX[:, w, :]).then_inc(lists_out, 16)
                        sp.dma_start(k.dig_dram[w][:, bass.ds(blk * BW, BW)], DIG[:, w, :]).then_inc(lists_out, 16)
                    sp.wait_ge(lists_out, 64)

            @block.vector
            def _(dve):
                with dve.If(held > 0):
                    dve.wait_ge(block_in, 16)
                    dve.tensor_scalar(lim[:, 0:1], g.left[:], 1.0, None, ALU.mult)
                    dve.tensor_scalar(S_[:], VB[:], (1 << SHIFT_BITS) - 1, None, ALU.bitwise_and)
                    dve.drain()
                    dve.tensor_scalar(LIVE[:], g.iota_b[:], lim[:, 0:1], None, ALU.is_lt)
                    dve.tensor_scalar(g.left[:], g.left[:], -float(BW), None, ALU.add)
                    dve.tensor_copy(CH_[:], S_[:])
                    dve.drain()
                    dve.scalar_tensor_tensor(LAST[:], CH_[:], float(M - 1), LIVE[:], ALU.is_equal, ALU.mult)
                    dve.drain()
                    dve.tensor_tensor(LIVE[:], LIVE[:], LAST[:], ALU.subtract)
                    digits(dve, VB, LOF[:], HIF[:])
                    dve.scalar_tensor_tensor(HIF[:], HIF[:], 1.0, LAST[:], ALU.add, ALU.mult)
                    dve.tensor_copy(LOB[:], LOF[:])
                    dve.drain()
                    dve.tensor_scalar(HIB[:], HIF[:], -1.0, None, ALU.add)
                    dve.drain()
                    with dve.Fori(0, BW // (NU * HC_)) as i:
                        with dve.If(held > i * (NU * HC_)):
                            for u in range(NU):
                                at = bass.ds(i * (NU * HC_) + u * HC_, HC_)
                                dve.wait_ge(hot_used, i * NU + u + 1)
                                dve.tensor_tensor(OLB[:, u, :, :], g.iota_h[:].rearrange("p (o n) -> p o n", o=1)
                                                  .broadcast_to([P, HC_, P]),
                                                  LOB[:, at].rearrange("p (c o) -> p c o", o=1).broadcast_to([P, HC_, P]),
                                                  ALU.is_equal)
                                dve.tensor_tensor(OHB[:, u, :, :], g.iota_h[:, 0:TM].rearrange("p (o n) -> p o n", o=1)
                                                  .broadcast_to([P, HC_, TM]),
                                                  HIB[:, at].rearrange("p (c o) -> p c o", o=1).broadcast_to([P, HC_, TM]),
                                                  ALU.is_equal).then_inc(hot_done, 1)
                    dve.tensor_scalar(MV[:], LIVE[:], -1.0, 1.0, ALU.mult, ALU.add)
                    dve.drain()
                    dve.tensor_tensor_scan(D[:], MV[:], MV[:], 0.0, ALU.add, ALU.max)
                    dve.drain()
                    dve.tensor_scalar(lim[:, 1:2], D[:, BW - 1:BW], -1.0, float(BW), ALU.mult, ALU.add).then_inc(count_done, 1)
                    dve.scalar_tensor_tensor(D2[:], MV[:], 0.0, D[:], ALU.is_equal, ALU.mult)
                    dve.drain()
                    front(dve, VB, D2, D, MV, BW)
                    dve.tensor_scalar(IDX[:, 0, :], VB[:], (1 << SHIFT_BITS) - 1, None, ALU.bitwise_and)
                    dve.tensor_scalar(IDX[:, 1, :], VB[:], SHIFT_BITS, None, ALU.arith_shift_right)
                    dve.tensor_scalar(LIVE[:], g.iota_b[:], lim[:, 1:2], None, ALU.is_lt)
                    digits(dve, VB, DIG[:, 0, :], HIF[:])
                    dve.tensor_scalar(IDX[:, 1, :], IDX[:, 1, :], float(M - 1), None, ALU.min)
                    dve.scalar_tensor_tensor(HIF[:], HIF[:], 1.0, LIVE[:], ALU.add, ALU.mult)
                    dve.drain()
                    dve.tensor_scalar(DIG[:, 1, :], HIF[:], -1.0, None, ALU.add)
                    dve.wait_ge(count_row, 1)
                    dve.tensor_reduce(g.most[:, 0:1], k.PS[0:1, 1, 0:P], AX.X, ALU.max)
                    dve.drain()
                    dve.tensor_copy(g.most_b[:, bass.ds(blk, 1)], g.most[:])
                    dve.tensor_tensor(g.HIST[:], g.HIST[:], k.PS[:, 0, 0:TM], ALU.add).then_inc(lists_done, 1)

            @block.tensor
            def _(pe):
                with pe.If(held > 0):
                    pe.sem_inc(hot_used, NU)
                    pe.matmul(k.PS[:, 0, 0:TM], k.zero_w[:], k.X[:, 0, 0:TM], start=True, stop=False)
                    with pe.Fori(0, BW // (NU * HC_)) as i:
                        with pe.If(held > i * (NU * HC_)):
                            for u in range(NU):
                                pe.wait_ge(hot_done, i * NU + u + 1)
                                for c in range(HC_):
                                    mm = pe.matmul(k.PS[:, 0, 0:TM], OLB[:, u, c, :], OHB[:, u, c, :], start=False, stop=False)
                                mm.then_inc(hot_used, 1)
                    pe.matmul(k.PS[:, 0, 0:TM], k.zero_w[:], k.X[:, 0, 0:TM], start=False, stop=True)
                    pe.wait_ge(count_done, 1)
                    pe.matmul(k.PS[0:1, 1, 0:P], lim[:, 1:2], k.ident[:], start=True, stop=True).then_inc(count_row, 1)
        fresh(nc, used)


def split_edges(nc, k, A, g):
    with ExitStack() as own:
        g.iota_b = own.enter_context(nc.sbuf_tensor("iota_b", [P, BW], F32))
        g.iota_h = own.enter_context(nc.sbuf_tensor("iota_h", [P, P], BF16))
        g.ahead = own.enter_context(nc.sbuf_tensor("ahead", [1, NBLK], F32))
        g.left = own.enter_context(nc.sbuf_tensor("left", [P, 1], F32))
        used = sems(nc, own, "iota_in")
        with nc.Block() as block:
            @block.sync
            def _(sp):
                sp.dma_start(g.iota_b[:], A["c_iota"].broadcast_to([P, BW])).then_inc(used[0], 16)

            @block.vector
            def _(dve):
                dve.memset(g.HIST[:], 0.0)
                dve.tensor_copy(g.left[:], g.cnt[:])
                dve.wait_ge(used[0], 16)
                dve.tensor_copy(g.iota_h[:], g.iota_b[:, 0:P])
                dve.tensor_scalar(g.ahead[:], g.iota_b[0:1, 0:NBLK], -float(BW), g.most[:], ALU.mult, ALU.add)
                dve.drain()
                dve.tensor_scalar(g.ahead[:], g.ahead[:], 0.0, float(BW), ALU.max, ALU.min)
                dve.drain()
                dve.tensor_copy(g.most_b[:], g.ahead[:])
        fresh(nc, used)
        with nc.Fori(0, NBLK) as blk:
            held = nc.values_load(g.most_b[0:1, bass.ds(blk, 1)], min_val=0, max_val=BW)
            split_block(nc, k, blk, held, g)


def graph_features(nc, k, A, b, g):
    norm_image(nc, k, b, k.eps5)
    with ExitStack() as ctx:
        tmp = ctx.enter_context(nc.sbuf_tensor(k.name("tmp_h"), [P, 2, LT, HE], F32))
        used = sems(nc, ctx, "h_ready")
        with nc.Block() as block:
            @block.tensor
            def _(pe):
                for t in range(LT):
                    for i in range(KC):
                        mm = pe.matmul(k.PS[:, 0, t * HE:(t + 1) * HE], k.N[:, i, t * P:(t + 1) * P], g.w_gat[:, i, :],
                                       start=(i == 0), stop=(i == KC - 1))
                mm.then_inc(used[0], 1)

            @block.vector
            def _(dve):
                dve.wait_ge(used[0], 1)
                h = k.PS[:, 0, 0:LT * HE].rearrange("p (t f) -> p t f", f=HE)
                dve.tensor_copy(g.GS[:, bass.ds(b * LT, LT), E2:ROW], h)
                for w in range(2):
                    att = g.att[:, w, :].rearrange("p (o f) -> p o f", o=1).broadcast_to([P, LT, HE])
                    dve.tensor_tensor(tmp[:, w, :, :], h, att, ALU.mult)
                dve.drain()
                for w in range(2):
                    dst = (g.GS if w == 0 else g.GD)[:, bass.ds(b * LT, LT), 0:E2]
                    dve.tensor_reduce(dst, tmp[:, w, :, :].rearrange("p t (h e) -> p t h e", e=E2), AX.X, ALU.add)
        fresh(nc, used)


def graph_mixture(nc, k, A):
    with ExitStack() as top:
        g = Core()

        def keep(name, shape, dt=F32):
            return top.enter_context(nc.sbuf_tensor(k.name(name), shape, dt))

        g.cnt = keep("cnt", [P, 1])
        g.most = keep("most", [1, 1])
        g.most_b = keep("most_b", [1, NBLK], I32)
        g.HIST = keep("HIST", [P, TM])
        compact_edges(nc, k, A, g)
        split_edges(nc, k, A, g)
        with ExitStack() as own:
            def sbo(name, shape, dt=F32):
                return own.enter_context(nc.sbuf_tensor(k.name(name), shape, dt))

            g.GS = sbo("GS", [P, TM, ROW])
            g.GD = sbo("GD", [P, TM, 2 * E2])
            g.w_gat = sbo("w_gat", [P, KC, HE])
            g.att = sbo("att", [P, 2, HE])
            g.rows = sbo("g_rows", [P, 3, HE])
            g.iota = sbo("g_iota", [P, P])
            g.SELF = sbo("SELF", [P, TM, E2])
            used = sems(nc, own, "g_loaded")
            with nc.Block() as block:
                @block.sync
                def _(sp):
                    sp.dma_start(g.w_gat[:], A["l2_w_gat"]).then_inc(used[0], 16)
                    sp.dma_start(g.att[:], A["l2_att"].broadcast_to([P, 2, HE])).then_inc(used[0], 16)
                    sp.dma_start(g.rows[:], A["l2_g_rows"].broadcast_to([P, 3, HE])).then_inc(used[0], 16)
                    sp.dma_start(g.iota[:], A["c_iota"][:, 0:P].broadcast_to([P, P])).then_inc(used[0], 16)
                    sp.wait_ge(used[0], 64)
            fresh(nc, used)
            with nc.Fori(0, NB) as b:
                graph_features(nc, k, A, b, g)
            graph_tables(nc, k, g)
            edge_sums(nc, k, g)
            gates(nc, k, g)
        with nc.Fori(0, NB) as b:
            gated_experts(nc, k, A, b)


def graph_tables(nc, k, g):
    with ExitStack() as ctx:
        def sb(name, shape, dt=F32):
            return ctx.enter_context(nc.sbuf_tensor(k.name(name), shape, dt))

        pm = sb("pm", [P, 2, E2])
        U = sb("U", [P, TM, E2])
        used = sems(nc, ctx, "part_max", "all_max", "table_done", "self_done", "tables_out")
        part_max, all_max, table_done, self_done, tables_out = used

        def leaky(dve, x):
            dve.scalar_tensor_tensor(x, x, SLOPE, x, ALU.mult, ALU.max)

        with nc.Block() as block:
            @block.vector
            def _(dve):
                dve.tensor_reduce(pm[:, 0, :], g.GS[:, :, 0:E2].rearrange("p t h -> p h t"), AX.X, ALU.max)\
                   .then_inc(part_max, 1)
                dve.tensor_tensor(g.SELF[:], g.GS[:, :, 0:E2], g.GD[:, :, 0:E2], ALU.add)
                dve.drain()
                leaky(dve, g.SELF[:])
                dve.wait_ge(all_max, 1)
                dve.tensor_tensor(U[:], g.GD[:, :, 0:E2],
                                  pm[:, 1, :].rearrange("p (o h) -> p o h", o=1).broadcast_to([P, TM, E2]), ALU.add)
                dve.drain()
                leaky(dve, U[:])
                dve.drain()
                dve.scalar_tensor_tensor(U[:], U[:], -WINDOW, g.SELF[:], ALU.add, ALU.max)
                dve.drain()
                dve.tensor_scalar(g.GD[:, :, E2:2 * E2], U[:], -1.0, None, ALU.mult)
                dve.tensor_tensor(g.SELF[:], g.SELF[:], U[:], ALU.subtract).then_inc(table_done, 1)

            @block.gpsimd
            def _(pool):
                pool.wait_ge(part_max, 1)
                pool.partition_all_reduce(pm[:, 1, :], pm[:, 0, :], P, bass.bass_isa.ReduceOp.max).then_inc(all_max, 1)

            @block.scalar
            def _(act):
                act.wait_ge(table_done, 1)
                act.activation(g.SELF[:], g.SELF[:], ACT.Exp).then_inc(self_done, 1)

            @block.sync
            def _(sp):
                sp.wait_ge(table_done, 1)
                sp.dma_start(k.src_dram.rearrange("(t p) f -> p t f", p=P), g.GS[:]).then_inc(tables_out, 16)
                sp.dma_start(k.dst_dram.rearrange("(t p) f -> p t f", p=P), g.GD[:]).then_inc(tables_out, 16)
                sp.wait_ge(tables_out, 32)
        fresh(nc, used)


def edge_sums(nc, k, g):
    def zeroes(start):
        with nc.Block() as block:
            @block.tensor
            def _(pe):
                for n in range(2):
                    pe.matmul(k.PS[:, 4 + n, 0:HI * ROW], k.zero_w[:], k.X[:, 0, 0:HI * ROW], start=start, stop=not start)

    zeroes(True)
    with nc.Fori(0, NBLK) as blk:
        longest = nc.values_load(g.most_b[0:1, bass.ds(blk, 1)], min_val=0, max_val=BW)
        with nc.If(longest > 0):
            block_sums(nc, k, g, blk, longest)
    zeroes(False)


def block_sums(nc, k, g, blk, longest):
    with ExitStack() as ctx:
        def sb(name, shape, dt=F32):
            return ctx.enter_context(nc.sbuf_tensor(k.name(name), shape, dt))

        IX = sb("IX", [P, NU, 2, GC], I32)
        DG = sb("DG", [P, NU, 2, GC])
        RS = sb("RS", [P, NU, GC * ROW])
        RD = sb("RD", [P, NU, GC * 2 * E2])
        W = sb("Wt", [P, NU, GC, E2])
        VL = sb("VL", [P, NU, GC, ROW])
        OL = sb("OL", [P, NU, GC, P])
        OH = sb("OHI", [P, NU, GC, TM])
        R = sb("Rr", [P, NU, GC, TM, ROW])
        used = sems(nc, ctx, "ix_in0", "ix_in1", "dg_in0", "dg_in1", "e_sum", "e_exp", "r_done", "added")
        ix_in0, ix_in1, dg_in0, dg_in1, e_sum, e_exp, r_done, added = used
        ix_in, dg_in = (ix_in0, ix_in1), (dg_in0, dg_in1)
        STEP = NU * GC
        rs_in, rd_in = k.rs_in, k.rd_in

        def hot(ap, n):
            return ap.rearrange("p (c o) -> p c o", o=1).broadcast_to([P, GC, n])

        with nc.Block() as block:
            @block.sync
            def _(sp):
                with sp.Fori(0, BW // STEP) as i:
                    with sp.If(longest > i * STEP):
                        for u in range(NU):
                            sp.wait_ge(r_done, i * NU + u + 1)
                            sp.sem_inc(k.turns, 1)
                            for w in range(2):
                                at = bass.ds(blk * BW + i * STEP + u * GC, GC)
                                sp.dma_start(IX[:, u, w, :], k.idx_dram[w][:, at]).then_inc(ix_in[u], 16)
                                sp.dma_start(DG[:, u, w, :], k.dig_dram[w][:, at]).then_inc(dg_in[u], 16)

            @block.gpsimd
            def _(pool):
                with pool.Fori(0, BW // STEP) as i:
                    with pool.If(longest > i * STEP):
                        for u in range(NU):
                            pool.wait_ge(ix_in[u], i * 32 + 32)
                            pool.sem_inc(k.turns, 1)
                            for c in range(GC):
                                pool.indirect_dma_start(
                                    out=RS[:, u, c * ROW:(c + 1) * ROW], out_offset=None, in_=k.src_dram,
                                    in_offset=bass.IndirectOffsetOnAxis(ap=IX[:, u, 0, c:c + 1], axis=0),
                                    bounds_check=M - 1, oob_is_err=False).then_inc(rs_in[u], 16)
                                pool.indirect_dma_start(
                                    out=RD[:, u, c * 2 * E2:(c + 1) * 2 * E2], out_offset=None, in_=k.dst_dram,
                                    in_offset=bass.IndirectOffsetOnAxis(ap=IX[:, u, 1, c:c + 1], axis=0),
                                    bounds_check=M - 1, oob_is_err=False).then_inc(rd_in[u], 16)

            def weigh(dve, i, u):
                rs = RS[:, u, :].rearrange("p (c f) -> p c f", f=ROW)
                rd = RD[:, u, :].rearrange("p (c f) -> p c f", f=2 * E2)
                w = W[:, u, :, :]
                dve.wait_ge(dg_in[u], i * 32 + 32)
                dve.wait_ge(added, i * NU + u + 1)
                dve.tensor_tensor(OL[:, u, :, :], g.iota[:].rearrange("p (o n) -> p o n", o=1).broadcast_to([P, GC, P]),
                                  hot(DG[:, u, 0, :], P), ALU.is_equal)
                dve.tensor_tensor(OH[:, u, :, :], g.iota[:, 0:TM].rearrange("p (o n) -> p o n", o=1)
                                  .broadcast_to([P, GC, TM]), hot(DG[:, u, 1, :], TM), ALU.is_equal)
                dve.wait_ge(rs_in[u], i * (16 * GC) + 16 * GC)
                dve.wait_ge(rd_in[u], i * (16 * GC) + 16 * GC)
                dve.tensor_tensor(w, rs[:, :, 0:E2], rd[:, :, 0:E2], ALU.add)
                dve.drain()
                dve.scalar_tensor_tensor(w, w, SLOPE, w, ALU.mult, ALU.max)
                dve.drain()
                dve.tensor_tensor(w, w, rd[:, :, E2:2 * E2], ALU.add).then_inc(e_sum, 1)
                dve.wait_ge(e_exp, i * NU + u + 1)
                vl = VL[:, u, :, :]
                dve.tensor_copy(vl[:, :, 0:E2], w)
                for c in range(GC):
                    dve.tensor_tensor(vl[:, c, E2:ROW].rearrange("p (h e) -> p h e", e=E2),
                                      rs[:, c, E2:ROW].rearrange("p (h e) -> p h e", e=E2),
                                      w[:, c, :].rearrange("p (h o) -> p h o", o=1).broadcast_to([P, E2, E2]), ALU.mult)
                dve.drain()
                for c in range(GC):
                    op = dve.tensor_tensor(R[:, u, c, :, :],
                                           OH[:, u, c, :].rearrange("p (t o) -> p t o", o=1).broadcast_to([P, TM, ROW]),
                                           vl[:, c, :].rearrange("p (o f) -> p o f", o=1).broadcast_to([P, TM, ROW]),
                                           ALU.mult)
                op.then_inc(r_done, 1)

            @block.vector
            def _(dve):
                dve.sem_inc(r_done, NU)
                with dve.Fori(0, BW // STEP) as i:
                    with dve.If(longest > i * STEP):
                        for u in range(NU):
                            weigh(dve, i, u)

            @block.scalar
            def _(act):
                with act.Fori(0, BW // STEP) as i:
                    with act.If(longest > i * STEP):
                        for u in range(NU):
                            act.wait_ge(e_sum, i * NU + u + 1)
                            act.activation(W[:, u, :, :], W[:, u, :, :], ACT.Exp).then_inc(e_exp, 1)

            @block.tensor
            def _(pe):
                pe.sem_inc(added, NU)
                with pe.Fori(0, BW // STEP) as i:
                    with pe.If(longest > i * STEP):
                        for u in range(NU):
                            pe.wait_ge(r_done, i * NU + u + 1 + NU)
                            for c in range(GC):
                                for n in range(2):
                                    mm = pe.matmul(k.PS[:, 4 + n, 0:HI * ROW], OL[:, u, c, :],
                                                   R[:, u, c, n * HI:(n + 1) * HI, :].rearrange("p t f -> p (t f)"),
                                                   start=False, stop=False)
                            mm.then_inc(added, 1)
        fresh(nc, used)
        with nc.Block() as block:
            @block.gpsimd
            def _(pool):
                for s in k.rs_in + k.rd_in:
                    pool.dma_reset(range(s.num, s.num + 1))
                    pool.sem_clear(s)


def gates(nc, k, g):
    with ExitStack() as ctx:
        def sb(name, shape, dt=F32):
            return ctx.enter_context(nc.sbuf_tensor(k.name(name), shape, dt))

        AG = sb("AG", [P, TM, ROW])
        Y = sb("Yg", [P, TM, HE])
        SQ = sb("SQg", [P, TM, HE])
        st = sb("stg", [P, 4, TM])
        SC = sb("SCg", [P, TM, E2])
        RK = sb("RKg", [P, TM, E2])
        GE = sb("GEg", [P, E2, TM])
        GR = sb("GRg", [2 * TM, 2, P])
        LR = sb("LRg", [P, ROW])
        LW = sb("LWg", [P, TM, E2])
        used = sems(nc, ctx, "lr_in", "lw_sum", "lw_exp", "g_var", "g_root", "g_diff", "g_exp", "ge_done", "gt_ready", "gt_done", "gates_out")
        lr_in, lw_sum, lw_exp, g_var, g_root, g_diff, g_exp, ge_done, gt_ready, gt_done, gates_out = used

        def over(ap, n):
            return ap.rearrange("p (t o) -> p t o", o=1).broadcast_to([P, TM, n])

        def row(i):
            return g.rows[:, i, :].rearrange("p (o f) -> p o f", o=1).broadcast_to([P, TM, HE])

        with nc.Block() as block:
            @block.vector
            def _(dve):
                for n in range(2):
                    dve.tensor_copy(AG[:, n * HI:(n + 1) * HI, :],
                                    k.PS[:, 4 + n, 0:HI * ROW].rearrange("p (t f) -> p t f", f=ROW))
                for h in range(E2):
                    dve.tensor_tensor(Y[:, :, h * E2:(h + 1) * E2], g.GS[:, :, E2 + h * E2:E2 + (h + 1) * E2],
                                      g.SELF[:, :, h:h + 1].broadcast_to([P, TM, E2]), ALU.mult)
                dve.drain()
                dve.tensor_tensor(AG[:, :, 0:E2], AG[:, :, 0:E2], g.SELF[:], ALU.add)
                dve.tensor_tensor(AG[:, :, E2:ROW], AG[:, :, E2:ROW], Y[:], ALU.add)
                dve.wait_ge(lr_in, 16)
                dve.tensor_tensor(LW[:], g.GD[:, :, 0:E2], LR[:, 0:E2].rearrange("p (o h) -> p o h", o=1)
                                  .broadcast_to([P, TM, E2]), ALU.add)
                dve.drain()
                dve.scalar_tensor_tensor(LW[:], LW[:], SLOPE, LW[:], ALU.mult, ALU.max)
                dve.drain()
                dve.tensor_tensor(LW[:], LW[:], g.GD[:, :, E2:2 * E2], ALU.add).then_inc(lw_sum, 1)
                dve.wait_ge(lw_exp, 1)
                dve.tensor_tensor(LW[:], LW[:], over(g.HIST[:], E2), ALU.mult)
                dve.drain()
                dve.tensor_tensor(AG[:, :, 0:E2], AG[:, :, 0:E2], LW[:], ALU.add)
                for h in range(E2):
                    for e in range(E2):
                        f = E2 + h * E2 + e
                        dve.scalar_tensor_tensor(AG[:, :, f], LW[:, :, h], LR[:, f:f + 1], AG[:, :, f], ALU.mult, ALU.add)
                dve.drain()
                dve.reciprocal(AG[:, :, 0:E2], AG[:, :, 0:E2])
                dve.drain()
                for h in range(E2):
                    dve.tensor_tensor(Y[:, :, h * E2:(h + 1) * E2], AG[:, :, E2 + h * E2:E2 + (h + 1) * E2],
                                      AG[:, :, h:h + 1].broadcast_to([P, TM, E2]), ALU.mult)
                dve.drain()
                dve.tensor_tensor(Y[:], Y[:], row(0), ALU.add)
                dve.drain()
                mean, var, diff, first = (st[:, i, :] for i in range(4))
                dve.tensor_reduce(mean, Y[:], AX.X, ALU.add)
                dve.drain()
                dve.tensor_scalar(mean, mean, 1.0 / HE, None, ALU.mult)
                dve.drain()
                dve.tensor_tensor(Y[:], Y[:], over(mean, HE), ALU.subtract)
                dve.drain()
                dve.tensor_tensor(SQ[:], Y[:], Y[:], ALU.mult)
                dve.drain()
                dve.tensor_reduce(var, SQ[:], AX.X, ALU.add)
                dve.drain()
                dve.tensor_scalar(var, var, 1.0 / HE, None, ALU.mult).then_inc(g_var, 1)
                dve.wait_ge(g_root, 1)
                dve.reciprocal(var, var)
                dve.drain()
                dve.tensor_tensor(Y[:], Y[:], over(var, HE), ALU.mult)
                dve.drain()
                dve.tensor_tensor(Y[:], Y[:], row(1), ALU.mult)
                dve.drain()
                dve.tensor_tensor(Y[:], Y[:], row(2), ALU.add)
                dve.drain()
                dve.tensor_reduce(SC[:], Y[:].rearrange("p t (h e) -> p t e h", e=E2), AX.X, ALU.add)
                dve.drain()
                dve.tensor_scalar(SC[:], SC[:], 1.0 / E2, None, ALU.mult)
                dve.memset(RK[:], 0.0)
                dve.drain()
                for e in range(E2):
                    for o in range(E2):
                        if o != e:
                            dve.tensor_tensor(diff, SC[:, :, o], SC[:, :, e], ALU.is_ge if o < e else ALU.is_gt)
                            dve.drain()
                            dve.tensor_tensor(RK[:, :, e], RK[:, :, e], diff, ALU.add)
                            dve.drain()
                dve.tensor_reduce(first, SC[:], AX.X, ALU.max)
                dve.tensor_scalar(SQ[:, :, 0:E2], RK[:], 1.0, None, ALU.is_equal)
                dve.tensor_scalar(SQ[:, :, E2:2 * E2], RK[:], 0.0, None, ALU.is_equal)
                dve.drain()
                dve.tensor_tensor(SC[:], SC[:], SQ[:, :, 0:E2], ALU.mult)
                dve.drain()
                dve.tensor_reduce(diff, SC[:], AX.X, ALU.add)
                dve.drain()
                dve.tensor_tensor(diff, diff, first, ALU.subtract).then_inc(g_diff, 1)
                dve.wait_ge(g_exp, 1)
                dve.tensor_scalar(first, diff, 1.0, None, ALU.add)
                dve.drain()
                dve.reciprocal(first, first)
                dve.tensor_tensor(SC[:], SQ[:, :, 0:E2], over(diff, E2), ALU.mult)
                dve.drain()
                dve.tensor_tensor(SC[:], SC[:], SQ[:, :, E2:2 * E2], ALU.add)
                dve.drain()
                dve.tensor_tensor(GE[:].rearrange("p e t -> p t e"), SC[:], over(first, E2), ALU.mult)\
                   .then_inc(ge_done, 1)
                dve.wait_ge(gt_ready, 1)
                dve.tensor_copy(GR[:], k.PS[0:2 * TM, 0:2, 0:P]).then_inc(gt_done, 1)

            @block.scalar
            def _(act):
                act.wait_ge(lw_sum, 1)
                act.activation(LW[:], LW[:], ACT.Exp).then_inc(lw_exp, 1)
                act.wait_ge(g_var, 1)
                act.activation(st[:, 1, :], st[:, 1, :], ACT.Sqrt, bias=k.eps5[:]).then_inc(g_root, 1)
                act.wait_ge(g_diff, 1)
                act.activation(st[:, 2, :], st[:, 2, :], ACT.Exp).then_inc(g_exp, 1)

            @block.tensor
            def _(pe):
                pe.wait_ge(ge_done, 1)
                for n in range(2):
                    mm = pe.transpose(k.PS[0:2 * TM, n, 0:P], GE[:, 2 * n:2 * n + 2, :].rearrange("p e t -> p (e t)"),
                                      k.ident[:])
                mm.then_inc(gt_ready, 1)

            @block.sync
            def _(sp):
                sp.dma_start(LR[:], k.src_dram[M - 1:M, :].broadcast_to([P, ROW])).then_inc(lr_in, 16)
                sp.wait_ge(lr_in, 16)
                sp.wait_ge(gt_done, 1)
                for n in range(2):
                    sp.dma_start(k.gate_dram[n * 2 * TM:(n + 1) * 2 * TM, :], GR[:, n, :]).then_inc(gates_out, 16)
                sp.wait_ge(gates_out, 32)
        fresh(nc, used)


def gated_experts(nc, k, A, b):
    norm_image(nc, k, b, k.eps5)
    with ExitStack() as ctx:
        def sb(name, shape, dt=F32):
            return ctx.enter_context(nc.sbuf_tensor(k.name(name), shape, dt))

        w1 = sb("w1g", [P, KC, E2 * F2])
        w2 = sb("w2g", [P, NM, C])
        b1 = sb("b1g", [P, NM])
        b2 = sb("b2g", [E2, C])
        GB = sb("GB", [P, E2, L])
        G4 = sb("G4", [E2, L])
        used = sems(nc, ctx, "x_loaded")
        with nc.Block() as block:
            @block.sync
            def _(sp):
                for dst, name in ((w1, "l2_w1"), (w2, "l2_w2"), (b1, "l2_b1"), (b2, "l2_b2")):
                    sp.dma_start(dst[:], A[name]).then_inc(used[0], 16)
                rows = k.gate_dram.rearrange("(e t) p -> e (t p)", e=E2)[:, bass.ds(b * L, L)]
                sp.dma_start(G4[:], rows).then_inc(used[0], 16)
                for e in range(E2):
                    sp.dma_start(GB[:, e, :], rows[e:e + 1, :].broadcast_to([P, L])).then_inc(used[0], 16)
                sp.wait_ge(used[0], 16 * (5 + E2))
        fresh(nc, used)

        def bias(pe, c):
            for o in range(KC):
                pe.matmul(k.PS[:, 4 + o, :T], b2[:, o * P:(o + 1) * P], G4[:, bass.ds(c * T, T)], start=True, stop=False)

        def add(dve, c):
            x = k.X[:, :, bass.ds(b * L + c * T, T)]
            return dve.tensor_tensor(x, x, k.PS[:, 4:4 + KC, :T], ALU.add)

        two_layer(nc, ctx, k, b, k.N, lambda i, m: w1[:, i, m * P:(m + 1) * P], lambda m: b1[:, m:m + 1],
                  lambda m, o: w2[:, m, o * P:(o + 1) * P], None,
                  gate=lambda m, c: GB[:, m // E2, bass.ds(c * T, T)], first=bias, last=add)




def transposed_image(nc, k, dst):
    with ExitStack() as own:
        used = sems(nc, own, "t_ready", "t_done")
        t_ready, t_done = used
        with nc.Block() as block:
            @block.tensor
            def _(pe):
                for t in range(LT):
                    if t >= 4:
                        pe.wait_ge(t_done, t - 3)
                    for i in range(KC):
                        mm = pe.transpose(k.PS[:, t % 4, i * P:(i + 1) * P], k.N[:, i, t * P:(t + 1) * P], k.ident[:])
                    mm.then_inc(t_ready, 1)

            @block.vector
            def _(dve):
                for t in range(LT):
                    dve.wait_ge(t_ready, t + 1)
                    dve.tensor_copy(dst[:, t, :], k.PS[:, t % 4, 0:C]).then_inc(t_done, 1)
        fresh(nc, used)


def sigmoid_attention(nc, k, A, b):
    norm_image(nc, k, b, k.eps5)
    with ExitStack() as ctx:
        def sb(name, shape, dt=F32):
            return ctx.enter_context(nc.sbuf_tensor(k.name(name), shape, dt))

        w_q = sb("w_q", [P, KC, C])
        QT = sb("QT3", [P, KC, L])
        XT = sb("XT3", [P, LT, C])
        NA = 3
        AT = sb("AT", [P, NA, T])
        transposed_image(nc, k, XT)
        used = sems(nc, ctx, "l3_loaded", "q3_ready", "q3_done")
        l3_loaded, q3_ready, q3_done = used
        with nc.Block() as block:
            @block.sync
            def _(sp):
                sp.dma_start(w_q[:], A["l3_w_q"]).then_inc(l3_loaded, 16)
                sp.wait_ge(l3_loaded, 16)

            @block.tensor
            def _(pe):
                pe.wait_ge(l3_loaded, 16)
                for n in range(KC * NT):
                    m, c = n // NT, n % NT
                    if n >= 4:
                        pe.wait_ge(q3_done, n - 3)
                    for i in range(KC):
                        mm = pe.matmul(k.PS[:, n % 4, :T], w_q[:, i, m * P:(m + 1) * P], k.N[:, i, c * T:(c + 1) * T],
                                       start=(i == 0), stop=(i == KC - 1))
                    mm.then_inc(q3_ready, 1)

            @block.scalar
            def _(act):
                for n in range(KC * NT):
                    m, c = n // NT, n % NT
                    act.wait_ge(q3_ready, n + 1)
                    act.activation(QT[:, m, c * T:(c + 1) * T], k.PS[:, n % 4, :T], ACT.Copy).then_inc(q3_done, 1)
        fresh(nc, used)

        used = sems(nc, ctx, "sc_ready", "att_done", "att_used", "val_ready", "val_used")
        sc_ready, att_done, att_used, val_ready, val_used = used
        with nc.Block() as block:
            @block.tensor
            def _(pe):
                pe.sem_inc(att_used, NA)
                with pe.Fori(0, NT) as c:
                    for s in range(LT + 2):
                        if s < LT:
                            pe.wait_ge(att_done, c * LT + s + 1)
                            for i in range(KC):
                                mm = pe.matmul(k.PS[:, s % NA, :T], k.N[:, i, s * P:(s + 1) * P],
                                               QT[:, i, bass.ds(c * T, T)], start=(i == 0), stop=(i == KC - 1))
                            mm.then_inc(sc_ready, 1)
                        if s >= 2:
                            m = s - 2
                            pe.wait_ge(att_done, c * LT + m + 1 + NA)
                            if m == 0:
                                pe.wait_ge(val_used, c + 1)
                            for o in range(KC):
                                mm = pe.matmul(k.PS[:, 4 + o, :T], XT[:, m, o * P:(o + 1) * P], AT[:, m % NA, :],
                                               start=(m == 0), stop=(m == LT - 1))
                            mm.then_inc(att_used, 1)
                    pe.drain().then_inc(val_ready, 1)

            @block.scalar
            def _(act):
                act.sem_inc(att_done, NA)
                with act.Fori(0, NT) as c:
                    for m in range(LT):
                        act.wait_ge(sc_ready, c * LT + m + 1)
                        act.wait_ge(att_used, c * LT + m + 1)
                        act.activation(AT[:, m % NA, :], k.PS[:, m % NA, :T], ACT.Sigmoid).then_inc(att_done, 1)

            @block.vector
            def _(dve):
                dve.sem_inc(val_used, 1)
                with dve.Fori(0, NT) as c:
                    dve.wait_ge(val_ready, c + 1)
                    x = k.X[:, :, bass.ds(b * L + c * T, T)]
                    dve.tensor_tensor(x, x, k.PS[:, 4:4 + KC, :T], ALU.add).then_inc(val_used, 1)
        fresh(nc, used)


NE = 8
F = 4 * C
FBE = F // P
CAP = (5 * M // 4 + NE - 1) // NE
RT = 120
NR = CAP // RT
CH = CAP // 2
NO_SLOT = 8192.0
ZW = NE * CAP * C // (P * 9)


def route_image(nc, k, A, b, st):
    norm_image(nc, k, b, k.eps5)
    with ExitStack() as ctx:
        def sb(name, shape, dt=F32):
            return ctx.enter_context(nc.sbuf_tensor(k.name(name), shape, dt))

        XT = sb("XT5", [P, LT, C])
        transposed_image(nc, k, XT)
        LG = sb("LG", [P, LT, NE])
        OH = sb("OH", [P, LT, NE])
        POS = sb("POS", [P, LT, NE])
        SEEN = sb("SEEN", [P, LT, 1])
        red = sb("red", [P, 6, LT])
        SI = sb("SI", [P, LT], I32)
        used = sems(nc, ctx, "lg_ready", "lg_shifted", "lg_exp", "oh_done", "count_ready", "slot_done")
        lg_ready, lg_shifted, lg_exp, oh_done, count_ready, slot_done = used

        def wide(ap):
            return ap.rearrange("p (t o) -> p t o", o=1).broadcast_to([P, LT, NE])

        with nc.Block() as block:
            @block.tensor
            def _(pe):
                for t in range(LT):
                    for i in range(KC):
                        mm = pe.matmul(k.PS[:, 0, t * NE:(t + 1) * NE], k.N[:, i, t * P:(t + 1) * P], st.gate_w[:, i, :],
                                       start=(i == 0), stop=(i == KC - 1))
                mm.then_inc(lg_ready, 1)
                pe.wait_ge(oh_done, 1)
                oh = OH[:].rearrange("p t e -> p (t e)")
                pe.matmul(k.PS[:, 1, 0:LT * NE], st.tri[:], oh, start=True, stop=True)
                pe.matmul(k.PS[:, 2, 0:LT * NE], st.ones[:], oh, start=True, stop=True).then_inc(count_ready, 1)

            @block.scalar
            def _(act):
                act.wait_ge(lg_shifted, 1)
                act.activation(LG[:], LG[:], ACT.Exp).then_inc(lg_exp, 1)

            @block.vector
            def _(dve):
                mx, total, prb, pos, base, kept = (red[:, i, :] for i in range(6))
                dve.wait_ge(lg_ready, 1)
                logits = k.PS[:, 0, 0:LT * NE].rearrange("p (t e) -> p t e", e=NE)
                dve.tensor_tensor(LG[:], logits,
                                  st.gate_b[:].rearrange("p (o e) -> p o e", o=1).broadcast_to([P, LT, NE]), ALU.add)
                dve.drain()
                dve.tensor_reduce(mx, LG[:], AX.X, ALU.max)
                dve.drain()
                dve.tensor_tensor(LG[:], LG[:], wide(mx), ALU.subtract).then_inc(lg_shifted, 1)
                dve.wait_ge(lg_exp, 1)
                dve.tensor_reduce(total, LG[:], AX.X, ALU.add)
                dve.drain()
                dve.reciprocal(total, total)
                dve.drain()
                dve.tensor_tensor(LG[:], LG[:], wide(total), ALU.mult)
                dve.drain()
                dve.tensor_reduce(prb, LG[:], AX.X, ALU.max)
                dve.drain()
                dve.tensor_tensor(OH[:], LG[:], wide(prb), ALU.is_equal)
                dve.drain()
                dve.tensor_copy(SEEN[:, :, 0], OH[:, :, 0])
                for e in range(1, NE):
                    dve.drain()
                    dve.tensor_copy(POS[:, :, 0], OH[:, :, e])
                    dve.drain()
                    dve.tensor_tensor(OH[:, :, e], POS[:, :, 0], SEEN[:, :, 0], ALU.is_gt)
                    dve.tensor_tensor(SEEN[:, :, 0], SEEN[:, :, 0], POS[:, :, 0], ALU.max)
                dve.drain()
                dve.tensor_copy(OH[:, 0, 0:1], OH[:, 0, 0:1]).then_inc(oh_done, 1)
                dve.wait_ge(count_ready, 1)
                tot = k.PS[:, 2, 0:LT * NE].rearrange("p (t e) -> p t e", e=NE)
                for t in range(LT):
                    dve.tensor_tensor(st.PF[:, t + 1, :], st.PF[:, t, :], tot[:, t, :], ALU.add)
                    dve.drain()
                dve.tensor_tensor(POS[:], k.PS[:, 1, 0:LT * NE].rearrange("p (t e) -> p t e", e=NE),
                                  st.PF[:, 0:LT, :], ALU.add)
                dve.drain()
                dve.tensor_copy(st.PF[:, 0, :], st.PF[:, LT, :])
                dve.tensor_tensor(POS[:], POS[:], OH[:], ALU.mult)
                dve.drain()
                dve.tensor_reduce(pos, POS[:], AX.X, ALU.add)
                dve.tensor_tensor(OH[:], OH[:], st.slot0[:].rearrange("p (o e) -> p o e", o=1)
                                  .broadcast_to([P, LT, NE]), ALU.mult)
                dve.drain()
                dve.tensor_reduce(base, OH[:], AX.X, ALU.add)
                dve.tensor_scalar(pos, pos, -1.0, None, ALU.add)
                dve.drain()
                dve.tensor_scalar(kept, pos, float(CAP), None, ALU.is_lt)
                dve.drain()
                dve.tensor_tensor(st.WT[:, bass.ds(b * LT, LT)], prb, kept, ALU.mult)
                dve.tensor_scalar(kept, kept, -NO_SLOT, NO_SLOT, ALU.mult, ALU.add)
                dve.tensor_scalar(total, pos, float(CAP - 1), None, ALU.min)
                dve.drain()
                dve.tensor_tensor(kept, kept, pos, ALU.add)
                dve.tensor_tensor(st.GI[:, bass.ds(b * LT, LT)], total, base, ALU.add)
                dve.drain()
                dve.tensor_tensor(SI[:], kept, base, ALU.add).then_inc(slot_done, 1)

            @block.gpsimd
            def _(pool):
                pool.wait_ge(slot_done, 1)
                for t in range(LT):
                    pool.indirect_dma_start(
                        out=k.buf_dram, out_offset=bass.IndirectOffsetOnAxis(ap=SI[:, t:t + 1], axis=0),
                        in_=XT[:, t, :], in_offset=None, bounds_check=NE * CAP - 1, oob_is_err=False)\
                        .then_inc(k.row_sent, 16)
                pool.wait_ge(k.row_sent, (b + 1) * (16 * LT))
        fresh(nc, used)


def capacity_mixture(nc, k, A):
    with ExitStack() as top:
        st = Core()

        def keep(name, shape, dt=F32):
            return top.enter_context(nc.sbuf_tensor(k.name(name), shape, dt))

        st.gate_w = keep("gate_w", [P, KC, NE])
        st.gate_b = keep("gate_b", [P, NE])
        st.slot0 = keep("slot0", [P, NE])
        st.tri = keep("tri", [P, P])
        st.ones = keep("ones", [P, P])
        st.PF = keep("PF", [P, LT + 1, NE])
        st.GI = keep("GI", [P, NB * LT], I32)
        st.WT = keep("WT", [P, NB * LT])
        with ExitStack() as own:
            zero = own.enter_context(nc.sbuf_tensor(k.name("zero"), [P, ZW], F32))
            used = sems(nc, own, "zeroed", "gate_in", "buf_clear")
            zeroed, gate_in, buf_clear = used
            with nc.Block() as block:
                @block.vector
                def _(dve):
                    dve.memset(st.PF[:, 0, :], 0.0)
                    dve.memset(st.ones[:], 1.0)
                    dve.memset(zero[:], 0.0).then_inc(zeroed, 1)

                @block.sync
                def _(sp):
                    sp.dma_start(st.gate_w[:], A["l3_gate_w"]).then_inc(gate_in, 16)
                    sp.dma_start(st.tri[:], A["c_tri"]).then_inc(gate_in, 16)
                    sp.dma_start(st.gate_b[:], A["l3_gate_b"].broadcast_to([P, NE])).then_inc(gate_in, 16)
                    sp.dma_start(st.slot0[:], A["c_slot0"].broadcast_to([P, NE])).then_inc(gate_in, 16)
                    sp.wait_ge(zeroed, 1)
                    for i in range(9):
                        sp.dma_start(k.buf_dram.rearrange("(i p r) c -> i p (r c)", i=9, p=P)[i], zero[:])\
                          .then_inc(buf_clear, 16)
                    sp.wait_ge(gate_in, 64)
                    sp.wait_ge(buf_clear, 144)
            fresh(nc, used)
        with nc.Fori(0, NB) as b:
            route_image(nc, k, A, b, st)
        with ExitStack() as own:
            experts(nc, own, k, A)
        with nc.Fori(0, NB) as b:
            combine_image(nc, k, b, st)


def experts(nc, ctx, k, A):
    def sb(name, shape, dt=F32):
        return ctx.enter_context(nc.sbuf_tensor(k.name(name), shape, dt))

    w1 = sb("ew1", [P, KC, F])
    w2 = sb("ew2", [P, FBE, C])
    b1 = sb("eb1", [P, FBE])
    b2 = sb("eb2", [P, C])
    XR = sb("XR", [RT, NR, C])
    XB = sb("XB", [P, KC, CAP])
    H = sb("HE", [P, FBE, CAP])
    YB = sb("YB", [RT, NR, C])
    used = sems(nc, ctx, "e_loaded", "rows_in", "x_ready", "x_done", "h5_ready", "h5_done", "y_ready", "y_done", "y_sent")
    e_loaded, rows_in, x_ready, x_done, h5_ready, h5_done, y_ready, y_done, y_sent = used
    with nc.Fori(0, NE) as e:
        with nc.Block() as block:
            @block.sync
            def _(sp):
                sp.dma_start(XR[:], k.buf_dram[bass.ds(e * CAP, CAP), :].rearrange("(t p) c -> p t c", p=RT))\
                  .then_inc(rows_in, 16)
                sp.dma_start(w1[:], A["l3_w1"][bass.ds(e, 1)].rearrange("o p i n -> (o p) i n")).then_inc(e_loaded, 16)
                sp.dma_start(w2[:], A["l3_w2"][bass.ds(e, 1)].rearrange("o p i n -> (o p) i n")).then_inc(e_loaded, 16)
                sp.dma_start(b1[:], A["l3_b1"][bass.ds(e, 1)].rearrange("o p i -> (o p) i")).then_inc(e_loaded, 16)
                sp.dma_start(b2[:], A["l3_b2"][bass.ds(e, 1), :].broadcast_to([P, C])).then_inc(e_loaded, 16)
                sp.wait_ge(e_loaded, 64)
                for t in range(NR):
                    sp.wait_ge(y_done, t + 1)
                    sp.dma_start(k.y_dram[bass.ds(e * CAP + t * RT, RT), :], YB[:, t, :]).then_inc(y_sent, 16)
                sp.wait_ge(y_sent, 16 * NR)

            @block.tensor
            def _(pe):
                pe.wait_ge(rows_in, 16)
                for t in range(NR):
                    if t >= 2:
                        pe.wait_ge(x_done, t - 1)
                    for i in range(KC):
                        mm = pe.transpose(k.PS[:, t % 2, i * RT:(i + 1) * RT], XR[:, t, i * P:(i + 1) * P],
                                          k.ident[0:RT, 0:RT])
                    mm.then_inc(x_ready, 1)
                pe.wait_ge(x_done, NR)
                pe.wait_ge(e_loaded, 64)
                for n in range(FBE * 2):
                    f, c = n // 2, n % 2
                    if n >= 3:
                        pe.wait_ge(h5_done, n - 2)
                    for i in range(KC):
                        mm = pe.matmul(k.PS[:, 2 + n % 3, :CH], w1[:, i, f * P:(f + 1) * P], XB[:, i, c * CH:(c + 1) * CH],
                                       start=(i == 0), stop=(i == KC - 1))
                    mm.then_inc(h5_ready, 1)
                pe.wait_ge(h5_done, FBE * 2)
                for t in range(NR):
                    if t >= 2:
                        pe.wait_ge(y_done, t - 1)
                    for f in range(FBE):
                        mm = pe.matmul(k.PS[0:RT, 6 + t % 2, :C], H[:, f, t * RT:(t + 1) * RT], w2[:, f, :],
                                       start=(f == 0), stop=(f == FBE - 1))
                    mm.then_inc(y_ready, 1)

            @block.scalar
            def _(act):
                act.wait_ge(e_loaded, 64)
                for n in range(FBE * 2):
                    f, c = n // 2, n % 2
                    act.wait_ge(h5_ready, n + 1)
                    act.activation(H[:, f, c * CH:(c + 1) * CH], k.PS[:, 2 + n % 3, :CH], ACT.Relu, bias=b1[:, f:f + 1])\
                       .then_inc(h5_done, 1)

            @block.vector
            def _(dve):
                for t in range(NR):
                    dve.wait_ge(x_ready, t + 1)
                    dve.tensor_copy(XB[:, :, t * RT:(t + 1) * RT],
                                    k.PS[:, t % 2, 0:KC * RT].rearrange("p (i r) -> p i r", i=KC)).then_inc(x_done, 1)
                dve.wait_ge(e_loaded, 64)
                for t in range(NR):
                    dve.wait_ge(y_ready, t + 1)
                    dve.tensor_tensor(YB[:, t, :], k.PS[0:RT, 6 + t % 2, :C], b2[0:RT, :], ALU.add).then_inc(y_done, 1)
        fresh(nc, used)


FMAX = float(np.finfo(np.float32).max)


def combine_image(nc, k, b, st):
    with ExitStack() as ctx:
        def sb(name, shape, dt=F32):
            return ctx.enter_context(nc.sbuf_tensor(k.name(name), shape, dt))

        YG = sb("YG", [P, LT, C])
        OK = sb("OK", [P, LT, C])
        MK = sb("MK", [P, 2, C], I32)
        big = sb("big", [P, 2, C])
        gi = sb("gi", [P, LT], I32)
        used = sems(nc, ctx, "gi_done", "y_clean", "yt_ready", "yt_added")
        gi_done, y_clean, yt_ready, yt_added = used

        def add(dve, t):
            dve.wait_ge(yt_ready, t + 1)
            x = k.X[:, :, bass.ds(b * L + t * P, P)]
            dve.tensor_tensor(x, x, k.PS[:, t % 4, 0:C].rearrange("p (i n) -> p i n", i=KC), ALU.add)\
               .then_inc(yt_added, 1)

        with nc.Block() as block:
            @block.gpsimd
            def _(pool):
                pool.wait_ge(gi_done, 1)
                for t in range(LT):
                    pool.indirect_dma_start(
                        out=YG[:, t, :], out_offset=None, in_=k.y_dram,
                        in_offset=bass.IndirectOffsetOnAxis(ap=gi[:, t:t + 1], axis=0),
                        bounds_check=NE * CAP - 1, oob_is_err=False).then_inc(k.row_in, 16)
                pool.wait_ge(k.row_in, (b + 1) * (16 * LT))

            @block.vector
            def _(dve):
                dve.tensor_copy(gi[:], st.GI[:, bass.ds(b * LT, LT)]).then_inc(gi_done, 1)
                dve.memset(OK[:], 0.0)
                dve.memset(big[:, 0, :], 1e4)
                dve.memset(big[:, 1, :], -1e4)
                dve.wait_ge(k.row_in, (b + 1) * (16 * LT))
                for t in range(LT):
                    y = YG[:, t, :]
                    dve.tensor_scalar(y, y, st.WT[:, bass.ds(b * LT + t, 1)], None, ALU.mult)
                    dve.drain()
                    dve.tensor_tensor(MK[:, 0, :], y, y, ALU.is_equal)
                    dve.drain()
                    dve.copy_predicated(OK[:, t, :], MK[:, 0, :], y)
                    dve.drain()
                    dve.tensor_scalar(MK[:, 0, :], OK[:, t, :], FMAX, None, ALU.is_gt)
                    dve.tensor_scalar(MK[:, 1, :], OK[:, t, :], -FMAX, None, ALU.is_lt)
                    dve.drain()
                    dve.copy_predicated(OK[:, t, :], MK[:, 0, :], big[:, 0, :])
                    dve.drain()
                    dve.copy_predicated(OK[:, t, :], MK[:, 1, :], big[:, 1, :]).then_inc(y_clean, 1)
                    if t >= 1:
                        add(dve, t - 1)
                add(dve, LT - 1)

            @block.tensor
            def _(pe):
                for t in range(LT):
                    pe.wait_ge(y_clean, t + 1)
                    if t >= 4:
                        pe.wait_ge(yt_added, t - 3)
                    for i in range(KC):
                        mm = pe.transpose(k.PS[:, t % 4, i * P:(i + 1) * P], OK[:, t, i * P:(i + 1) * P], k.ident[:])
                    mm.then_inc(yt_ready, 1)
        fresh(nc, used)




def build(nc, A, out, start=0, upto=99):
    with ExitStack() as ctx:
        k = Core()
        k.serial = 0

        def name(n):
            k.serial += 1
            return f"{n}_{k.serial}"

        k.name = name
        k.X = ctx.enter_context(nc.sbuf_tensor("X", [P, KC, M], F32))
        k.N = ctx.enter_context(nc.sbuf_tensor("N", [P, KC, L], F32))
        k.ident = ctx.enter_context(nc.sbuf_tensor("ident", [P, P], F32))
        k.mean_w = ctx.enter_context(nc.sbuf_tensor("mean_w", [P, P], F32))
        k.group_w = ctx.enter_context(nc.sbuf_tensor("group_w", [P, P], F32))
        k.zero_w = ctx.enter_context(nc.sbuf_tensor("zero_w", [P, P], F32))
        k.eps5 = ctx.enter_context(nc.sbuf_tensor("eps5", [P, 1], F32))
        k.PS = ctx.enter_context(nc.psum_tensor("PS", [P, 8, BANK], F32))
        k.proj_dram = nc.dram_tensor("proj_dram", [DR + 2 * DS, L], F32, kind="Internal").ap()
        k.edges_dram = nc.dram_tensor("edges_dram", [P, EC], I32, kind="Internal").ap()
        k.idx_dram = nc.dram_tensor("idx_dram", [2, P, EC], I32, kind="Internal").ap()
        k.dig_dram = nc.dram_tensor("dig_dram", [2, P, EC], F32, kind="Internal").ap()
        k.src_dram = nc.dram_tensor("src_dram", [M, ROW], F32, kind="Internal").ap()
        k.dst_dram = nc.dram_tensor("dst_dram", [M, 2 * E2], F32, kind="Internal").ap()
        k.gate_dram = nc.dram_tensor("gate_dram", [E2 * TM, P], F32, kind="Internal").ap()
        k.buf_dram = nc.dram_tensor("buf_dram", [NE * CAP, C], F32, kind="Internal").ap()
        k.y_dram = nc.dram_tensor("y_dram", [NE * CAP, C], F32, kind="Internal").ap()
        k.row_sent = ctx.enter_context(nc.semaphore("row_sent"))
        k.row_in = ctx.enter_context(nc.semaphore("row_in"))
        k.turns = ctx.enter_context(nc.semaphore("turns"))
        k.rs_in = [ctx.enter_context(nc.semaphore(f"rs_in{u}")) for u in range(NU)]
        k.rd_in = [ctx.enter_context(nc.semaphore(f"rd_in{u}")) for u in range(NU)]
        with nc.Block() as block:
            @block.vector
            def _(dve):
                dve.memset(k.zero_w[:], 0.0)
                dve.memset(k.eps5[:], 1e-5)
        load_constants(nc, ctx, k, A)
        if start <= 0 <= upto:
            with nc.Fori(0, NB) as b:
                mamba(nc, k, A, b)
        if start <= 1 <= upto:
            with nc.Fori(0, NB) as b:
                linear_attention_block(nc, k, A, b)
        if start <= 2 <= upto:
            with nc.Fori(0, NB) as b:
                softmax_attention(nc, k, A, b)
        if start <= 3 <= upto:
            graph_mixture(nc, k, A)
        if start <= 4 <= upto:
            with nc.Fori(0, NB) as b:
                sigmoid_attention(nc, k, A, b)
        if start <= 5 <= upto:
            capacity_mixture(nc, k, A)
        with ExitStack() as own:
            (stored,) = sems(nc, own, "stored")
            with nc.Block() as block:
                @block.sync
                def _(sp):
                    for b in range(NB):
                        sp.dma_start(out[b].rearrange("(k p) n -> p k n", p=P), k.X[:, :, b * L:(b + 1) * L])\
                          .then_inc(stored, 16)
                    sp.wait_ge(stored, 16 * NB)


def layout(inputs):
    a = {n: np.asarray(v) for n, v in inputs.items()}
    A = {"x": a["x"].reshape(NB, C, L)}

    def cols(w, kc):
        return w.reshape(kc, P, -1).transpose(1, 0, 2)

    A["c_ident"] = np.eye(P, dtype=np.float32)
    A["c_mean"] = np.full((P, P), 1.0 / C, np.float32)
    A["c_group"] = np.kron(np.eye(P // 8), np.full((8, 8), 1.0 / 8)).astype(np.float32)
    inv = (np.float32(1.0) / np.power(np.float32(10000.0), np.arange(0, C, 2, dtype=np.float32) / np.float32(C)))
    ang = (np.arange(L, dtype=np.float32)[:, None] * inv.astype(np.float32)[None, :]).astype(np.float32)
    pos = np.concatenate([np.sin(ang.astype(np.float64)), np.cos(ang.astype(np.float64))], -1).astype(np.float32)
    A["c_pos"] = cols(pos.T, KC)
    A["l0_ln"] = np.stack([a["L0_conv_ln_g"], a["L0_conv_ln_b"]], -1).reshape(KC, P, 2).transpose(1, 0, 2)
    A["L0_conv_pos_scale"] = a["L0_conv_pos_scale"]
    A["l0_w_in"] = cols(a["L0_conv_in_proj_w"].T, KC)
    A["l0_w_out"] = cols(a["L0_conv_out_proj_w"].T, JD)
    for d in "fb":
        A["l0_conv_w_" + d] = cols(a["L0_conv_conv_w_" + d], JD)
        A["l0_vec_" + d] = cols(np.stack([a["L0_conv_conv_b_" + d], a["L0_conv_dtproj_b_" + d], a["L0_conv_D_" + d]], -1), JD)
        A["l0_alog_" + d] = cols(a["L0_conv_A_log_" + d], JD)
        A["l0_w_x_" + d] = cols(a["L0_conv_xproj_w_" + d].T, JD)
        A["l0_w_dt_" + d] = a["L0_conv_dtproj_w_" + d].T
    A["c_head"] = np.kron(np.eye(P // 32), np.full((32, 32), 32.0 ** -0.5)).astype(np.float32)
    A["l1_vec"] = np.stack([a["L1_conv_bqkv"][:C], a["L1_conv_dw_b"], a["L1_conv_bproj"]]
                           + [a[f"L1_conv_bn{w}_{s}"] for w in "12" for s in "gbmv"] + [a["L1_conv_bfc2"]], -1)\
        .reshape(KC, P, 12).transpose(1, 0, 2)
    A["l1_bkv"] = a["L1_conv_bqkv"][C:].reshape(1, 2 * C)
    A["l1_alpha"] = np.stack([a["L1_conv_alpha1"], a["L1_conv_alpha2"]], -1).reshape(1, 2)
    A["l1_w_qkv"] = cols(a["L1_conv_Wqkv"], KC)
    A["l1_w_proj"] = cols(a["L1_conv_Wproj"], KC)
    A["l1_dw"] = cols(a["L1_conv_dw_w"].reshape(C, TAPS * TAPS), KC)
    A["l1_w_fc1"] = cols(a["L1_conv_Wfc1"], KC)
    A["l1_w_fc2"] = cols(a["L1_conv_Wfc2"], NM)
    A["l1_b_fc1"] = a["L1_conv_bfc1"].reshape(NM, P).T
    A["l2_w_et"] = a["L2_attn_W_embed"].transpose(0, 2, 1).reshape(NH, KC, P, H3).transpose(0, 2, 1, 3)
    A["l2_w_e"] = a["L2_attn_W_embed"].reshape(NH, FB, P, C).transpose(0, 2, 1, 3)
    A["l2_b_e"] = a["L2_attn_b_embed"].reshape(NH, FB, P).transpose(0, 2, 1)
    A["l2_w_out"] = cols(a["L2_attn_W_out"].T, FB)
    A["l2_b_out"] = a["L2_attn_b_out"].reshape(KC, P).T
    A["edges"] = a["L2_ffn_edge_index"]
    A["l2_w_gat"] = cols(a["L2_ffn_W_gat"], KC)
    A["l2_att"] = np.stack([a["L2_ffn_att_src"], a["L2_ffn_att_dst"]]).reshape(1, 2, HE)
    A["l2_g_rows"] = np.stack([a["L2_ffn_b_gat"], a["L2_ffn_ln_gamma"], a["L2_ffn_ln_beta"]]).reshape(1, 3, HE)
    A["c_iota"] = np.arange(BW, dtype=np.float32).reshape(1, BW)
    A["l2_w1"] = cols(a["L2_ffn_W1"].transpose(1, 0, 2).reshape(C, E2 * F2), KC)
    A["l2_w2"] = cols(a["L2_ffn_W2"].reshape(E2 * F2, C), NM)
    A["l2_b1"] = a["L2_ffn_b1"].reshape(NM, P).T
    A["l2_b2"] = a["L2_ffn_b2"]
    A["l3_w_q"] = cols(a["L3_attn_q_weight"], KC)
    A["c_tri"] = np.triu(np.ones((P, P), np.float32))
    A["c_slot0"] = (np.arange(NE, dtype=np.float32) * CAP).reshape(1, NE)
    A["l3_gate_w"] = cols(a["L3_ffn_gate_w"], KC)
    A["l3_gate_b"] = a["L3_ffn_gate_b"].reshape(1, NE)
    A["l3_w1"] = a["L3_ffn_w1"].reshape(NE, KC, P, F).transpose(0, 2, 1, 3)
    A["l3_w2"] = a["L3_ffn_w2"].reshape(NE, FBE, P, C).transpose(0, 2, 1, 3)
    A["l3_b1"] = a["L3_ffn_b1"].reshape(NE, FBE, P).transpose(0, 2, 1)
    A["l3_b2"] = a["L3_ffn_b2"]
    return {n: np.ascontiguousarray(v) for n, v in A.items()}


def kernel(**inputs):
    import concourse.bacc as bacc
    from concourse.bass_utils import run_bass_kernel_spmd

    nc = bacc.Bacc("TRN2", target_bir_lowering=False, num_devices=1)
    arrays = layout(inputs)
    A = {n: nc.dram_tensor(f"in_{n}", v.shape, mybir.dt.from_np(v.dtype), kind="ExternalInput").ap()
         for n, v in arrays.items()}
    out = nc.dram_tensor("out_0", (NB, C, L), F32, kind="ExternalOutput").ap()
    build(nc, A, out)
    r = run_bass_kernel_spmd(nc, [{f"in_{n}": v for n, v in arrays.items()}], core_ids=[0])
    return np.asarray(r.results[0]["out_0"]).reshape(NB, C, HW, HW)
```

```python
import concourse.bass as bass
from concourse import mybir
from contextlib import ExitStack

import numpy as np

F32 = mybir.dt.float32
I32 = mybir.dt.int32
I16 = mybir.dt.int16
BF16 = mybir.dt.bfloat16
ALU = mybir.AluOpType
ACT = mybir.ActivationFunctionType
AX = mybir.AxisListType

P = 128
NB = 2
C = 256
KC = C // P
HW = 48
L = HW * HW
M = NB * L
T = 384
NT = L // T
BANK = 512

DI = 512
JD = DI // P
DS = 16
DR = 16
NQ = 3
Q = L // NQ


def sems(nc, ctx, *names):
    return [ctx.enter_context(nc.semaphore(n)) for n in names]


def fresh(nc, used):
    with nc.Block() as block:
        @block.sync
        def _(sp):
            for s in used:
                sp.sem_clear(s)


class Core:
    pass


def load_constants(nc, ctx, k, A):
    with ExitStack() as own:
        (loaded,) = sems(nc, own, "loaded")
        with nc.Block() as block:
            @block.sync
            def _(sp):
                n = 0
                for b in range(NB):
                    sp.dma_start(k.X[:, :, b * L:(b + 1) * L],
                                 A["x"][b].rearrange("(k p) n -> p k n", p=P)).then_inc(loaded, 16)
                    n += 16
                for dst, name in ((k.ident, "c_ident"), (k.mean_w, "c_mean"), (k.group_w, "c_group")):
                    sp.dma_start(dst[:], A[name]).then_inc(loaded, 16)
                    n += 16
                sp.wait_ge(loaded, n)
        fresh(nc, [loaded])


def norm_image(nc, k, b, eps):
    DEEP = 3
    TT = T // P
    with ExitStack() as ctx:
        xs = ctx.enter_context(nc.sbuf_tensor(k.name("xs"), [P, DEEP, T], F32))
        sq = ctx.enter_context(nc.sbuf_tensor(k.name("sq"), [P, DEEP, KC, T], F32))
        rstd = ctx.enter_context(nc.sbuf_tensor(k.name("rstd"), [P, DEEP, TT], F32))
        used = sems(nc, ctx, "x_summed", "mean_ready", "centered", "squared", "var_ready", "rooted", "inverted",
                    "spread", "normalized")
        x_summed, mean_ready, centered, squared, var_ready, rooted, inverted, spread, normalized = used
        with nc.Block() as block:
            @block.gpsimd
            def _(pool):
                for s in range(NT):
                    if s >= DEEP:
                        pool.wait_ge(mean_ready, s - DEEP + 1)
                    at = bass.ds(b * L + s * T, T)
                    pool.tensor_tensor(xs[:, s % DEEP, :], k.X[:, 0, at], k.X[:, 1, at], ALU.add).then_inc(x_summed, 1)

            @block.tensor
            def _(pe):
                for s in range(NT + 2):
                    if s < NT:
                        pe.wait_ge(x_summed, s + 1)
                        if s >= DEEP:
                            pe.wait_ge(centered, s - DEEP + 1)
                        pe.matmul(k.PS[:, s % DEEP, :T], k.mean_w[:], xs[:, s % DEEP, :], start=True, stop=True)\
                          .then_inc(mean_ready, 1)
                    if 1 <= s <= NT:
                        v = s - 1
                        pe.wait_ge(squared, v + 1)
                        if v >= DEEP:
                            pe.wait_ge(normalized, v - DEEP + 1)
                        for t in range(TT):
                            for c in range(KC):
                                mm = pe.matmul(k.PS[:, DEEP + v % DEEP, t:t + 1], sq[:, v % DEEP, c, t * P:(t + 1) * P],
                                               k.mean_w[:, 0:1], start=(c == 0), stop=(c == KC - 1))
                        mm.then_inc(var_ready, 1)
                    if s >= 2:
                        v = s - 2
                        pe.wait_ge(inverted, v + 1)
                        for t in range(TT):
                            mm = pe.matmul(k.PS[:, DEEP + v % DEEP, P + t * P:2 * P + t * P],
                                           rstd[:, v % DEEP, t:t + 1].broadcast_to([P, P]), k.ident[:],
                                           start=True, stop=True)
                        mm.then_inc(spread, 1)

            @block.vector
            def _(dve):
                for s in range(NT + 2):
                    if s < NT:
                        dve.wait_ge(mean_ready, s + 1)
                        mean = k.PS[:, s % DEEP, :T].rearrange("p (o t) -> p o t", o=1).broadcast_to([P, KC, T])
                        dve.tensor_tensor(k.N[:, :, s * T:(s + 1) * T], k.X[:, :, bass.ds(b * L + s * T, T)],
                                          mean, ALU.subtract).then_inc(centered, 1)
                    if 1 <= s <= NT:
                        v = s - 1
                        dve.wait_ge(rooted, v + 1)
                        dve.reciprocal(rstd[:, v % DEEP, :], rstd[:, v % DEEP, :]).then_inc(inverted, 1)
                    if s >= 2:
                        v = s - 2
                        dve.wait_ge(spread, v + 1)
                        root = k.PS[:, DEEP + v % DEEP, P:P + T].rearrange("p (o t) -> p o t", o=1)\
                                .broadcast_to([P, KC, T])
                        n = k.N[:, :, v * T:(v + 1) * T]
                        dve.tensor_tensor(n, n, root, ALU.mult).then_inc(normalized, 1)

            @block.scalar
            def _(act):
                for s in range(NT + 1):
                    if s < NT:
                        act.wait_ge(centered, s + 1)
                        if s >= DEEP:
                            act.wait_ge(var_ready, s - DEEP + 1)
                        act.activation(sq[:, s % DEEP, :, :], k.N[:, :, s * T:(s + 1) * T], ACT.Square)\
                           .then_inc(squared, 1)
                    if s >= 1:
                        v = s - 1
                        act.wait_ge(var_ready, v + 1)
                        if v >= DEEP:
                            act.wait_ge(spread, v - DEEP + 1)
                        act.activation(rstd[:, v % DEEP, :], k.PS[:, DEEP + v % DEEP, 0:TT], ACT.Sqrt, bias=eps[:])\
                           .then_inc(rooted, 1)
        fresh(nc, used)


def mamba(nc, k, A, b):
    with ExitStack() as ctx:
        def sb(name, shape, dt=F32):
            return ctx.enter_context(nc.sbuf_tensor(k.name(name), shape, dt))

        w_in = sb("w_in", [P, KC, DI])
        XS = sb("XS", [P, JD, L])
        Y = sb("Y", [P, JD, L])
        gb = sb("gb", [P, KC, 2])
        pscale = sb("pscale", [P, 1])
        used = sems(nc, ctx, "l0_loaded", "l0_scaled")
        l0_loaded, l0_scaled = used
        pos = Y[:, 0:KC, :]
        with nc.Block() as block:
            @block.sync
            def _(sp):
                sp.dma_start(pos, A["c_pos"]).then_inc(l0_loaded, 16)
                sp.dma_start(gb[:], A["l0_ln"]).then_inc(l0_loaded, 16)
                sp.dma_start(pscale[:], A["L0_conv_pos_scale"].rearrange("(o n) -> o n", o=1)
                             .broadcast_to([P, 1])).then_inc(l0_loaded, 16)
                sp.dma_start(w_in[:], A["l0_w_in"][:, :, 0:DI]).then_inc(l0_loaded, 16)
        norm_image(nc, k, b, k.eps5)
        with nc.Block() as block:
            @block.scalar
            def _(act):
                act.wait_ge(l0_loaded, 64)
                act.activation(k.N[:, 1, :], k.N[:, 1, :], ACT.Identity, bias=gb[:, 1, 1:2], scale=gb[:, 1, 0:1])\
                   .then_inc(l0_scaled, 1)

            @block.vector
            def _(dve):
                dve.wait_ge(l0_loaded, 64)
                dve.tensor_scalar(k.N[:, 0, :], k.N[:, 0, :], gb[:, 0, 0:1], gb[:, 0, 1:2], ALU.mult, ALU.add)
                dve.drain()
                for c in range(KC):
                    if c == 1:
                        dve.wait_ge(l0_scaled, 1)
                    dve.scalar_tensor_tensor(k.N[:, c, :], pos[:, c, :], pscale[:], k.N[:, c, :], ALU.mult, ALU.add)
        fresh(nc, used)
        for rev in range(2):
            with ExitStack() as own:
                mamba_direction(nc, own, k, A, w_in, XS, Y, rev)
        mamba_output(nc, ctx, k, A, b, w_in, Y)


def mamba_direction(nc, ctx, k, A, w_in, XS, Y, rev):
    def sb(name, shape, dt=F32):
        return ctx.enter_context(nc.sbuf_tensor(k.name(name), shape, dt))

    d = "fb"[rev]
    PAD = 3
    region = sb("region", [P, 2 * JD * Q + 64])
    XP2 = region[:, 0:2 * (L + 2 * PAD)].rearrange("p (u t) -> p u t", u=2)
    DT = region[:, 0:JD * Q].rearrange("p (j t) -> p j t", j=JD)
    DU = region[:, JD * Q:2 * JD * Q].rearrange("p (j t) -> p j t", j=JD)
    work = sb("work", [P, 10, Q])
    PJ = work[0:3 * DS, 0:3, :].rearrange("p a t -> p (a t)")
    DA, DBU, G = (work[:, 2 * i:2 * i + 2, :] for i in range(3))
    HS = work[:, 6:6 + JD, :]
    diag = sb("diag", [P, JD, P])
    BB = sb("BB", [P, 2, Q])
    CB = sb("CB", [P, 2, Q])
    dtr = BB[0:DR, 0, :]
    conv_w = sb("conv_w", [P, JD, 4])
    vec = sb("vec", [P, JD, 3])
    alog = sb("alog", [P, JD, DS])
    w_x = sb("w_x", [P, JD, 3 * DS])
    w_dt = sb("w_dt", [DR, DI])
    HC = sb("HC", [P, JD, DS])

    used = sems(nc, ctx, "params", "xi_ready", "xi_copied", "conv_done", "xs_done", "pj_ready", "pj_copied",
                "pj_stored", "padded")
    params, xi_ready, xi_copied, conv_done, xs_done, pj_ready, pj_copied, pj_stored, padded = used
    with nc.Block() as block:
        @block.sync
        def _(sp):
            for dst, name in ((conv_w, "l0_conv_w_"), (vec, "l0_vec_"), (alog, "l0_alog_"), (w_x, "l0_w_x_"),
                              (w_dt, "l0_w_dt_")):
                sp.dma_start(dst[:], A[name + d]).then_inc(params, 16)
            sp.wait_ge(params, 80)
            sp.wait_ge(pj_copied, NT)
            sp.dma_start(k.proj_dram, PJ).then_inc(pj_stored, 16)
            sp.wait_ge(pj_stored, 16)

        @block.tensor
        def _(pe):
            for j in range(JD + 1):
                if j < JD:
                    for c in range(NT):
                        n = j * NT + c
                        if n >= 2:
                            pe.wait_ge(xi_copied, n - 1)
                        for i in range(KC):
                            mm = pe.matmul(k.PS[:, n % 2, :T], w_in[:, i, j * P:(j + 1) * P],
                                           k.N[:, i, c * T:(c + 1) * T], start=(i == 0), stop=(i == KC - 1))
                        mm.then_inc(xi_ready, 1)
                if j == 1:
                    pe.wait_ge(params, 80)
                if j >= 1:
                    pe.wait_ge(xs_done, j)
                    for c in range(NT):
                        mm = pe.matmul(k.PS[0:3 * DS, 2 + c, :T], w_x[:, j - 1, :], XS[:, j - 1, c * T:(c + 1) * T],
                                       start=(j == 1), stop=(j == JD))
                        if j == JD:
                            mm.then_inc(pj_ready, 1)

        @block.scalar
        def _(act):
            act.wait_ge(params, 80)
            for j in range(JD + 1):
                if j < JD:
                    if j >= 2:
                        act.wait_ge(conv_done, j - 1)
                    for c in range(NT):
                        act.wait_ge(xi_ready, j * NT + c + 1)
                        act.activation(XP2[:, j % 2, PAD + c * T:PAD + (c + 1) * T], k.PS[:, (j * NT + c) % 2, :T],
                                       ACT.Copy).then_inc(xi_copied, 1)
                if j >= 1:
                    act.wait_ge(conv_done, j)
                    act.activation(XS[:, j - 1, :], XS[:, j - 1, :], ACT.Silu, bias=vec[:, j - 1, 0:1])\
                       .then_inc(xs_done, 1)
            for c in range(NT):
                act.wait_ge(pj_ready, c + 1)
                act.activation(PJ[:, c * T:(c + 1) * T], k.PS[0:3 * DS, 2 + c, :T], ACT.Copy).then_inc(pj_copied, 1)

        @block.vector
        def _(dve):
            for u in range(2):
                dve.memset(XP2[:, u, 0:PAD], 0.0)
                dve.memset(XP2[:, u, PAD + L:2 * PAD + L], 0.0)
            dve.memset(HC[:], 0.0)
            dve.drain()
            dve.wait_ge(params, 80)
            for j in range(JD):
                dve.tensor_scalar(diag[:, j, :], k.ident[:], vec[:, j, 2:3], None, ALU.mult)
            for j in range(JD):
                dve.wait_ge(xi_copied, (j + 1) * NT)
                out = XS[:, j, :]
                for t in range(4):
                    at = 2 * PAD - t if rev else t
                    xp = XP2[:, j % 2, at:at + L]
                    if t == 0:
                        dve.tensor_scalar(out, xp, conv_w[:, j, 0:1], None, ALU.mult)
                    else:
                        dve.drain()
                        op = dve.scalar_tensor_tensor(out, xp, conv_w[:, j, t:t + 1], out, ALU.mult, ALU.add)
                op.then_inc(conv_done, 1)
    fresh(nc, used)

    with nc.Block() as block:
        @block.scalar
        def _(act):
            act.activation(alog[:], alog[:], ACT.Exp)
            act.drain()
            act.mul(alog[:], alog[:], -1.0)

    pieces = range(NQ - 1, -1, -1) if rev else range(NQ)
    H = Q // 2
    for q in pieces:
        t0 = q * Q
        used = sems(nc, ctx, "dtr_in", "dt_ready", "dt_exp", "dt_left", "dt_rest", "dt_log", "dt_done",
                    "b_in0", "b_in1", "c_in0", "c_in1", "da_done", "dbu_done", "h_done", "hc_done", "g_done", "acc_done") \
            if q == pieces[0] else used
        (dtr_in, dt_ready, dt_exp, dt_left, dt_rest, dt_log, dt_done,
         b_in0, b_in1, c_in0, c_in1, da_done, dbu_done, h_done, hc_done, g_done, acc_done) = used
        b_in, c_in = (b_in0, b_in1), (c_in0, c_in1)
        E, U, LN = work[:, 0:JD, :], work[:, JD:JD + 2, :], work[:, JD + 2:JD + 4, :]
        with nc.Block() as block:
            @block.sync
            def _(sp):
                sp.dma_start(dtr, k.proj_dram[0:DR, t0:t0 + Q]).then_inc(dtr_in, 16)
                sp.wait_ge(dtr_in, 16)

            @block.tensor
            def _(pe):
                pe.wait_ge(dtr_in, 16)
                for j in range(JD):
                    for h in range(2):
                        mm = pe.matmul(k.PS[:, 2 * j + h, :H], w_dt[:, j * P:(j + 1) * P], dtr[:, h * H:(h + 1) * H],
                                       start=True, stop=True)
                    mm.then_inc(dt_ready, 1)

            @block.scalar
            def _(act):
                def halves(ap):
                    return ap.rearrange("p (h t) -> p h t", h=2)

                for j in range(JD):
                    act.wait_ge(dt_ready, j + 1)
                    x = k.PS[:, 2 * j:2 * j + 2, :H]
                    act.activation(halves(E[:, j, :]), x, ACT.Abs, bias=vec[:, j, 1:2])
                    act.activation(halves(DT[:, j, :]), x, ACT.Relu, bias=vec[:, j, 1:2])
                    act.drain()
                    act.activation(E[:, j, :], E[:, j, :], ACT.Exp, scale=-1.0).then_inc(dt_exp, 1)
                act.drain()
                for j in range(JD):
                    if j >= 2:
                        act.wait_ge(dt_done, j - 1)
                    act.activation(LN[:, j % 2, :], E[:, j, :], ACT.Ln, bias=1.0).then_inc(dt_log, 1)

            @block.vector
            def _(dve):
                for j in range(JD):
                    dve.wait_ge(dt_exp, j + 1)
                    if j >= 2:
                        dve.wait_ge(dt_rest, j - 1)
                    dve.tensor_scalar(U[:, j % 2, :], E[:, j, :], 1.0, 1.0, ALU.add, ALU.subtract)
                    dve.drain()
                    dve.tensor_tensor(U[:, j % 2, :], E[:, j, :], U[:, j % 2, :], ALU.subtract).then_inc(dt_left, 1)
                for j in range(JD):
                    dve.wait_ge(dt_rest, j + 1)
                    dve.wait_ge(dt_log, j + 1)
                    dve.tensor_tensor(DT[:, j, :], DT[:, j, :], LN[:, j % 2, :], ALU.add).then_inc(dt_done, 1)
                    dve.drain()
                    if j % 2:
                        dve.tensor_tensor(DU[:, j, :], DT[:, j, :], XS[:, j, t0:t0 + Q], ALU.mult)

            @block.gpsimd
            def _(pool):
                for j in range(JD):
                    pool.wait_ge(dt_left, j + 1)
                    pool.tensor_tensor(DT[:, j, :], DT[:, j, :], U[:, j % 2, :], ALU.add).then_inc(dt_rest, 1)
                for j in range(0, JD, 2):
                    pool.wait_ge(dt_done, j + 1)
                    pool.tensor_tensor(DU[:, j, :], DT[:, j, :], XS[:, j, t0:t0 + Q], ALU.mult)

        def flow(ap):
            return ap[:, ::-1] if rev else ap

        FREE, SPARE = 2, JD + 1
        last = 0 if rev else Q - 1
        with nc.Block() as block:
            @block.sync
            def _(sp):
                with sp.Fori(0, DS // 2) as n2:
                    for u in range(2):
                        sp.wait_ge(dbu_done, n2 * (2 * JD) + u * JD + 1)
                        sp.wait_ge(g_done, n2 * (2 * JD) + u * JD + 1)
                        for row, dst, s in ((DR, BB, b_in[u]), (DR + DS, CB, c_in[u])):
                            sp.dma_start(dst[:, u, :],
                                         k.proj_dram[bass.ds(row + u + n2 * 2, 1), t0:t0 + Q].broadcast_to([P, Q]))\
                              .then_inc(s, 16)

            @block.scalar
            def _(act):
                def keep_state(n2, s):
                    u, j = divmod(s, JD)
                    act.activation(HC[:, j, bass.ds(n2 * 2 + u, 1)], HS[:, j, last:last + 1], ACT.Copy)\
                       .then_inc(hc_done, 1)

                act.sem_inc(hc_done, JD)
                with act.Fori(0, DS // 2) as n2:
                    for s in range(2 * JD):
                        u, j = divmod(s, JD)
                        act.wait_ge(h_done, n2 * (2 * JD) + s + 1)
                        act.activation(DA[:, j % 2, :], DT[:, j, :], ACT.Exp,
                                       scale=alog[:, j, bass.ds(n2 * 2 + u, 1)]).then_inc(da_done, 1)
                        if s >= FREE:
                            keep_state(n2, s - FREE)
                    for s in range(2 * JD - FREE, 2 * JD):
                        act.wait_ge(h_done, n2 * (2 * JD) + s + 1 + FREE)
                        keep_state(n2, s)

            @block.gpsimd
            def _(pool):
                pool.sem_inc(dbu_done, SPARE)
                with pool.Fori(0, DS // 2) as n2:
                    for u in range(2):
                        pool.wait_ge(b_in[u], n2 * 16 + 16)
                        for j in range(JD):
                            s = u * JD + j
                            pool.wait_ge(h_done, n2 * (2 * JD) + s + 1)
                            pool.tensor_tensor(DBU[:, j % 2, :], DU[:, j, :], BB[:, u, :], ALU.mult)\
                                .then_inc(dbu_done, 1)

            @block.vector
            def _(dve):
                dve.sem_inc(h_done, FREE)
                dve.sem_inc(g_done, SPARE)
                def weigh(n2, s):
                    u, j = divmod(s, JD)
                    if j == 0:
                        dve.wait_ge(c_in[u], n2 * 16 + 16)
                    dve.wait_ge(h_done, n2 * (2 * JD) + s + 1 + FREE)
                    dve.wait_ge(acc_done, n2 * (2 * JD) + s + 1)
                    dve.tensor_tensor(G[:, j % 2, :], HS[:, j, :], CB[:, u, :], ALU.mult).then_inc(g_done, 1)

                with dve.Fori(0, DS // 2) as n2:
                    for s in range(2 * JD):
                        u, j = divmod(s, JD)
                        dve.wait_ge(da_done, n2 * (2 * JD) + s + 1)
                        dve.wait_ge(dbu_done, n2 * (2 * JD) + s + 1 + SPARE)
                        dve.wait_ge(hc_done, n2 * (2 * JD) + s + 1)
                        dve.tensor_tensor_scan(flow(HS[:, j, :]), flow(DA[:, j % 2, :]), flow(DBU[:, j % 2, :]),
                                               HC[:, j, bass.ds(n2 * 2 + u, 1)], ALU.mult, ALU.add).then_inc(h_done, 1)
                        if s >= 1:
                            weigh(n2, s - 1)
                    weigh(n2, 2 * JD - 1)

            @block.tensor
            def _(pe):
                pe.sem_inc(acc_done, FREE)
                for j in range(JD):
                    for h in range(2):
                        at = slice(t0 + h * H, t0 + (h + 1) * H)
                        pe.matmul(k.PS[:, 2 * j + h, :H], diag[:, j, :], XS[:, j, at], start=True, stop=False)
                        if rev:
                            pe.matmul(k.PS[:, 2 * j + h, :H], k.ident[:], Y[:, j, at], start=False, stop=False)
                with pe.Fori(0, DS // 2) as n2:
                    for u in range(2):
                        for j in range(JD):
                            pe.wait_ge(g_done, n2 * (2 * JD) + u * JD + j + 1 + SPARE)
                            for h in range(2):
                                mm = pe.matmul(k.PS[:, 2 * j + h, :H], k.ident[:], G[:, j % 2, h * H:(h + 1) * H],
                                               start=False, stop=False)
                            mm.then_inc(acc_done, 1)
                for j in range(JD):
                    for h in range(2):
                        pe.matmul(k.PS[:, 2 * j + h, :H], k.zeros[:, 0:P], k.zeros[:, 0:H], start=False, stop=True)
        with nc.Block() as block:
            @block.vector
            def _(dve):
                for j in range(0, JD, 2):
                    dve.tensor_copy(Y[:, j, t0:t0 + Q].rearrange("p (h t) -> p h t", h=2), k.PS[:, 2 * j:2 * j + 2, :H])

            @block.scalar
            def _(act):
                for j in range(1, JD, 2):
                    act.activation(Y[:, j, t0:t0 + Q].rearrange("p (h t) -> p h t", h=2), k.PS[:, 2 * j:2 * j + 2, :H],
                                   ACT.Copy)
        fresh(nc, used)


def mamba_output(nc, ctx, k, A, b, w_in, Y):
    w_out = ctx.enter_context(nc.sbuf_tensor(k.name("w_out"), [P, JD, C], F32))
    Z = ctx.enter_context(nc.sbuf_tensor(k.name("Z"), [P, 2, T], F32))
    used = sems(nc, ctx, "wz_in", "wo_in", "z_ready", "z_done", "gated", "o_ready", "o_added")
    wz_in, wo_in, z_ready, z_done, gated, o_ready, o_added = used
    with nc.Block() as block:
        @block.sync
        def _(sp):
            sp.dma_start(w_in[:], A["l0_w_in"][:, :, DI:2 * DI]).then_inc(wz_in, 16)
            sp.dma_start(w_out[:], A["l0_w_out"]).then_inc(wo_in, 16)
            sp.wait_ge(wz_in, 16)
            sp.wait_ge(wo_in, 16)

        @block.tensor
        def _(pe):
            pe.wait_ge(wz_in, 16)
            for c in range(NT):
                for j in range(JD):
                    n = c * JD + j
                    if n >= 2:
                        pe.wait_ge(z_done, n - 1)
                    for i in range(KC):
                        mm = pe.matmul(k.PS[:, n % 2, :T], w_in[:, i, j * P:(j + 1) * P],
                                       k.N[:, i, c * T:(c + 1) * T], start=(i == 0), stop=(i == KC - 1))
                    mm.then_inc(z_ready, 1)
                pe.wait_ge(gated, (c + 1) * JD)
                if c == 0:
                    pe.wait_ge(wo_in, 16)
                else:
                    pe.wait_ge(o_added, c)
                for m in range(KC):
                    for j in range(JD):
                        mm = pe.matmul(k.PS[:, 2 + m, :T], w_out[:, j, m * P:(m + 1) * P], Y[:, j, c * T:(c + 1) * T],
                                       start=(j == 0), stop=(j == JD - 1))
                mm.then_inc(o_ready, 1)

        @block.scalar
        def _(act):
            for n in range(NT * JD):
                act.wait_ge(z_ready, n + 1)
                if n >= 2:
                    act.wait_ge(gated, n - 1)
                act.activation(Z[:, n % 2, :], k.PS[:, n % 2, :T], ACT.Silu).then_inc(z_done, 1)

        @block.vector
        def _(dve):
            for c in range(NT):
                for j in range(JD):
                    n = c * JD + j
                    dve.wait_ge(z_done, n + 1)
                    dve.tensor_tensor(Y[:, j, c * T:(c + 1) * T], Y[:, j, c * T:(c + 1) * T], Z[:, n % 2, :], ALU.mult)\
                       .then_inc(gated, 1)
                dve.wait_ge(o_ready, c + 1)
                x = k.X[:, :, bass.ds(b * L + c * T, T)]
                dve.tensor_tensor(x, x, k.PS[:, 2:2 + KC, :T], ALU.add).then_inc(o_added, 1)
    fresh(nc, used)


NHEAD = 8
CM = 2048
NM = CM // P
LT = L // P
ROWS = T // HW
TAPS = 3


def two_layer(nc, ctx, k, b, src, w1, b1, w2, gate=None, first=None, last=None,
              beside=None, last_act=None, last_pool=None):
    H = ctx.enter_context(nc.sbuf_tensor(k.name("H"), [P, NM, T], F32))
    used = sems(nc, ctx, "hid_ready", "hid_done", "hid_gated", "hid_used", "sum_ready", "sum_used", "sum_added")
    hid_ready, hid_done, hid_gated, hid_used, sum_ready, sum_used, sum_added = used
    feed = hid_gated if gate is not None else hid_done
    credit = 0 if gate is not None else 3
    with nc.Block() as block:
        @block.tensor
        def _(pe):
            pe.sem_inc(sum_ready, 1)
            with pe.Fori(0, NT) as c:
                for s in range(NM + 2):
                    if s < NM:
                        pe.wait_ge(hid_done, c * NM + s + 1)
                        for i in range(KC):
                            mm = pe.matmul(k.PS[:, (s % 3), :T], w1(i, s), src[:, i, bass.ds(c * T, T)],
                                           start=(i == 0), stop=(i == KC - 1))
                        mm.then_inc(hid_ready, 1)
                    if s >= 2:
                        m = s - 2
                        pe.wait_ge(feed, c * NM + m + 1 + credit)
                        if m == 0:
                            pe.wait_ge(sum_used, c + 1)
                            if first is not None:
                                first(pe, c)
                        for o in range(KC):
                            mm = pe.matmul(k.PS[:, 4 + o, :T], w2(m, o), H[:, m, :],
                                           start=(m == 0 and first is None), stop=(m == NM - 1))
                        mm.then_inc(hid_used if m < NM - 1 else sum_ready, 1)

        @block.scalar
        def _(act):
            act.sem_inc(hid_done, 3)
            with act.Fori(0, NT) as c:
                act.wait_ge(sum_ready, c + 1)
                for m in range(NM):
                    act.wait_ge(hid_ready, c * NM + m + 1)
                    act.activation(H[:, m, :], k.PS[:, m % 3, :T], ACT.Gelu, bias=b1(m)).then_inc(hid_done, 1)
                if beside is not None:
                    act.wait_ge(sum_ready, c + 2)
                    act.wait_ge(sum_added, c + 1)
                    last_act(act, c).then_inc(sum_used, 1)

        if beside is not None:
            @block.gpsimd
            def _(pool):
                pool.sem_inc(sum_added, 1)
                with pool.Fori(0, NT) as c:
                    pool.wait_ge(sum_used, c + 2)
                    last_pool(pool, c).then_inc(sum_added, 1)

            @block.sync
            def _(sp):
                beside.move(sp)

        @block.vector
        def _(dve):
            if beside is not None:
                dve.sem_inc(sum_used, 1)
                beside.pack(dve)
                return
            dve.sem_inc(sum_used, 1)
            with dve.Fori(0, NT) as c:
                if gate is not None:
                    for m in range(NM):
                        dve.wait_ge(hid_done, c * NM + m + 1 + 3)
                        dve.tensor_tensor(H[:, m, :], H[:, m, :], gate(m, c), ALU.mult).then_inc(hid_gated, 1)
                dve.wait_ge(sum_ready, c + 2)
                last(dve, c).then_inc(sum_used, 1)
    fresh(nc, used)


def linear_attention_block(nc, k, A, b):
    with ExitStack() as ctx:
        def sb(name, shape, dt=F32):
            return ctx.enter_context(nc.sbuf_tensor(k.name(name), shape, dt))

        vec = sb("vec1", [P, KC, 12])
        alpha = sb("alpha", [P, 2])
        SB = sb("SB", [P, KC, 2, 2])
        TT = sb("TT", [P, KC, L])
        sq = sb("sq1", [P, KC, 4])
        (BQ, DWB, BPROJ, BN, BFC2) = (0, 1, 2, 3, 11)
        w1 = sb("w_fc1", [P, KC, CM])
        w2 = sb("w_fc2", [P, NM, C])
        b1 = sb("b_fc1", [P, NM])
        (fc_loaded,) = sems(nc, ctx, "fc_loaded")

        with ExitStack() as own:
            def sbo(name, shape, dt=F32):
                return own.enter_context(nc.sbuf_tensor(k.name(name), shape, dt))

            w_qkv = sbo("w_qkv", [P, KC, 3 * C])
            w_pr = sbo("w_pr", [P, KC, C])
            bkv = sbo("bkv", [P, 2 * C])
            dw = sbo("dw", [P, KC, TAPS * TAPS])
            hmask = sbo("hmask", [P, P])
            QT = sbo("QT", [P, KC, L])
            KV = sbo("KV", [P, LT, 2 * C])
            CTX = sbo("CTX", [P, KC, P])
            IMG = sbo("IMG", [P, KC, HW + 2, HW + 2])
            stats = sbo("stats", [P, KC, NT, 6])
            mv = sbo("mv", [P, KC, 2])
            g = sbo("g", [P, KC, 4])
            used = sems(nc, own, "l1_loaded", "mv_done", "mg_ready", "vg_done", "root_done")
            l1_loaded, mv_done, mg_ready, vg_done, root_done = used
            with nc.Block() as block:
                @block.sync
                def _(sp):
                    n = 0
                    for dst, name in ((vec, "l1_vec"), (w_qkv, "l1_w_qkv"), (w_pr, "l1_w_proj"), (dw, "l1_dw"),
                                      (hmask, "c_head")):
                        sp.dma_start(dst[:], A[name]).then_inc(l1_loaded, 16)
                        n += 16
                    for dst, src in ((bkv[:], A["l1_bkv"].broadcast_to([P, 2 * C])),
                                     (alpha[:], A["l1_alpha"].broadcast_to([P, 2]))):
                        sp.dma_start(dst, src).then_inc(l1_loaded, 16)
                        n += 16
                    assert n == 112
                    for dst, name in ((w1, "l1_w_fc1"), (w2, "l1_w_fc2"), (b1, "l1_b_fc1")):
                        sp.dma_start(dst[:], A[name]).then_inc(fc_loaded, 16)
                    sp.wait_ge(l1_loaded, n)

                @block.vector
                def _(dve):
                    for i in range(KC):
                        for c in range(NT):
                            dve.bn_stats(stats[:, i, c, :], k.X[:, i, bass.ds(b * L + c * T, T)])
                    dve.drain()
                    for i in range(KC):
                        dve.bn_aggr(mv[:, i, :], stats[:, i, :, :].rearrange("p c s -> p (c s)"))
                    dve.drain()
                    dve.tensor_tensor(g[:, :, 0], mv[:, :, 0], mv[:, :, 0], ALU.mult)
                    dve.drain()
                    dve.tensor_tensor(mv[:, :, 1], mv[:, :, 1], g[:, :, 0], ALU.add).then_inc(mv_done, 1)
                    dve.wait_ge(mg_ready, 1)
                    gm = k.PS[:, 0, 0:2 * KC].rearrange("p (i s) -> p i s", i=KC)
                    dve.tensor_copy(g[:, :, 0:2], gm)
                    dve.drain()
                    dve.tensor_tensor(g[:, :, 2], g[:, :, 0], g[:, :, 0], ALU.mult)
                    dve.drain()
                    dve.tensor_tensor(g[:, :, 2], g[:, :, 1], g[:, :, 2], ALU.subtract).then_inc(vg_done, 1)
                    dve.wait_ge(root_done, 1)
                    dve.reciprocal(g[:, :, 3], g[:, :, 3])
                    dve.reciprocal(sq[:], sq[:])
                    dve.drain()
                    for i in range(KC):
                        dve.tensor_scalar(k.N[:, i, :], k.X[:, i, bass.ds(b * L, L)], g[:, i, 0:1], g[:, i, 3:4],
                                          ALU.subtract, ALU.mult)
                    for w in range(2):
                        bn = BN + 4 * w
                        dve.tensor_tensor(SB[:, :, w, 0], vec[:, :, bn], sq[:, :, w], ALU.mult)
                        dve.drain()
                        dve.tensor_tensor(SB[:, :, w, 1], vec[:, :, bn + 2], SB[:, :, w, 0], ALU.mult)
                        dve.drain()
                        dve.tensor_tensor(SB[:, :, w, 1], vec[:, :, bn + 1], SB[:, :, w, 1], ALU.subtract)
                        dve.tensor_scalar(SB[:, :, w, 0], SB[:, :, w, 0], alpha[:, w:w + 1], None, ALU.add)

                @block.tensor
                def _(pe):
                    pe.wait_ge(mv_done, 1)
                    pe.matmul(k.PS[:, 0, 0:2 * KC], k.group_w[:], mv[:].rearrange("p i s -> p (i s)"),
                              start=True, stop=True).then_inc(mg_ready, 1)

                @block.scalar
                def _(act):
                    act.wait_ge(l1_loaded, 112)
                    for w in range(2):
                        act.activation(sq[:, :, w], vec[:, :, BN + 4 * w + 3], ACT.Sqrt, bias=k.eps5[:])
                        act.activation(sq[:, :, 2 + w], vec[:, :, BN + 4 * w + 3], ACT.Sqrt, bias=k.eps5[:])
                    act.wait_ge(vg_done, 1)
                    act.activation(g[:, :, 3], g[:, :, 2], ACT.Sqrt, bias=k.eps5[:]).then_inc(root_done, 1)
            fresh(nc, used)

            used = sems(nc, own, "q_ready", "q_done", "kv_ready", "kv_added", "kv_done", "ctx_ready", "ctx_done",
                        "img_ready", "img_done", "img_zero", "conv1_done", "pr_ready", "tt_done")
            (q_ready, q_done, kv_ready, kv_added, kv_done, ctx_ready, ctx_done,
             img_ready, img_done, img_zero, conv1_done, pr_ready, tt_done) = used
            with nc.Block() as block:
                @block.tensor
                def _(pe):
                    for n in range(KC * NT):
                        m, c = n // NT, n % NT
                        if n >= 2:
                            pe.wait_ge(q_done, n - 1)
                        for i in range(KC):
                            mm = pe.matmul(k.PS[:, n % 2, :T], w_qkv[:, i, m * P:(m + 1) * P],
                                           k.N[:, i, c * T:(c + 1) * T], start=(i == 0), stop=(i == KC - 1))
                        mm.then_inc(q_ready, 1)
                    for t in range(LT + 1):
                        if t < LT:
                            if t >= 2:
                                pe.wait_ge(kv_added, t - 1)
                            for i in range(KC):
                                mm = pe.matmul(k.PS[:, 2 + t % 2, :], k.N[:, i, t * P:(t + 1) * P], w_qkv[:, i, C:3 * C],
                                               start=(i == 0), stop=(i == KC - 1))
                            mm.then_inc(kv_ready, 1)
                        if t >= 1:
                            pe.wait_ge(kv_done, t)
                            for i in range(KC):
                                mm = pe.matmul(k.PS[:, 4 + i, 0:P], KV[:, t - 1, i * P:(i + 1) * P],
                                               KV[:, t - 1, C + i * P:C + (i + 1) * P], start=(t == 1), stop=(t == LT))
                    mm.then_inc(ctx_ready, 1)
                    pe.wait_ge(ctx_done, 1)
                    pe.wait_ge(q_done, KC * NT)
                    for n in range(KC * NT):
                        i, c = n // NT, n % NT
                        if n >= 2:
                            pe.wait_ge(img_done, n - 1)
                        pe.matmul(k.PS[:, 6 + n % 2, :T], CTX[:, i, :], QT[:, i, c * T:(c + 1) * T],
                                  start=True, stop=True).then_inc(img_ready, 1)
                    pe.wait_ge(conv1_done, KC)
                    for n in range(KC * NT):
                        m, c = n // NT, n % NT
                        if n >= 2:
                            pe.wait_ge(tt_done, n - 1)
                        for i in range(KC):
                            mm = pe.matmul(k.PS[:, n % 2, :T], w_pr[:, i, m * P:(m + 1) * P],
                                           QT[:, i, c * T:(c + 1) * T], start=(i == 0), stop=(i == KC - 1))
                        mm.then_inc(pr_ready, 1)

                @block.scalar
                def _(act):
                    for n in range(KC * NT):
                        m, c = n // NT, n % NT
                        act.wait_ge(q_ready, n + 1)
                        act.activation(QT[:, m, c * T:(c + 1) * T], k.PS[:, n % 2, :T], ACT.Relu,
                                       bias=vec[:, m, BQ:BQ + 1]).then_inc(q_done, 1)
                    for t in range(LT):
                        act.wait_ge(kv_added, t + 1)
                        act.activation(KV[:, t, 0:C], KV[:, t, 0:C], ACT.Relu).then_inc(kv_done, 1)
                    act.wait_ge(img_zero, 1)
                    for n in range(KC * NT):
                        i, c = n // NT, n % NT
                        act.wait_ge(img_ready, n + 1)
                        act.activation(IMG[:, i, 1 + c * ROWS:1 + (c + 1) * ROWS, 1:1 + HW],
                                       k.PS[:, 6 + n % 2, :T].rearrange("p (r w) -> p r w", w=HW), ACT.Copy)\
                           .then_inc(img_done, 1)

                @block.gpsimd
                def _(pool):
                    pool.memset(IMG[:], 0.0).then_inc(img_zero, 1)

                @block.vector
                def _(dve):
                    for t in range(LT):
                        dve.wait_ge(kv_ready, t + 1)
                        dve.tensor_tensor(KV[:, t, :], k.PS[:, 2 + t % 2, :], bkv[:], ALU.add).then_inc(kv_added, 1)
                    dve.wait_ge(ctx_ready, 1)
                    for i in range(KC):
                        op = dve.tensor_tensor(CTX[:, i, :], k.PS[:, 4 + i, 0:P], hmask[:], ALU.mult)
                    op.then_inc(ctx_done, 1)
                    for i in range(KC):
                        dve.wait_ge(img_done, (i + 1) * NT)
                        acc = QT[:, i, :].rearrange("p (r w) -> p r w", w=HW)
                        for t in range(TAPS * TAPS):
                            y, x = t // TAPS, t % TAPS
                            win = IMG[:, i, y:y + HW, x:x + HW]
                            if t == 0:
                                dve.tensor_scalar(acc, win, dw[:, i, 0:1], vec[:, i, DWB:DWB + 1], ALU.mult, ALU.add)
                            else:
                                dve.drain()
                                op = dve.scalar_tensor_tensor(acc, win, dw[:, i, t:t + 1], acc, ALU.mult, ALU.add)
                        op.then_inc(conv1_done, 1)
                    for n in range(KC * NT):
                        m, c = n // NT, n % NT
                        dve.wait_ge(pr_ready, n + 1)
                        tt = TT[:, m, c * T:(c + 1) * T]
                        dve.scalar_tensor_tensor(tt, k.PS[:, n % 2, :T], vec[:, m, BPROJ:BPROJ + 1],
                                                 k.N[:, m, c * T:(c + 1) * T], ALU.add, ALU.add).then_inc(tt_done, 1)
                    dve.drain()
                    for m in range(KC):
                        dve.tensor_scalar(TT[:, m, :], TT[:, m, :], SB[:, m, 0, 0:1], SB[:, m, 0, 1:2], ALU.mult, ALU.add)
            fresh(nc, used)

        FF = sb("FF", [P, KC, L])
        EV = sb("EV", [P, KC, T])
        lists = EdgeLists(nc, ctx, k, A["edges"], b)
        with nc.Block() as block:
            @block.scalar
            def _(act):
                act.wait_ge(fc_loaded, 48)
                for o in range(KC):
                    act.activation(SB[:, o, 1, 1:2], vec[:, o, BFC2:BFC2 + 1], ACT.Identity, bias=SB[:, o, 1, 1:2],
                                   scale=SB[:, o, 1, 0:1])
                act.drain()
                for o in range(KC):
                    act.activation(FF[:, o, :], TT[:, o, :], ACT.Identity, bias=SB[:, o, 1, 1:2], scale=SB[:, o, 1, 0:1])
        fresh(nc, [fc_loaded])

        def empty(act, c):
            for o in range(KC):
                op = act.activation(EV[:, o, :], k.PS[:, 4 + o, :T], ACT.Copy, scale=SB[:, o, 1, 0:1])
            return op

        def add(pool, c):
            x = k.X[:, :, bass.ds(b * L + c * T, T)]
            pool.tensor_tensor(x, x, FF[:, :, bass.ds(c * T, T)], ALU.add)
            pool.drain()
            return pool.tensor_tensor(x, x, EV[:], ALU.add)

        two_layer(nc, ctx, k, b, TT, lambda i, m: w1[:, i, m * P:(m + 1) * P], lambda m: b1[:, m:m + 1],
                  lambda m, o: w2[:, m, o * P:(o + 1) * P], beside=lists, last_act=empty, last_pool=add)
        fresh(nc, lists.used)
H3 = 3 * C
FB = H3 // P
NH = 3
S = L // 3
ST = S // P
S2 = S // 2


def softmax_attention(nc, k, A, b):
    norm_image(nc, k, b, k.eps5)
    with ExitStack() as ctx:
        def sb(name, shape, dt=F32):
            return ctx.enter_context(nc.sbuf_tensor(k.name(name), shape, dt))

        w_e = sb("w_e", [P, FB, C])
        w_et = sb("w_et", [P, KC, H3])
        b_e = sb("b_e", [P, FB])
        w_o = sb("w_o2", [P, FB, C])
        b_o = sb("b_o2", [P, KC])
        XV = sb("XV", [P, ST, C])
        QE = sb("QE", [P, FB, S])
        R = sb("R", [P, KC, S])
        PR = sb("PR", [P, 2, S])
        PT = sb("PT", [P, ST, S])
        mx = sb("mx", [P, 2, 4])
        used = sems(nc, ctx, "l2_loaded", "xv_ready", "xv_done")
        l2_loaded, xv_ready, xv_done = used
        with nc.Block() as block:
            @block.sync
            def _(sp):
                sp.dma_start(w_o[:], A["l2_w_out"]).then_inc(l2_loaded, 16)
                sp.dma_start(b_o[:], A["l2_b_out"]).then_inc(l2_loaded, 16)
                sp.wait_ge(l2_loaded, 32)

            @block.tensor
            def _(pe):
                for t in range(ST):
                    if t >= 2:
                        pe.wait_ge(xv_done, t - 1)
                    for i in range(KC):
                        mm = pe.transpose(k.PS[:, t % 2, i * P:(i + 1) * P], k.N[:, i, 2 * S + t * P:2 * S + (t + 1) * P],
                                          k.ident[:])
                    mm.then_inc(xv_ready, 1)

            @block.vector
            def _(dve):
                for t in range(ST):
                    dve.wait_ge(xv_ready, t + 1)
                    dve.tensor_copy(XV[:, t, :], k.PS[:, t % 2, 0:C]).then_inc(xv_done, 1)
        fresh(nc, used)

        used = sems(nc, ctx, "head_loaded", "qe_ready", "qe_done", "r_ready", "r_done", "s_ready", "max_done",
                    "exp_done", "p_done", "pt_ready", "pt_done", "av_ready", "av_done", "ho_ready", "ho_done",
                    "out_ready", "out_done")
        (head_loaded, qe_ready, qe_done, r_ready, r_done, s_ready, max_done,
         exp_done, p_done, pt_ready, pt_done, av_ready, av_done, ho_ready, ho_done, out_ready, out_done) = used
        with nc.Fori(0, NH) as h:
            with nc.Block() as block:
                @block.sync
                def _(sp):
                    sp.dma_start(w_et[:], A["l2_w_et"][bass.ds(h, 1)].rearrange("o p i n -> (o p) i n")).then_inc(head_loaded, 16)
                    sp.dma_start(w_e[:], A["l2_w_e"][bass.ds(h, 1)].rearrange("o p i n -> (o p) i n")).then_inc(head_loaded, 16)
                    sp.dma_start(b_e[:], A["l2_b_e"][bass.ds(h, 1)].rearrange("o p i -> (o p) i")).then_inc(head_loaded, 16)
                    sp.wait_ge(head_loaded, 48)

                @block.tensor
                def _(pe):
                    pe.wait_ge(head_loaded, 48)
                    for n in range(FB * 2):
                        f, c = n // 2, n % 2
                        if n >= 2:
                            pe.wait_ge(qe_done, n - 1)
                        for i in range(KC):
                            mm = pe.matmul(k.PS[:, n % 2, :S2], w_et[:, i, f * P:(f + 1) * P],
                                           k.N[:, i, c * S2:(c + 1) * S2], start=(i == 0), stop=(i == KC - 1))
                        mm.then_inc(qe_ready, 1)
                    pe.wait_ge(qe_done, FB * 2)
                    for n in range(KC * 2):
                        o, c = n // 2, n % 2
                        for f in range(FB):
                            mm = pe.matmul(k.PS[:, 4 + n, :S2], w_e[:, f, o * P:(o + 1) * P],
                                           QE[:, f, c * S2:(c + 1) * S2], start=(f == 0), stop=(f == FB - 1))
                        mm.then_inc(r_ready, 1)
                    pe.wait_ge(r_done, KC * 2)
                    for t in range(ST + 1):
                        if t < ST:
                            if t >= 2:
                                pe.wait_ge(exp_done, t - 1)
                            for c in range(2):
                                for i in range(KC):
                                    mm = pe.matmul(k.PS[:, 2 * (t % 2) + c, :S2], R[:, i, t * P:(t + 1) * P],
                                                   k.N[:, i, S + c * S2:S + (c + 1) * S2],
                                                   start=(i == 0), stop=(i == KC - 1))
                            mm.then_inc(s_ready, 1)
                        if t >= 1:
                            v = t - 1
                            pe.wait_ge(p_done, v + 1)
                            for g in range(2):
                                if v >= 1:
                                    pe.wait_ge(pt_done, 2 * (v - 1) + g + 1)
                                for a in range(3):
                                    kt = 3 * g + a
                                    mm = pe.transpose(k.PS[:, 4 + g, a * P:(a + 1) * P], PR[:, v % 2, kt * P:(kt + 1) * P],
                                                      k.ident[:])
                                mm.then_inc(pt_ready, 1)
                    pe.wait_ge(pt_done, 2 * ST)
                    for n in range(KC * 2):
                        o, c = n // 2, n % 2
                        for kt in range(ST):
                            mm = pe.matmul(k.PS[:, n, :S2], XV[:, kt, o * P:(o + 1) * P],
                                           PT[:, kt, c * S2:(c + 1) * S2], start=(kt == 0), stop=(kt == ST - 1))
                        mm.then_inc(av_ready, 1)
                    pe.wait_ge(av_done, KC * 2)
                    for n in range(FB * 2):
                        f, c = n // 2, n % 2
                        if n >= 2:
                            pe.wait_ge(ho_done, n - 1)
                        for i in range(KC):
                            mm = pe.matmul(k.PS[:, 6 + n % 2, :S2], w_et[:, i, f * P:(f + 1) * P],
                                           R[:, i, c * S2:(c + 1) * S2], start=(i == 0), stop=(i == KC - 1))
                        mm.then_inc(ho_ready, 1)
                    pe.wait_ge(ho_done, FB * 2)
                    for n in range(KC * 2):
                        o, c = n // 2, n % 2
                        for f in range(FB):
                            mm = pe.matmul(k.PS[:, n, :S2], w_o[:, f, o * P:(o + 1) * P],
                                           QE[:, f, c * S2:(c + 1) * S2], start=(f == 0), stop=(f == FB - 1))
                        mm.then_inc(out_ready, 1)

                @block.scalar
                def _(act):
                    for n in range(FB * 2):
                        f, c = n // 2, n % 2
                        act.wait_ge(qe_ready, n + 1)
                        act.activation(QE[:, f, c * S2:(c + 1) * S2], k.PS[:, n % 2, :S2], ACT.Identity,
                                       bias=b_e[:, f:f + 1]).then_inc(qe_done, 1)
                    for t in range(ST):
                        act.wait_ge(max_done, t + 1)
                        act.activation(PR[:, t % 2, :].rearrange("p (c n) -> p c n", c=2),
                                       k.PS[:, 2 * (t % 2):2 * (t % 2) + 2, :S2], ACT.Exp, scale=C ** -0.5,
                                       bias=mx[:, t % 2, 1:2], accum_out=mx[:, t % 2, 2:3]).then_inc(exp_done, 1)
                        for g in range(2):
                            act.wait_ge(pt_ready, 2 * t + g + 1)
                            act.activation(PT[:, 3 * g:3 * g + 3, t * P:(t + 1) * P],
                                           k.PS[:, 4 + g, 0:3 * P].rearrange("p (a n) -> p a n", a=3), ACT.Copy)\
                               .then_inc(pt_done, 1)
                    for n in range(FB * 2):
                        f, c = n // 2, n % 2
                        act.wait_ge(ho_ready, n + 1)
                        act.activation(QE[:, f, c * S2:(c + 1) * S2], k.PS[:, 6 + n % 2, :S2], ACT.Identity,
                                       bias=b_e[:, f:f + 1]).then_inc(ho_done, 1)

                @block.vector
                def _(dve):
                    for n in range(KC * 2):
                        o, c = n // 2, n % 2
                        dve.wait_ge(r_ready, n + 1)
                        dve.tensor_copy(R[:, o, c * S2:(c + 1) * S2], k.PS[:, 4 + n, :S2]).then_inc(r_done, 1)
                    for t in range(ST):
                        m = mx[:, t % 2, :]
                        dve.wait_ge(s_ready, t + 1)
                        dve.tensor_reduce(m[:, 0:1], k.PS[:, 2 * (t % 2):2 * (t % 2) + 2, :S2], AX.XY, ALU.max)
                        dve.drain()
                        dve.tensor_scalar(m[:, 1:2], m[:, 0:1], -(C ** -0.5), None, ALU.mult).then_inc(max_done, 1)
                        dve.wait_ge(exp_done, t + 1)
                        dve.reciprocal(m[:, 3:4], m[:, 2:3])
                        dve.drain()
                        dve.tensor_scalar(PR[:, t % 2, :], PR[:, t % 2, :], m[:, 3:4], None, ALU.mult).then_inc(p_done, 1)
                    for n in range(KC * 2):
                        o, c = n // 2, n % 2
                        dve.wait_ge(av_ready, n + 1)
                        dve.tensor_copy(R[:, o, c * S2:(c + 1) * S2], k.PS[:, n, :S2]).then_inc(av_done, 1)
                    for n in range(KC * 2):
                        o, c = n // 2, n % 2
                        dve.wait_ge(out_ready, n + 1)
                        n_in = k.N[:, o, bass.ds(h * S + c * S2, S2)]
                        y = PR[:, 0, (n % 2) * S2:(n % 2 + 1) * S2]
                        dve.scalar_tensor_tensor(y, k.PS[:, n, :S2], b_o[:, o:o + 1], n_in, ALU.add, ALU.add)
                        dve.drain()
                        x = k.X[:, o, bass.ds(b * L + h * S + c * S2, S2)]
                        dve.tensor_tensor(x, x, y, ALU.add)
            fresh(nc, used)


E2 = 4
HE = E2 * E2
F2 = 2 * C
TM = M // P
EDGES = 1048576
EC = EDGES // P
EH = EC // 2
SHIFT_BITS = 13
ROW = E2 + HE
TOP2 = 2
WINDOW = 60.0
GC = 8
HC_ = 16
NU = 2
BW = 1024
BH = BW // NU
NBLK = EC // BW
HI = TM // 2
SLOPE = 0.2


def front(dve, V, D, D2, MV, width):
    cur, nxt = D, D2
    bits = width.bit_length() - 1
    for s in range(bits):
        w = width - (1 << s)
        dve.tensor_scalar(MV[:], cur[:], 1 << s, None, ALU.bitwise_and)
        dve.drain()
        if s < bits - 1:
            dve.scalar_tensor_tensor(nxt[:], MV[:], 0.0, cur[:], ALU.is_equal, ALU.mult)
            dve.drain()
            dve.copy_predicated(nxt[:, 0:w], MV[:, 1 << s:width], cur[:, 1 << s:width])
        dve.copy_predicated(V[:, 0:w], MV[:, 1 << s:width], V[:, 1 << s:width])
        dve.drain()
        cur, nxt = nxt, cur


class EdgeLists:

    def __init__(self, nc, ctx, k, edges, h):
        def sb(name, shape, dt=I32):
            return ctx.enter_context(nc.sbuf_tensor(k.name(name), shape, dt))

        self.k, self.edges, self.h = k, edges, h
        self.V, self.DSTS = sb("V", [P, EH]), sb("dsts", [P, EH])
        self.D, self.D2, self.MV = (sb(n, [P, EH], I16) for n in ("D", "D2", "MV"))
        self.used = sems(nc, ctx, "edges_in", "packed", "edges_out")
        self.edges_in, self.packed, self.edges_out = self.used

    def move(self, sp):
        for dst, w in ((self.V, 0), (self.DSTS, 1)):
            src = self.edges[w].rearrange("(p c) -> p c", p=P)[:, bass.ds(self.h * EH, EH)]
            sp.dma_start(dst[:], src).then_inc(self.edges_in, 16)
        sp.wait_ge(self.packed, 1)
        sp.dma_start(self.k.edges_dram[:, bass.ds(self.h * EH, EH)], self.V[:]).then_inc(self.edges_out, 16)
        sp.wait_ge(self.edges_out, 16)

    def pack(self, dve):
        V, DSTS, D, D2, MV = self.V, self.DSTS, self.D, self.D2, self.MV
        dve.wait_ge(self.edges_in, 32)
        dve.tensor_scalar(MV[:], DSTS[:], float(M), None, ALU.is_ge)
        dve.tensor_scalar(V[:], V[:], float(M - 1), None, ALU.min)
        dve.drain()
        dve.tensor_tensor_scan(D[:], MV[:], MV[:], 0.0, ALU.add, ALU.max)
        dve.tensor_scalar(DSTS[:], DSTS[:], SHIFT_BITS, None, ALU.arith_shift_left)
        dve.drain()
        dve.tensor_tensor(V[:], V[:], DSTS[:], ALU.bitwise_or)
        dve.tensor_scalar(self.k.cnt[:, bass.ds(self.h, 1)], D[:, EH - 1:EH], -1.0, float(EH), ALU.mult, ALU.add)
        dve.drain()
        dve.scalar_tensor_tensor(D[:], MV[:], 0.0, D[:], ALU.is_equal, ALU.mult)
        dve.drain()
        front(dve, V, D, D2, MV, EH)
        dve.sem_inc(self.packed, 1)


def split_block(nc, k, blk, held, g):
    with ExitStack() as ctx:
        def sb(name, shape, dt=I32):
            return ctx.enter_context(nc.sbuf_tensor(k.name(name), shape, dt))

        VB = sb("VB", [P, BW])
        S_, T_, X_ = (sb(n, [P, BW]) for n in ("S_", "T_", "X_"))
        LIVE, LAST, LOF, HIF, CH_ = (sb(n, [P, BW], F32) for n in ("LIVE", "LAST", "LOF", "HIFb", "CHb"))
        LOB, HIB = (sb(n, [P, BW], BF16) for n in ("LOB", "HIB"))
        OLB = sb("OLB", [P, NU, HC_, P], BF16)
        OHB = sb("OHB", [P, NU, HC_, TM], BF16)
        D, D2, MV = (sb(n, [P, BW], I16) for n in ("Db", "D2b", "MVb"))
        IDX = sb("IDX", [P, 2, BW])
        DIG = sb("DIG", [P, 2, BW], F32)
        lim = sb("lim", [P, 3], F32)
        used = sems(nc, ctx, "block_in", "hot_done", "hot_used", "count_done", "count_row", "lists_done", "lists_out")
        block_in, hot_done, hot_used, count_done, count_row, lists_done, lists_out = used

        def digits(dve, V, lo, hi):
            dve.tensor_scalar(T_[:], V[:], SHIFT_BITS, None, ALU.arith_shift_right)
            dve.drain()
            dve.tensor_scalar(X_[:], T_[:], P - 1, None, ALU.bitwise_and)
            dve.drain()
            dve.tensor_copy(lo, X_[:])
            dve.drain()
            dve.tensor_scalar(X_[:], T_[:], 7, None, ALU.arith_shift_right)
            dve.drain()
            dve.tensor_copy(hi, X_[:])
            dve.drain()

        with nc.Block() as block:
            @block.sync
            def _(sp):
                with sp.If(held > 0):
                    for h in range(NU):
                        sp.dma_start(VB[:, h * BH:(h + 1) * BH], k.edges_dram[:, bass.ds(blk * BH + h * EH, BH)])\
                          .then_inc(block_in, 16)
                    sp.wait_ge(lists_done, 1)
                    for w in range(2):
                        sp.dma_start(k.idx_dram[w][:, bass.ds(blk * BW, BW)], IDX[:, w, :]).then_inc(lists_out, 16)
                        sp.dma_start(k.dig_dram[w][:, bass.ds(blk * BW, BW)], DIG[:, w, :]).then_inc(lists_out, 16)
                    sp.wait_ge(lists_out, 64)

            @block.vector
            def _(dve):
                with dve.If(held > 0):
                    dve.wait_ge(block_in, 16 * NU)
                    dve.tensor_copy(lim[:, 0:NU], g.left[:])
                    dve.tensor_scalar(S_[:], VB[:], (1 << SHIFT_BITS) - 1, None, ALU.bitwise_and)
                    dve.drain()
                    for h in range(NU):
                        dve.tensor_scalar(LIVE[:, h * BH:(h + 1) * BH], g.iota_b[:, 0:BH], lim[:, h:h + 1], None, ALU.is_lt)
                    dve.tensor_scalar(g.left[:], g.left[:], -float(BH), None, ALU.add)
                    dve.tensor_copy(CH_[:], S_[:])
                    dve.drain()
                    dve.scalar_tensor_tensor(LAST[:], CH_[:], float(M - 1), LIVE[:], ALU.is_equal, ALU.mult)
                    dve.drain()
                    dve.tensor_tensor(LIVE[:], LIVE[:], LAST[:], ALU.subtract)
                    digits(dve, VB, LOF[:], HIF[:])
                    dve.scalar_tensor_tensor(HIF[:], HIF[:], 1.0, LAST[:], ALU.add, ALU.mult)
                    dve.tensor_copy(LOB[:], LOF[:])
                    dve.drain()
                    dve.tensor_scalar(HIB[:], HIF[:], -1.0, None, ALU.add)
                    dve.drain()
                    with dve.Fori(0, BH // HC_) as i:
                        with dve.If(held > i * HC_):
                            for u in range(NU):
                                at = bass.ds(i * HC_ + u * BH, HC_)
                                dve.wait_ge(hot_used, i * NU + u + 1)
                                dve.tensor_tensor(OLB[:, u, :, :], g.iota_h[:].rearrange("p (o n) -> p o n", o=1)
                                                  .broadcast_to([P, HC_, P]),
                                                  LOB[:, at].rearrange("p (c o) -> p c o", o=1).broadcast_to([P, HC_, P]),
                                                  ALU.is_equal)
                                dve.tensor_tensor(OHB[:, u, :, :], g.iota_h[:, 0:TM].rearrange("p (o n) -> p o n", o=1)
                                                  .broadcast_to([P, HC_, TM]),
                                                  HIB[:, at].rearrange("p (c o) -> p c o", o=1).broadcast_to([P, HC_, TM]),
                                                  ALU.is_equal).then_inc(hot_done, 1)
                    dve.tensor_scalar(MV[:], LIVE[:], -1.0, 1.0, ALU.mult, ALU.add)
                    dve.drain()
                    dve.tensor_tensor_scan(D[:], MV[:], MV[:], 0.0, ALU.add, ALU.max)
                    dve.drain()
                    dve.tensor_scalar(lim[:, NU:NU + 1], D[:, BW - 1:BW], -1.0, float(BW), ALU.mult, ALU.add).then_inc(count_done, 1)
                    dve.scalar_tensor_tensor(D2[:], MV[:], 0.0, D[:], ALU.is_equal, ALU.mult)
                    dve.drain()
                    front(dve, VB, D2, D, MV, BW)
                    dve.tensor_scalar(IDX[:, 0, :], VB[:], (1 << SHIFT_BITS) - 1, None, ALU.bitwise_and)
                    dve.tensor_scalar(IDX[:, 1, :], VB[:], SHIFT_BITS, None, ALU.arith_shift_right)
                    dve.tensor_scalar(LIVE[:], g.iota_b[:], lim[:, NU:NU + 1], None, ALU.is_lt)
                    digits(dve, VB, DIG[:, 0, :], HIF[:])
                    dve.tensor_scalar(IDX[:, 1, :], IDX[:, 1, :], float(M - 1), None, ALU.min)
                    dve.scalar_tensor_tensor(HIF[:], HIF[:], 1.0, LIVE[:], ALU.add, ALU.mult)
                    dve.drain()
                    dve.tensor_scalar(DIG[:, 1, :], HIF[:], -1.0, None, ALU.add)
                    dve.wait_ge(count_row, 1)
                    dve.tensor_reduce(g.most[:, 0:1], k.PS[0:1, 1, 0:P], AX.X, ALU.max)
                    dve.drain()
                    dve.tensor_copy(g.most_b[:, bass.ds(blk, 1)], g.most[:])
                    dve.tensor_tensor(g.HIST[:], g.HIST[:], k.PS[:, 0, 0:TM], ALU.add).then_inc(lists_done, 1)

            @block.tensor
            def _(pe):
                with pe.If(held > 0):
                    pe.sem_inc(hot_used, NU)
                    pe.matmul(k.PS[:, 0, 0:TM], k.zeros[:, 0:P], k.zeros[:, 0:TM], start=True, stop=False)
                    with pe.Fori(0, BH // HC_) as i:
                        with pe.If(held > i * HC_):
                            for u in range(NU):
                                pe.wait_ge(hot_done, i * NU + u + 1)
                                for c in range(HC_):
                                    mm = pe.matmul(k.PS[:, 0, 0:TM], OLB[:, u, c, :], OHB[:, u, c, :], start=False, stop=False)
                                mm.then_inc(hot_used, 1)
                    pe.matmul(k.PS[:, 0, 0:TM], k.zeros[:, 0:P], k.zeros[:, 0:TM], start=False, stop=True)
                    pe.wait_ge(count_done, 1)
                    pe.matmul(k.PS[0:1, 1, 0:P], lim[:, NU:NU + 1], k.ident[:], start=True, stop=True).then_inc(count_row, 1)
        fresh(nc, used)


def split_edges(nc, k, A, g):
    with ExitStack() as own:
        g.iota_b = own.enter_context(nc.sbuf_tensor("iota_b", [P, BW], F32))
        g.iota_h = own.enter_context(nc.sbuf_tensor("iota_h", [P, P], BF16))
        g.left = own.enter_context(nc.sbuf_tensor("left", [P, NU], F32))
        g.ahead = own.enter_context(nc.sbuf_tensor("ahead", [1, NBLK], F32))
        used = sems(nc, own, "iota_in", "cnt_row")
        iota_in, cnt_row = used
        with nc.Block() as block:
            @block.sync
            def _(sp):
                sp.dma_start(g.iota_b[:], A["c_iota"].broadcast_to([P, BW])).then_inc(iota_in, 16)

            @block.tensor
            def _(pe):
                for h in range(NU):
                    mm = pe.matmul(k.PS[0:1, 0, h * P:(h + 1) * P], k.cnt[:, h:h + 1], k.ident[:], start=True, stop=True)
                mm.then_inc(cnt_row, 1)

            @block.vector
            def _(dve):
                dve.memset(g.HIST[:], 0.0)
                dve.tensor_copy(g.left[:], k.cnt[:])
                dve.wait_ge(cnt_row, 1)
                dve.tensor_reduce(g.most[:], k.PS[0:1, 0, 0:NU * P], AX.X, ALU.max)
                dve.wait_ge(iota_in, 16)
                dve.drain()
                dve.tensor_copy(g.iota_h[:], g.iota_b[:, 0:P])
                dve.tensor_scalar(g.ahead[:], g.iota_b[0:1, 0:NBLK], -float(BH), g.most[:], ALU.mult, ALU.add)
                dve.drain()
                dve.tensor_scalar(g.ahead[:], g.ahead[:], 0.0, float(BH), ALU.max, ALU.min)
                dve.drain()
                dve.tensor_copy(g.most_b[:], g.ahead[:])
        fresh(nc, used)
        with nc.Fori(0, NBLK) as blk:
            held = nc.values_load(g.most_b[0:1, bass.ds(blk, 1)], min_val=0, max_val=BH)
            split_block(nc, k, blk, held, g)


def graph_features(nc, k, A, b, g):
    norm_image(nc, k, b, k.eps5)
    with ExitStack() as ctx:
        tmp = ctx.enter_context(nc.sbuf_tensor(k.name("tmp_h"), [P, 2, LT, HE], F32))
        used = sems(nc, ctx, "h_ready")
        with nc.Block() as block:
            @block.tensor
            def _(pe):
                for t in range(LT):
                    for i in range(KC):
                        mm = pe.matmul(k.PS[:, 0, t * HE:(t + 1) * HE], k.N[:, i, t * P:(t + 1) * P], g.w_gat[:, i, :],
                                       start=(i == 0), stop=(i == KC - 1))
                mm.then_inc(used[0], 1)

            @block.vector
            def _(dve):
                dve.wait_ge(used[0], 1)
                h = k.PS[:, 0, 0:LT * HE].rearrange("p (t f) -> p t f", f=HE)
                dve.tensor_copy(g.GS[:, bass.ds(b * LT, LT), E2:ROW], h)
                for w in range(2):
                    att = g.att[:, w, :].rearrange("p (o f) -> p o f", o=1).broadcast_to([P, LT, HE])
                    dve.tensor_tensor(tmp[:, w, :, :], h, att, ALU.mult)
                dve.drain()
                for w in range(2):
                    dst = (g.GS if w == 0 else g.GD)[:, bass.ds(b * LT, LT), 0:E2]
                    dve.tensor_reduce(dst, tmp[:, w, :, :].rearrange("p t (h e) -> p t h e", e=E2), AX.X, ALU.add)
        fresh(nc, used)


def graph_mixture(nc, k, A):
    with ExitStack() as top:
        g = Core()

        def keep(name, shape, dt=F32):
            return top.enter_context(nc.sbuf_tensor(k.name(name), shape, dt))

        g.most = keep("most", [1, 1])
        g.most_b = keep("most_b", [1, NBLK], I32)
        g.HIST = keep("HIST", [P, TM])
        split_edges(nc, k, A, g)
        with ExitStack() as own:
            def sbo(name, shape, dt=F32):
                return own.enter_context(nc.sbuf_tensor(k.name(name), shape, dt))

            g.GS = sbo("GS", [P, TM, ROW])
            g.GD = sbo("GD", [P, TM, 2 * E2])
            g.w_gat = sbo("w_gat", [P, KC, HE])
            g.att = sbo("att", [P, 2, HE])
            g.rows = sbo("g_rows", [P, 3, HE])
            g.iota = sbo("g_iota", [P, P])
            g.SELF = sbo("SELF", [P, TM, E2])
            used = sems(nc, own, "g_loaded")
            with nc.Block() as block:
                @block.sync
                def _(sp):
                    sp.dma_start(g.w_gat[:], A["l2_w_gat"]).then_inc(used[0], 16)
                    sp.dma_start(g.att[:], A["l2_att"].broadcast_to([P, 2, HE])).then_inc(used[0], 16)
                    sp.dma_start(g.rows[:], A["l2_g_rows"].broadcast_to([P, 3, HE])).then_inc(used[0], 16)
                    sp.dma_start(g.iota[:], A["c_iota"][:, 0:P].broadcast_to([P, P])).then_inc(used[0], 16)
                    sp.wait_ge(used[0], 64)
            fresh(nc, used)
            with nc.Fori(0, NB) as b:
                graph_features(nc, k, A, b, g)
            graph_tables(nc, k, g)
            edge_sums(nc, k, g)
            gates(nc, k, g)
        with nc.Fori(0, NB) as b:
            gated_experts(nc, k, A, b)


def graph_tables(nc, k, g):
    with ExitStack() as ctx:
        def sb(name, shape, dt=F32):
            return ctx.enter_context(nc.sbuf_tensor(k.name(name), shape, dt))

        pm = sb("pm", [P, 2, E2])
        U = sb("U", [P, TM, E2])
        used = sems(nc, ctx, "part_max", "all_max", "table_done", "self_done", "tables_out")
        part_max, all_max, table_done, self_done, tables_out = used

        def leaky(dve, x):
            dve.scalar_tensor_tensor(x, x, SLOPE, x, ALU.mult, ALU.max)

        with nc.Block() as block:
            @block.vector
            def _(dve):
                dve.tensor_reduce(pm[:, 0, :], g.GS[:, :, 0:E2].rearrange("p t h -> p h t"), AX.X, ALU.max)\
                   .then_inc(part_max, 1)
                dve.tensor_tensor(g.SELF[:], g.GS[:, :, 0:E2], g.GD[:, :, 0:E2], ALU.add)
                dve.drain()
                leaky(dve, g.SELF[:])
                dve.wait_ge(all_max, 1)
                dve.tensor_tensor(U[:], g.GD[:, :, 0:E2],
                                  pm[:, 1, :].rearrange("p (o h) -> p o h", o=1).broadcast_to([P, TM, E2]), ALU.add)
                dve.drain()
                leaky(dve, U[:])
                dve.drain()
                dve.scalar_tensor_tensor(U[:], U[:], -WINDOW, g.SELF[:], ALU.add, ALU.max)
                dve.drain()
                dve.tensor_scalar(g.GD[:, :, E2:2 * E2], U[:], -1.0, None, ALU.mult)
                dve.tensor_tensor(g.SELF[:], g.SELF[:], U[:], ALU.subtract).then_inc(table_done, 1)

            @block.gpsimd
            def _(pool):
                pool.wait_ge(part_max, 1)
                pool.partition_all_reduce(pm[:, 1, :], pm[:, 0, :], P, bass.bass_isa.ReduceOp.max).then_inc(all_max, 1)

            @block.scalar
            def _(act):
                act.wait_ge(table_done, 1)
                act.activation(g.SELF[:], g.SELF[:], ACT.Exp).then_inc(self_done, 1)

            @block.sync
            def _(sp):
                sp.wait_ge(table_done, 1)
                sp.dma_start(k.src_dram.rearrange("(t p) f -> p t f", p=P), g.GS[:]).then_inc(tables_out, 16)
                sp.dma_start(k.dst_dram.rearrange("(t p) f -> p t f", p=P), g.GD[:]).then_inc(tables_out, 16)
                sp.wait_ge(tables_out, 32)
        fresh(nc, used)


def edge_sums(nc, k, g):
    def zeroes(start):
        with nc.Block() as block:
            @block.tensor
            def _(pe):
                for n in range(2):
                    pe.matmul(k.PS[:, 4 + n, 0:HI * ROW], k.zeros[:, 0:P], k.zeros[:, 0:HI * ROW], start=start, stop=not start)

    zeroes(True)
    with nc.Fori(0, NBLK) as blk:
        longest = nc.values_load(g.most_b[0:1, bass.ds(blk, 1)], min_val=0, max_val=BW)
        with nc.If(longest > 0):
            block_sums(nc, k, g, blk, longest)
    zeroes(False)


def block_sums(nc, k, g, blk, longest):
    with ExitStack() as ctx:
        def sb(name, shape, dt=F32):
            return ctx.enter_context(nc.sbuf_tensor(k.name(name), shape, dt))

        IX = sb("IX", [P, NU, 2, GC], I32)
        DG = sb("DG", [P, NU, 2, GC])
        RS = sb("RS", [P, NU, GC * ROW])
        RD = sb("RD", [P, NU, GC * 2 * E2])
        W = sb("Wt", [P, NU, GC, E2])
        VL = sb("VL", [P, NU, GC, ROW])
        OL = sb("OL", [P, NU, GC, P])
        OH = sb("OHI", [P, NU, GC, TM])
        R = sb("Rr", [P, NU, GC, TM, ROW])
        used = sems(nc, ctx, "ix_in0", "ix_in1", "dg_in0", "dg_in1", "e_sum", "e_exp", "r_done", "added")
        ix_in0, ix_in1, dg_in0, dg_in1, e_sum, e_exp, r_done, added = used
        ix_in, dg_in = (ix_in0, ix_in1), (dg_in0, dg_in1)
        STEP = NU * GC
        rs_in, rd_in = k.rs_in, k.rd_in

        def hot(ap, n):
            return ap.rearrange("p (c o) -> p c o", o=1).broadcast_to([P, GC, n])

        with nc.Block() as block:
            @block.sync
            def _(sp):
                with sp.Fori(0, BW // STEP) as i:
                    with sp.If(longest > i * STEP):
                        for u in range(NU):
                            sp.wait_ge(r_done, i * NU + u + 1)
                            sp.sem_inc(k.turns, 1)
                            for w in range(2):
                                at = bass.ds(blk * BW + i * STEP + u * GC, GC)
                                sp.dma_start(IX[:, u, w, :], k.idx_dram[w][:, at]).then_inc(ix_in[u], 16)
                                sp.dma_start(DG[:, u, w, :], k.dig_dram[w][:, at]).then_inc(dg_in[u], 16)

            @block.gpsimd
            def _(pool):
                with pool.Fori(0, BW // STEP) as i:
                    with pool.If(longest > i * STEP):
                        for u in range(NU):
                            pool.wait_ge(ix_in[u], i * 32 + 32)
                            pool.sem_inc(k.turns, 1)
                            for c in range(GC):
                                pool.indirect_dma_start(
                                    out=RS[:, u, c * ROW:(c + 1) * ROW], out_offset=None, in_=k.src_dram,
                                    in_offset=bass.IndirectOffsetOnAxis(ap=IX[:, u, 0, c:c + 1], axis=0),
                                    bounds_check=M - 1, oob_is_err=False).then_inc(rs_in[u], 16)
                                pool.indirect_dma_start(
                                    out=RD[:, u, c * 2 * E2:(c + 1) * 2 * E2], out_offset=None, in_=k.dst_dram,
                                    in_offset=bass.IndirectOffsetOnAxis(ap=IX[:, u, 1, c:c + 1], axis=0),
                                    bounds_check=M - 1, oob_is_err=False).then_inc(rd_in[u], 16)

            def weigh(dve, i, u):
                rs = RS[:, u, :].rearrange("p (c f) -> p c f", f=ROW)
                rd = RD[:, u, :].rearrange("p (c f) -> p c f", f=2 * E2)
                w = W[:, u, :, :]
                dve.wait_ge(dg_in[u], i * 32 + 32)
                dve.wait_ge(added, i * NU + u + 1)
                dve.tensor_tensor(OL[:, u, :, :], g.iota[:].rearrange("p (o n) -> p o n", o=1).broadcast_to([P, GC, P]),
                                  hot(DG[:, u, 0, :], P), ALU.is_equal)
                dve.tensor_tensor(OH[:, u, :, :], g.iota[:, 0:TM].rearrange("p (o n) -> p o n", o=1)
                                  .broadcast_to([P, GC, TM]), hot(DG[:, u, 1, :], TM), ALU.is_equal)
                dve.wait_ge(rs_in[u], i * (16 * GC) + 16 * GC)
                dve.wait_ge(rd_in[u], i * (16 * GC) + 16 * GC)
                dve.tensor_tensor(w, rs[:, :, 0:E2], rd[:, :, 0:E2], ALU.add)
                dve.drain()
                dve.scalar_tensor_tensor(w, w, SLOPE, w, ALU.mult, ALU.max)
                dve.drain()
                dve.tensor_tensor(w, w, rd[:, :, E2:2 * E2], ALU.add).then_inc(e_sum, 1)
                dve.wait_ge(e_exp, i * NU + u + 1)
                vl = VL[:, u, :, :]
                dve.tensor_copy(vl[:, :, 0:E2], w)
                for c in range(GC):
                    dve.tensor_tensor(vl[:, c, E2:ROW].rearrange("p (h e) -> p h e", e=E2),
                                      rs[:, c, E2:ROW].rearrange("p (h e) -> p h e", e=E2),
                                      w[:, c, :].rearrange("p (h o) -> p h o", o=1).broadcast_to([P, E2, E2]), ALU.mult)
                dve.drain()
                for c in range(GC):
                    op = dve.tensor_tensor(R[:, u, c, :, :],
                                           OH[:, u, c, :].rearrange("p (t o) -> p t o", o=1).broadcast_to([P, TM, ROW]),
                                           vl[:, c, :].rearrange("p (o f) -> p o f", o=1).broadcast_to([P, TM, ROW]),
                                           ALU.mult)
                op.then_inc(r_done, 1)

            @block.vector
            def _(dve):
                dve.sem_inc(r_done, NU)
                with dve.Fori(0, BW // STEP) as i:
                    with dve.If(longest > i * STEP):
                        for u in range(NU):
                            weigh(dve, i, u)

            @block.scalar
            def _(act):
                with act.Fori(0, BW // STEP) as i:
                    with act.If(longest > i * STEP):
                        for u in range(NU):
                            act.wait_ge(e_sum, i * NU + u + 1)
                            act.activation(W[:, u, :, :], W[:, u, :, :], ACT.Exp).then_inc(e_exp, 1)

            @block.tensor
            def _(pe):
                pe.sem_inc(added, NU)
                with pe.Fori(0, BW // STEP) as i:
                    with pe.If(longest > i * STEP):
                        for u in range(NU):
                            pe.wait_ge(r_done, i * NU + u + 1 + NU)
                            for c in range(GC):
                                for n in range(2):
                                    mm = pe.matmul(k.PS[:, 4 + n, 0:HI * ROW], OL[:, u, c, :],
                                                   R[:, u, c, n * HI:(n + 1) * HI, :].rearrange("p t f -> p (t f)"),
                                                   start=False, stop=False)
                            mm.then_inc(added, 1)
        fresh(nc, used)
        with nc.Block() as block:
            @block.gpsimd
            def _(pool):
                for s in k.rs_in + k.rd_in:
                    pool.dma_reset(range(s.num, s.num + 1))
                    pool.sem_clear(s)


def gates(nc, k, g):
    with ExitStack() as ctx:
        def sb(name, shape, dt=F32):
            return ctx.enter_context(nc.sbuf_tensor(k.name(name), shape, dt))

        AG = sb("AG", [P, TM, ROW])
        Y = sb("Yg", [P, TM, HE])
        SQ = sb("SQg", [P, TM, HE])
        st = sb("stg", [P, 4, TM])
        SC = sb("SCg", [P, TM, E2])
        RK = sb("RKg", [P, TM, E2])
        GE = sb("GEg", [P, E2, TM])
        GR = sb("GRg", [2 * TM, 2, P])
        LR = sb("LRg", [P, ROW])
        LW = sb("LWg", [P, TM, E2])
        used = sems(nc, ctx, "lr_in", "lw_sum", "lw_exp", "g_var", "g_root", "g_diff", "g_exp", "ge_done", "gt_ready", "gt_done", "gates_out")
        lr_in, lw_sum, lw_exp, g_var, g_root, g_diff, g_exp, ge_done, gt_ready, gt_done, gates_out = used

        def over(ap, n):
            return ap.rearrange("p (t o) -> p t o", o=1).broadcast_to([P, TM, n])

        def row(i):
            return g.rows[:, i, :].rearrange("p (o f) -> p o f", o=1).broadcast_to([P, TM, HE])

        with nc.Block() as block:
            @block.vector
            def _(dve):
                for n in range(2):
                    dve.tensor_copy(AG[:, n * HI:(n + 1) * HI, :],
                                    k.PS[:, 4 + n, 0:HI * ROW].rearrange("p (t f) -> p t f", f=ROW))
                for h in range(E2):
                    dve.tensor_tensor(Y[:, :, h * E2:(h + 1) * E2], g.GS[:, :, E2 + h * E2:E2 + (h + 1) * E2],
                                      g.SELF[:, :, h:h + 1].broadcast_to([P, TM, E2]), ALU.mult)
                dve.drain()
                dve.tensor_tensor(AG[:, :, 0:E2], AG[:, :, 0:E2], g.SELF[:], ALU.add)
                dve.tensor_tensor(AG[:, :, E2:ROW], AG[:, :, E2:ROW], Y[:], ALU.add)
                dve.wait_ge(lr_in, 16)
                dve.tensor_tensor(LW[:], g.GD[:, :, 0:E2], LR[:, 0:E2].rearrange("p (o h) -> p o h", o=1)
                                  .broadcast_to([P, TM, E2]), ALU.add)
                dve.drain()
                dve.scalar_tensor_tensor(LW[:], LW[:], SLOPE, LW[:], ALU.mult, ALU.max)
                dve.drain()
                dve.tensor_tensor(LW[:], LW[:], g.GD[:, :, E2:2 * E2], ALU.add).then_inc(lw_sum, 1)
                dve.wait_ge(lw_exp, 1)
                dve.tensor_tensor(LW[:], LW[:], over(g.HIST[:], E2), ALU.mult)
                dve.drain()
                dve.tensor_tensor(AG[:, :, 0:E2], AG[:, :, 0:E2], LW[:], ALU.add)
                for h in range(E2):
                    for e in range(E2):
                        f = E2 + h * E2 + e
                        dve.scalar_tensor_tensor(AG[:, :, f], LW[:, :, h], LR[:, f:f + 1], AG[:, :, f], ALU.mult, ALU.add)
                dve.drain()
                dve.reciprocal(AG[:, :, 0:E2], AG[:, :, 0:E2])
                dve.drain()
                for h in range(E2):
                    dve.tensor_tensor(Y[:, :, h * E2:(h + 1) * E2], AG[:, :, E2 + h * E2:E2 + (h + 1) * E2],
                                      AG[:, :, h:h + 1].broadcast_to([P, TM, E2]), ALU.mult)
                dve.drain()
                dve.tensor_tensor(Y[:], Y[:], row(0), ALU.add)
                dve.drain()
                mean, var, diff, first = (st[:, i, :] for i in range(4))
                dve.tensor_reduce(mean, Y[:], AX.X, ALU.add)
                dve.drain()
                dve.tensor_scalar(mean, mean, 1.0 / HE, None, ALU.mult)
                dve.drain()
                dve.tensor_tensor(Y[:], Y[:], over(mean, HE), ALU.subtract)
                dve.drain()
                dve.tensor_tensor(SQ[:], Y[:], Y[:], ALU.mult)
                dve.drain()
                dve.tensor_reduce(var, SQ[:], AX.X, ALU.add)
                dve.drain()
                dve.tensor_scalar(var, var, 1.0 / HE, None, ALU.mult).then_inc(g_var, 1)
                dve.wait_ge(g_root, 1)
                dve.reciprocal(var, var)
                dve.drain()
                dve.tensor_tensor(Y[:], Y[:], over(var, HE), ALU.mult)
                dve.drain()
                dve.tensor_tensor(Y[:], Y[:], row(1), ALU.mult)
                dve.drain()
                dve.tensor_tensor(Y[:], Y[:], row(2), ALU.add)
                dve.drain()
                dve.tensor_reduce(SC[:], Y[:].rearrange("p t (h e) -> p t e h", e=E2), AX.X, ALU.add)
                dve.drain()
                dve.tensor_scalar(SC[:], SC[:], 1.0 / E2, None, ALU.mult)
                dve.memset(RK[:], 0.0)
                dve.drain()
                for e in range(E2):
                    for o in range(E2):
                        if o != e:
                            dve.tensor_tensor(diff, SC[:, :, o], SC[:, :, e], ALU.is_ge if o < e else ALU.is_gt)
                            dve.drain()
                            dve.tensor_tensor(RK[:, :, e], RK[:, :, e], diff, ALU.add)
                            dve.drain()
                dve.tensor_reduce(first, SC[:], AX.X, ALU.max)
                dve.tensor_scalar(SQ[:, :, 0:E2], RK[:], 1.0, None, ALU.is_equal)
                dve.tensor_scalar(SQ[:, :, E2:2 * E2], RK[:], 0.0, None, ALU.is_equal)
                dve.drain()
                dve.tensor_tensor(SC[:], SC[:], SQ[:, :, 0:E2], ALU.mult)
                dve.drain()
                dve.tensor_reduce(diff, SC[:], AX.X, ALU.add)
                dve.drain()
                dve.tensor_tensor(diff, diff, first, ALU.subtract).then_inc(g_diff, 1)
                dve.wait_ge(g_exp, 1)
                dve.tensor_scalar(first, diff, 1.0, None, ALU.add)
                dve.drain()
                dve.reciprocal(first, first)
                dve.tensor_tensor(SC[:], SQ[:, :, 0:E2], over(diff, E2), ALU.mult)
                dve.drain()
                dve.tensor_tensor(SC[:], SC[:], SQ[:, :, E2:2 * E2], ALU.add)
                dve.drain()
                dve.tensor_tensor(GE[:].rearrange("p e t -> p t e"), SC[:], over(first, E2), ALU.mult)\
                   .then_inc(ge_done, 1)
                dve.wait_ge(gt_ready, 1)
                dve.tensor_copy(GR[:], k.PS[0:2 * TM, 0:2, 0:P]).then_inc(gt_done, 1)

            @block.scalar
            def _(act):
                act.wait_ge(lw_sum, 1)
                act.activation(LW[:], LW[:], ACT.Exp).then_inc(lw_exp, 1)
                act.wait_ge(g_var, 1)
                act.activation(st[:, 1, :], st[:, 1, :], ACT.Sqrt, bias=k.eps5[:]).then_inc(g_root, 1)
                act.wait_ge(g_diff, 1)
                act.activation(st[:, 2, :], st[:, 2, :], ACT.Exp).then_inc(g_exp, 1)

            @block.tensor
            def _(pe):
                pe.wait_ge(ge_done, 1)
                for n in range(2):
                    mm = pe.transpose(k.PS[0:2 * TM, n, 0:P], GE[:, 2 * n:2 * n + 2, :].rearrange("p e t -> p (e t)"),
                                      k.ident[:])
                mm.then_inc(gt_ready, 1)

            @block.sync
            def _(sp):
                sp.dma_start(LR[:], k.src_dram[M - 1:M, :].broadcast_to([P, ROW])).then_inc(lr_in, 16)
                sp.wait_ge(lr_in, 16)
                sp.wait_ge(gt_done, 1)
                for n in range(2):
                    sp.dma_start(k.gate_dram[n * 2 * TM:(n + 1) * 2 * TM, :], GR[:, n, :]).then_inc(gates_out, 16)
                sp.wait_ge(gates_out, 32)
        fresh(nc, used)


def gated_experts(nc, k, A, b):
    norm_image(nc, k, b, k.eps5)
    with ExitStack() as ctx:
        def sb(name, shape, dt=F32):
            return ctx.enter_context(nc.sbuf_tensor(k.name(name), shape, dt))

        w1 = sb("w1g", [P, KC, E2 * F2])
        w2 = sb("w2g", [P, NM, C])
        b1 = sb("b1g", [P, NM])
        b2 = sb("b2g", [E2, C])
        GB = sb("GB", [P, E2, L])
        G4 = sb("G4", [E2, L])
        used = sems(nc, ctx, "x_loaded")
        with nc.Block() as block:
            @block.sync
            def _(sp):
                for dst, name in ((w1, "l2_w1"), (w2, "l2_w2"), (b1, "l2_b1"), (b2, "l2_b2")):
                    sp.dma_start(dst[:], A[name]).then_inc(used[0], 16)
                rows = k.gate_dram.rearrange("(e t) p -> e (t p)", e=E2)[:, bass.ds(b * L, L)]
                sp.dma_start(G4[:], rows).then_inc(used[0], 16)
                for e in range(E2):
                    sp.dma_start(GB[:, e, :], rows[e:e + 1, :].broadcast_to([P, L])).then_inc(used[0], 16)
                sp.wait_ge(used[0], 16 * (5 + E2))
        fresh(nc, used)

        def bias(pe, c):
            for o in range(KC):
                pe.matmul(k.PS[:, 4 + o, :T], b2[:, o * P:(o + 1) * P], G4[:, bass.ds(c * T, T)], start=True, stop=False)

        def add(dve, c):
            x = k.X[:, :, bass.ds(b * L + c * T, T)]
            return dve.tensor_tensor(x, x, k.PS[:, 4:4 + KC, :T], ALU.add)

        two_layer(nc, ctx, k, b, k.N, lambda i, m: w1[:, i, m * P:(m + 1) * P], lambda m: b1[:, m:m + 1],
                  lambda m, o: w2[:, m, o * P:(o + 1) * P],
                  gate=lambda m, c: GB[:, m // E2, bass.ds(c * T, T)], first=bias, last=add)




def transposed_image(nc, k, dst):
    with ExitStack() as own:
        used = sems(nc, own, "t_ready", "t_done")
        t_ready, t_done = used
        with nc.Block() as block:
            @block.tensor
            def _(pe):
                for t in range(LT):
                    if t >= 4:
                        pe.wait_ge(t_done, t - 3)
                    for i in range(KC):
                        mm = pe.transpose(k.PS[:, t % 4, i * P:(i + 1) * P], k.N[:, i, t * P:(t + 1) * P], k.ident[:])
                    mm.then_inc(t_ready, 1)

            @block.vector
            def _(dve):
                for t in range(LT):
                    dve.wait_ge(t_ready, t + 1)
                    dve.tensor_copy(dst[:, t, :], k.PS[:, t % 4, 0:C]).then_inc(t_done, 1)
        fresh(nc, used)


def sigmoid_attention(nc, k, A, b):
    norm_image(nc, k, b, k.eps5)
    with ExitStack() as ctx:
        def sb(name, shape, dt=F32):
            return ctx.enter_context(nc.sbuf_tensor(k.name(name), shape, dt))

        w_q = sb("w_q", [P, KC, C])
        QT = sb("QT3", [P, KC, L])
        XT = sb("XT3", [P, LT, C])
        NA = 3
        AT = sb("AT", [P, NA, T])
        transposed_image(nc, k, XT)
        used = sems(nc, ctx, "l3_loaded", "q3_ready", "q3_done")
        l3_loaded, q3_ready, q3_done = used
        with nc.Block() as block:
            @block.sync
            def _(sp):
                sp.dma_start(w_q[:], A["l3_w_q"]).then_inc(l3_loaded, 16)
                sp.wait_ge(l3_loaded, 16)

            @block.tensor
            def _(pe):
                pe.wait_ge(l3_loaded, 16)
                for n in range(KC * NT):
                    m, c = n // NT, n % NT
                    if n >= 4:
                        pe.wait_ge(q3_done, n - 3)
                    for i in range(KC):
                        mm = pe.matmul(k.PS[:, n % 4, :T], w_q[:, i, m * P:(m + 1) * P], k.N[:, i, c * T:(c + 1) * T],
                                       start=(i == 0), stop=(i == KC - 1))
                    mm.then_inc(q3_ready, 1)

            @block.scalar
            def _(act):
                for n in range(KC * NT):
                    m, c = n // NT, n % NT
                    act.wait_ge(q3_ready, n + 1)
                    act.activation(QT[:, m, c * T:(c + 1) * T], k.PS[:, n % 4, :T], ACT.Copy).then_inc(q3_done, 1)
        fresh(nc, used)

        used = sems(nc, ctx, "sc_ready", "att_done", "att_used", "val_ready", "val_used")
        sc_ready, att_done, att_used, val_ready, val_used = used
        with nc.Block() as block:
            @block.tensor
            def _(pe):
                pe.sem_inc(att_used, NA)
                with pe.Fori(0, NT) as c:
                    for s in range(LT + 2):
                        if s < LT:
                            pe.wait_ge(att_done, c * LT + s + 1)
                            for i in range(KC):
                                mm = pe.matmul(k.PS[:, s % NA, :T], k.N[:, i, s * P:(s + 1) * P],
                                               QT[:, i, bass.ds(c * T, T)], start=(i == 0), stop=(i == KC - 1))
                            mm.then_inc(sc_ready, 1)
                        if s >= 2:
                            m = s - 2
                            pe.wait_ge(att_done, c * LT + m + 1 + NA)
                            if m == 0:
                                pe.wait_ge(val_used, c + 1)
                            for o in range(KC):
                                mm = pe.matmul(k.PS[:, 4 + o, :T], XT[:, m, o * P:(o + 1) * P], AT[:, m % NA, :],
                                               start=(m == 0), stop=(m == LT - 1))
                            mm.then_inc(att_used, 1)
                    pe.drain().then_inc(val_ready, 1)

            @block.scalar
            def _(act):
                act.sem_inc(att_done, NA)
                with act.Fori(0, NT) as c:
                    for m in range(LT):
                        act.wait_ge(sc_ready, c * LT + m + 1)
                        act.wait_ge(att_used, c * LT + m + 1)
                        act.activation(AT[:, m % NA, :], k.PS[:, m % NA, :T], ACT.Sigmoid).then_inc(att_done, 1)

            @block.vector
            def _(dve):
                dve.sem_inc(val_used, 1)
                with dve.Fori(0, NT) as c:
                    dve.wait_ge(val_ready, c + 1)
                    x = k.X[:, :, bass.ds(b * L + c * T, T)]
                    dve.tensor_tensor(x, x, k.PS[:, 4:4 + KC, :T], ALU.add).then_inc(val_used, 1)
        fresh(nc, used)


NE = 8
F = 4 * C
FBE = F // P
CAP = (5 * M // 4 + NE - 1) // NE
RT = 120
NR = CAP // RT
CH = CAP // 2
NO_SLOT = 8192.0
ZW = NE * CAP * C // (P * 9)


def route_image(nc, k, A, b, st):
    norm_image(nc, k, b, k.eps5)
    with ExitStack() as ctx:
        def sb(name, shape, dt=F32):
            return ctx.enter_context(nc.sbuf_tensor(k.name(name), shape, dt))

        XT = sb("XT5", [P, LT, C])
        transposed_image(nc, k, XT)
        LG = sb("LG", [P, LT, NE])
        OH = sb("OH", [P, LT, NE])
        POS = sb("POS", [P, LT, NE])
        SEEN = sb("SEEN", [P, LT, 1])
        red = sb("red", [P, 6, LT])
        SI = sb("SI", [P, LT], I32)
        used = sems(nc, ctx, "lg_ready", "lg_shifted", "lg_exp", "oh_done", "count_ready", "slot_done")
        lg_ready, lg_shifted, lg_exp, oh_done, count_ready, slot_done = used

        def wide(ap):
            return ap.rearrange("p (t o) -> p t o", o=1).broadcast_to([P, LT, NE])

        with nc.Block() as block:
            @block.tensor
            def _(pe):
                for t in range(LT):
                    for i in range(KC):
                        mm = pe.matmul(k.PS[:, 0, t * NE:(t + 1) * NE], k.N[:, i, t * P:(t + 1) * P], st.gate_w[:, i, :],
                                       start=(i == 0), stop=(i == KC - 1))
                mm.then_inc(lg_ready, 1)
                pe.wait_ge(oh_done, 1)
                oh = OH[:].rearrange("p t e -> p (t e)")
                pe.matmul(k.PS[:, 1, 0:LT * NE], st.tri[:], oh, start=True, stop=True)
                pe.matmul(k.PS[:, 2, 0:LT * NE], st.ones[:], oh, start=True, stop=True).then_inc(count_ready, 1)

            @block.scalar
            def _(act):
                act.wait_ge(lg_shifted, 1)
                act.activation(LG[:], LG[:], ACT.Exp).then_inc(lg_exp, 1)

            @block.vector
            def _(dve):
                mx, total, prb, pos, base, kept = (red[:, i, :] for i in range(6))
                dve.wait_ge(lg_ready, 1)
                logits = k.PS[:, 0, 0:LT * NE].rearrange("p (t e) -> p t e", e=NE)
                dve.tensor_tensor(LG[:], logits,
                                  st.gate_b[:].rearrange("p (o e) -> p o e", o=1).broadcast_to([P, LT, NE]), ALU.add)
                dve.drain()
                dve.tensor_reduce(mx, LG[:], AX.X, ALU.max)
                dve.drain()
                dve.tensor_tensor(LG[:], LG[:], wide(mx), ALU.subtract).then_inc(lg_shifted, 1)
                dve.wait_ge(lg_exp, 1)
                dve.tensor_reduce(total, LG[:], AX.X, ALU.add)
                dve.drain()
                dve.reciprocal(total, total)
                dve.drain()
                dve.tensor_tensor(LG[:], LG[:], wide(total), ALU.mult)
                dve.drain()
                dve.tensor_reduce(prb, LG[:], AX.X, ALU.max)
                dve.drain()
                dve.tensor_tensor(OH[:], LG[:], wide(prb), ALU.is_equal)
                dve.drain()
                dve.tensor_copy(SEEN[:, :, 0], OH[:, :, 0])
                for e in range(1, NE):
                    dve.drain()
                    dve.tensor_copy(POS[:, :, 0], OH[:, :, e])
                    dve.drain()
                    dve.tensor_tensor(OH[:, :, e], POS[:, :, 0], SEEN[:, :, 0], ALU.is_gt)
                    dve.tensor_tensor(SEEN[:, :, 0], SEEN[:, :, 0], POS[:, :, 0], ALU.max)
                dve.drain()
                dve.tensor_copy(OH[:, 0, 0:1], OH[:, 0, 0:1]).then_inc(oh_done, 1)
                dve.wait_ge(count_ready, 1)
                tot = k.PS[:, 2, 0:LT * NE].rearrange("p (t e) -> p t e", e=NE)
                for t in range(LT):
                    dve.tensor_tensor(st.PF[:, t + 1, :], st.PF[:, t, :], tot[:, t, :], ALU.add)
                    dve.drain()
                dve.tensor_tensor(POS[:], k.PS[:, 1, 0:LT * NE].rearrange("p (t e) -> p t e", e=NE),
                                  st.PF[:, 0:LT, :], ALU.add)
                dve.drain()
                dve.tensor_copy(st.PF[:, 0, :], st.PF[:, LT, :])
                dve.tensor_tensor(POS[:], POS[:], OH[:], ALU.mult)
                dve.drain()
                dve.tensor_reduce(pos, POS[:], AX.X, ALU.add)
                dve.tensor_tensor(OH[:], OH[:], st.slot0[:].rearrange("p (o e) -> p o e", o=1)
                                  .broadcast_to([P, LT, NE]), ALU.mult)
                dve.drain()
                dve.tensor_reduce(base, OH[:], AX.X, ALU.add)
                dve.tensor_scalar(pos, pos, -1.0, None, ALU.add)
                dve.drain()
                dve.tensor_scalar(kept, pos, float(CAP), None, ALU.is_lt)
                dve.drain()
                dve.tensor_tensor(st.WT[:, bass.ds(b * LT, LT)], prb, kept, ALU.mult)
                dve.tensor_scalar(kept, kept, -NO_SLOT, NO_SLOT, ALU.mult, ALU.add)
                dve.tensor_scalar(total, pos, float(CAP - 1), None, ALU.min)
                dve.drain()
                dve.tensor_tensor(kept, kept, pos, ALU.add)
                dve.tensor_tensor(st.GI[:, bass.ds(b * LT, LT)], total, base, ALU.add)
                dve.drain()
                dve.tensor_tensor(SI[:], kept, base, ALU.add).then_inc(slot_done, 1)

            @block.gpsimd
            def _(pool):
                pool.wait_ge(slot_done, 1)
                for t in range(LT):
                    pool.indirect_dma_start(
                        out=k.buf_dram, out_offset=bass.IndirectOffsetOnAxis(ap=SI[:, t:t + 1], axis=0),
                        in_=XT[:, t, :], in_offset=None, bounds_check=NE * CAP - 1, oob_is_err=False)\
                        .then_inc(k.row_sent, 16)
                pool.wait_ge(k.row_sent, (b + 1) * (16 * LT))
        fresh(nc, used)


def capacity_mixture(nc, k, A):
    with ExitStack() as top:
        st = Core()

        def keep(name, shape, dt=F32):
            return top.enter_context(nc.sbuf_tensor(k.name(name), shape, dt))

        st.gate_w = keep("gate_w", [P, KC, NE])
        st.gate_b = keep("gate_b", [P, NE])
        st.slot0 = keep("slot0", [P, NE])
        st.tri = keep("tri", [P, P])
        st.ones = keep("ones", [P, P])
        st.PF = keep("PF", [P, LT + 1, NE])
        st.GI = keep("GI", [P, NB * LT], I32)
        st.WT = keep("WT", [P, NB * LT])
        with ExitStack() as own:
            zero = own.enter_context(nc.sbuf_tensor(k.name("zero"), [P, ZW], F32))
            used = sems(nc, own, "zeroed", "gate_in", "buf_clear")
            zeroed, gate_in, buf_clear = used
            with nc.Block() as block:
                @block.vector
                def _(dve):
                    dve.memset(st.PF[:, 0, :], 0.0)
                    dve.memset(st.ones[:], 1.0)
                    dve.memset(zero[:], 0.0).then_inc(zeroed, 1)

                @block.sync
                def _(sp):
                    sp.dma_start(st.gate_w[:], A["l3_gate_w"]).then_inc(gate_in, 16)
                    sp.dma_start(st.tri[:], A["c_tri"]).then_inc(gate_in, 16)
                    sp.dma_start(st.gate_b[:], A["l3_gate_b"].broadcast_to([P, NE])).then_inc(gate_in, 16)
                    sp.dma_start(st.slot0[:], A["c_slot0"].broadcast_to([P, NE])).then_inc(gate_in, 16)
                    sp.wait_ge(zeroed, 1)
                    for i in range(9):
                        sp.dma_start(k.buf_dram.rearrange("(i p r) c -> i p (r c)", i=9, p=P)[i], zero[:])\
                          .then_inc(buf_clear, 16)
                    sp.wait_ge(gate_in, 64)
                    sp.wait_ge(buf_clear, 144)
            fresh(nc, used)
        with nc.Fori(0, NB) as b:
            route_image(nc, k, A, b, st)
        with ExitStack() as own:
            experts(nc, own, k, A)
        with nc.Fori(0, NB) as b:
            combine_image(nc, k, b, st)


def experts(nc, ctx, k, A):
    def sb(name, shape, dt=F32):
        return ctx.enter_context(nc.sbuf_tensor(k.name(name), shape, dt))

    w1 = sb("ew1", [P, KC, F])
    w2 = sb("ew2", [P, FBE, C])
    b1 = sb("eb1", [P, FBE])
    b2 = sb("eb2", [P, C])
    XR = sb("XR", [RT, NR, C])
    XB = sb("XB", [P, KC, CAP])
    H = sb("HE", [P, FBE, CAP])
    YB = sb("YB", [RT, NR, C])
    used = sems(nc, ctx, "e_loaded", "rows_in", "x_ready", "x_done", "h5_ready", "h5_done", "y_ready", "y_done", "y_sent")
    e_loaded, rows_in, x_ready, x_done, h5_ready, h5_done, y_ready, y_done, y_sent = used
    with nc.Fori(0, NE) as e:
        with nc.Block() as block:
            @block.sync
            def _(sp):
                sp.dma_start(XR[:], k.buf_dram[bass.ds(e * CAP, CAP), :].rearrange("(t p) c -> p t c", p=RT))\
                  .then_inc(rows_in, 16)
                sp.dma_start(w1[:], A["l3_w1"][bass.ds(e, 1)].rearrange("o p i n -> (o p) i n")).then_inc(e_loaded, 16)
                sp.dma_start(w2[:], A["l3_w2"][bass.ds(e, 1)].rearrange("o p i n -> (o p) i n")).then_inc(e_loaded, 16)
                sp.dma_start(b1[:], A["l3_b1"][bass.ds(e, 1)].rearrange("o p i -> (o p) i")).then_inc(e_loaded, 16)
                sp.dma_start(b2[:], A["l3_b2"][bass.ds(e, 1), :].broadcast_to([P, C])).then_inc(e_loaded, 16)
                sp.wait_ge(e_loaded, 64)
                for t in range(NR):
                    sp.wait_ge(y_done, t + 1)
                    sp.dma_start(k.y_dram[bass.ds(e * CAP + t * RT, RT), :], YB[:, t, :]).then_inc(y_sent, 16)
                sp.wait_ge(y_sent, 16 * NR)

            @block.tensor
            def _(pe):
                pe.wait_ge(rows_in, 16)
                for t in range(NR):
                    if t >= 2:
                        pe.wait_ge(x_done, t - 1)
                    for i in range(KC):
                        mm = pe.transpose(k.PS[:, t % 2, i * RT:(i + 1) * RT], XR[:, t, i * P:(i + 1) * P],
                                          k.ident[0:RT, 0:RT])
                    mm.then_inc(x_ready, 1)
                pe.wait_ge(x_done, NR)
                pe.wait_ge(e_loaded, 64)
                for n in range(FBE * 2):
                    f, c = n // 2, n % 2
                    if n >= 3:
                        pe.wait_ge(h5_done, n - 2)
                    for i in range(KC):
                        mm = pe.matmul(k.PS[:, 2 + n % 3, :CH], w1[:, i, f * P:(f + 1) * P], XB[:, i, c * CH:(c + 1) * CH],
                                       start=(i == 0), stop=(i == KC - 1))
                    mm.then_inc(h5_ready, 1)
                pe.wait_ge(h5_done, FBE * 2)
                for t in range(NR):
                    if t >= 2:
                        pe.wait_ge(y_done, t - 1)
                    for f in range(FBE):
                        mm = pe.matmul(k.PS[0:RT, 6 + t % 2, :C], H[:, f, t * RT:(t + 1) * RT], w2[:, f, :],
                                       start=(f == 0), stop=(f == FBE - 1))
                    mm.then_inc(y_ready, 1)

            @block.scalar
            def _(act):
                act.wait_ge(e_loaded, 64)
                for n in range(FBE * 2):
                    f, c = n // 2, n % 2
                    act.wait_ge(h5_ready, n + 1)
                    act.activation(H[:, f, c * CH:(c + 1) * CH], k.PS[:, 2 + n % 3, :CH], ACT.Relu, bias=b1[:, f:f + 1])\
                       .then_inc(h5_done, 1)

            @block.vector
            def _(dve):
                for t in range(NR):
                    dve.wait_ge(x_ready, t + 1)
                    dve.tensor_copy(XB[:, :, t * RT:(t + 1) * RT],
                                    k.PS[:, t % 2, 0:KC * RT].rearrange("p (i r) -> p i r", i=KC)).then_inc(x_done, 1)
                dve.wait_ge(e_loaded, 64)
                for t in range(NR):
                    dve.wait_ge(y_ready, t + 1)
                    dve.tensor_tensor(YB[:, t, :], k.PS[0:RT, 6 + t % 2, :C], b2[0:RT, :], ALU.add).then_inc(y_done, 1)
        fresh(nc, used)


FMAX = float(np.finfo(np.float32).max)


def combine_image(nc, k, b, st):
    with ExitStack() as ctx:
        def sb(name, shape, dt=F32):
            return ctx.enter_context(nc.sbuf_tensor(k.name(name), shape, dt))

        YG = sb("YG", [P, LT, C])
        OK = sb("OK", [P, LT, C])
        MK = sb("MK", [P, 2, C], I32)
        big = sb("big", [P, 2, C])
        gi = sb("gi", [P, LT], I32)
        used = sems(nc, ctx, "gi_done", "y_clean", "yt_ready", "yt_added")
        gi_done, y_clean, yt_ready, yt_added = used

        def add(dve, t):
            dve.wait_ge(yt_ready, t + 1)
            x = k.X[:, :, bass.ds(b * L + t * P, P)]
            dve.tensor_tensor(x, x, k.PS[:, t % 4, 0:C].rearrange("p (i n) -> p i n", i=KC), ALU.add)\
               .then_inc(yt_added, 1)

        with nc.Block() as block:
            @block.gpsimd
            def _(pool):
                pool.wait_ge(gi_done, 1)
                for t in range(LT):
                    pool.indirect_dma_start(
                        out=YG[:, t, :], out_offset=None, in_=k.y_dram,
                        in_offset=bass.IndirectOffsetOnAxis(ap=gi[:, t:t + 1], axis=0),
                        bounds_check=NE * CAP - 1, oob_is_err=False).then_inc(k.row_in, 16)
                pool.wait_ge(k.row_in, (b + 1) * (16 * LT))

            @block.vector
            def _(dve):
                dve.tensor_copy(gi[:], st.GI[:, bass.ds(b * LT, LT)]).then_inc(gi_done, 1)
                dve.memset(OK[:], 0.0)
                dve.memset(big[:, 0, :], 1e4)
                dve.memset(big[:, 1, :], -1e4)
                dve.wait_ge(k.row_in, (b + 1) * (16 * LT))
                for t in range(LT):
                    y = YG[:, t, :]
                    dve.tensor_scalar(y, y, st.WT[:, bass.ds(b * LT + t, 1)], None, ALU.mult)
                    dve.drain()
                    dve.tensor_tensor(MK[:, 0, :], y, y, ALU.is_equal)
                    dve.drain()
                    dve.copy_predicated(OK[:, t, :], MK[:, 0, :], y)
                    dve.drain()
                    dve.tensor_scalar(MK[:, 0, :], OK[:, t, :], FMAX, None, ALU.is_gt)
                    dve.tensor_scalar(MK[:, 1, :], OK[:, t, :], -FMAX, None, ALU.is_lt)
                    dve.drain()
                    dve.copy_predicated(OK[:, t, :], MK[:, 0, :], big[:, 0, :])
                    dve.drain()
                    dve.copy_predicated(OK[:, t, :], MK[:, 1, :], big[:, 1, :]).then_inc(y_clean, 1)
                    if t >= 1:
                        add(dve, t - 1)
                add(dve, LT - 1)

            @block.tensor
            def _(pe):
                for t in range(LT):
                    pe.wait_ge(y_clean, t + 1)
                    if t >= 4:
                        pe.wait_ge(yt_added, t - 3)
                    for i in range(KC):
                        mm = pe.transpose(k.PS[:, t % 4, i * P:(i + 1) * P], OK[:, t, i * P:(i + 1) * P], k.ident[:])
                    mm.then_inc(yt_ready, 1)
        fresh(nc, used)




def build(nc, A, out, start=0, upto=99):
    with ExitStack() as ctx:
        k = Core()
        k.serial = 0

        def name(n):
            k.serial += 1
            return f"{n}_{k.serial}"

        k.name = name
        k.X = ctx.enter_context(nc.sbuf_tensor("X", [P, KC, M], F32))
        k.N = ctx.enter_context(nc.sbuf_tensor("N", [P, KC, L], F32))
        k.ident = ctx.enter_context(nc.sbuf_tensor("ident", [P, P], F32))
        k.mean_w = ctx.enter_context(nc.sbuf_tensor("mean_w", [P, P], F32))
        k.group_w = ctx.enter_context(nc.sbuf_tensor("group_w", [P, P], F32))
        k.zeros = ctx.enter_context(nc.sbuf_tensor("zeros", [1, BANK], BF16))
        k.eps5 = ctx.enter_context(nc.sbuf_tensor("eps5", [P, 1], F32))
        k.cnt = ctx.enter_context(nc.sbuf_tensor("cnt", [P, NU], F32))
        k.PS = ctx.enter_context(nc.psum_tensor("PS", [P, 8, BANK], F32))
        k.proj_dram = nc.dram_tensor("proj_dram", [DR + 2 * DS, L], F32, kind="Internal").ap()
        k.edges_dram = nc.dram_tensor("edges_dram", [P, EC], I32, kind="Internal").ap()
        k.idx_dram = nc.dram_tensor("idx_dram", [2, P, EC], I32, kind="Internal").ap()
        k.dig_dram = nc.dram_tensor("dig_dram", [2, P, EC], F32, kind="Internal").ap()
        k.src_dram = nc.dram_tensor("src_dram", [M, ROW], F32, kind="Internal").ap()
        k.dst_dram = nc.dram_tensor("dst_dram", [M, 2 * E2], F32, kind="Internal").ap()
        k.gate_dram = nc.dram_tensor("gate_dram", [E2 * TM, P], F32, kind="Internal").ap()
        k.buf_dram = nc.dram_tensor("buf_dram", [NE * CAP, C], F32, kind="Internal").ap()
        k.y_dram = nc.dram_tensor("y_dram", [NE * CAP, C], F32, kind="Internal").ap()
        k.row_sent = ctx.enter_context(nc.semaphore("row_sent"))
        k.row_in = ctx.enter_context(nc.semaphore("row_in"))
        k.turns = ctx.enter_context(nc.semaphore("turns"))
        k.rs_in = [ctx.enter_context(nc.semaphore(f"rs_in{u}")) for u in range(NU)]
        k.rd_in = [ctx.enter_context(nc.semaphore(f"rd_in{u}")) for u in range(NU)]
        with nc.Block() as block:
            @block.vector
            def _(dve):
                dve.memset(k.zeros[:], 0.0)
                dve.memset(k.eps5[:], 1e-5)
        load_constants(nc, ctx, k, A)
        if start <= 0 <= upto:
            with nc.Fori(0, NB) as b:
                mamba(nc, k, A, b)
        if start <= 1 <= upto:
            with nc.Fori(0, NB) as b:
                linear_attention_block(nc, k, A, b)
        if start <= 2 <= upto:
            with nc.Fori(0, NB) as b:
                softmax_attention(nc, k, A, b)
        if start <= 3 <= upto:
            graph_mixture(nc, k, A)
        if start <= 4 <= upto:
            with nc.Fori(0, NB) as b:
                sigmoid_attention(nc, k, A, b)
        if start <= 5 <= upto:
            capacity_mixture(nc, k, A)
        with ExitStack() as own:
            (stored,) = sems(nc, own, "stored")
            with nc.Block() as block:
                @block.sync
                def _(sp):
                    for b in range(NB):
                        sp.dma_start(out[b].rearrange("(k p) n -> p k n", p=P), k.X[:, :, b * L:(b + 1) * L])\
                          .then_inc(stored, 16)
                    sp.wait_ge(stored, 16 * NB)


def layout(inputs):
    a = {n: np.asarray(v) for n, v in inputs.items()}
    A = {"x": a["x"].reshape(NB, C, L)}

    def cols(w, kc):
        return w.reshape(kc, P, -1).transpose(1, 0, 2)

    A["c_ident"] = np.eye(P, dtype=np.float32)
    A["c_mean"] = np.full((P, P), 1.0 / C, np.float32)
    A["c_group"] = np.kron(np.eye(P // 8), np.full((8, 8), 1.0 / 8)).astype(np.float32)
    inv = (np.float32(1.0) / np.power(np.float32(10000.0), np.arange(0, C, 2, dtype=np.float32) / np.float32(C)))
    ang = (np.arange(L, dtype=np.float32)[:, None] * inv.astype(np.float32)[None, :]).astype(np.float32)
    pos = np.concatenate([np.sin(ang.astype(np.float64)), np.cos(ang.astype(np.float64))], -1).astype(np.float32)
    A["c_pos"] = cols(pos.T, KC)
    A["l0_ln"] = np.stack([a["L0_conv_ln_g"], a["L0_conv_ln_b"]], -1).reshape(KC, P, 2).transpose(1, 0, 2)
    A["L0_conv_pos_scale"] = a["L0_conv_pos_scale"]
    A["l0_w_in"] = cols(a["L0_conv_in_proj_w"].T, KC)
    A["l0_w_out"] = cols(a["L0_conv_out_proj_w"].T, JD)
    for d in "fb":
        A["l0_conv_w_" + d] = cols(a["L0_conv_conv_w_" + d], JD)
        A["l0_vec_" + d] = cols(np.stack([a["L0_conv_conv_b_" + d], a["L0_conv_dtproj_b_" + d], a["L0_conv_D_" + d]], -1), JD)
        A["l0_alog_" + d] = cols(a["L0_conv_A_log_" + d], JD)
        A["l0_w_x_" + d] = cols(a["L0_conv_xproj_w_" + d].T, JD)
        A["l0_w_dt_" + d] = a["L0_conv_dtproj_w_" + d].T
    A["c_head"] = np.kron(np.eye(P // 32), np.full((32, 32), 32.0 ** -0.5)).astype(np.float32)
    A["l1_vec"] = np.stack([a["L1_conv_bqkv"][:C], a["L1_conv_dw_b"], a["L1_conv_bproj"]]
                           + [a[f"L1_conv_bn{w}_{s}"] for w in "12" for s in "gbmv"] + [a["L1_conv_bfc2"]], -1)\
        .reshape(KC, P, 12).transpose(1, 0, 2)
    A["l1_bkv"] = a["L1_conv_bqkv"][C:].reshape(1, 2 * C)
    A["l1_alpha"] = np.stack([a["L1_conv_alpha1"], a["L1_conv_alpha2"]], -1).reshape(1, 2)
    A["l1_w_qkv"] = cols(a["L1_conv_Wqkv"], KC)
    A["l1_w_proj"] = cols(a["L1_conv_Wproj"], KC)
    A["l1_dw"] = cols(a["L1_conv_dw_w"].reshape(C, TAPS * TAPS), KC)
    A["l1_w_fc1"] = cols(a["L1_conv_Wfc1"], KC)
    A["l1_w_fc2"] = cols(a["L1_conv_Wfc2"], NM)
    A["l1_b_fc1"] = a["L1_conv_bfc1"].reshape(NM, P).T
    A["l2_w_et"] = a["L2_attn_W_embed"].transpose(0, 2, 1).reshape(NH, KC, P, H3).transpose(0, 2, 1, 3)
    A["l2_w_e"] = a["L2_attn_W_embed"].reshape(NH, FB, P, C).transpose(0, 2, 1, 3)
    A["l2_b_e"] = a["L2_attn_b_embed"].reshape(NH, FB, P).transpose(0, 2, 1)
    A["l2_w_out"] = cols(a["L2_attn_W_out"].T, FB)
    A["l2_b_out"] = a["L2_attn_b_out"].reshape(KC, P).T
    A["edges"] = a["L2_ffn_edge_index"]
    A["l2_w_gat"] = cols(a["L2_ffn_W_gat"], KC)
    A["l2_att"] = np.stack([a["L2_ffn_att_src"], a["L2_ffn_att_dst"]]).reshape(1, 2, HE)
    A["l2_g_rows"] = np.stack([a["L2_ffn_b_gat"], a["L2_ffn_ln_gamma"], a["L2_ffn_ln_beta"]]).reshape(1, 3, HE)
    A["c_iota"] = np.arange(BW, dtype=np.float32).reshape(1, BW)
    A["l2_w1"] = cols(a["L2_ffn_W1"].transpose(1, 0, 2).reshape(C, E2 * F2), KC)
    A["l2_w2"] = cols(a["L2_ffn_W2"].reshape(E2 * F2, C), NM)
    A["l2_b1"] = a["L2_ffn_b1"].reshape(NM, P).T
    A["l2_b2"] = a["L2_ffn_b2"]
    A["l3_w_q"] = cols(a["L3_attn_q_weight"], KC)
    A["c_tri"] = np.triu(np.ones((P, P), np.float32))
    A["c_slot0"] = (np.arange(NE, dtype=np.float32) * CAP).reshape(1, NE)
    A["l3_gate_w"] = cols(a["L3_ffn_gate_w"], KC)
    A["l3_gate_b"] = a["L3_ffn_gate_b"].reshape(1, NE)
    A["l3_w1"] = a["L3_ffn_w1"].reshape(NE, KC, P, F).transpose(0, 2, 1, 3)
    A["l3_w2"] = a["L3_ffn_w2"].reshape(NE, FBE, P, C).transpose(0, 2, 1, 3)
    A["l3_b1"] = a["L3_ffn_b1"].reshape(NE, FBE, P).transpose(0, 2, 1)
    A["l3_b2"] = a["L3_ffn_b2"]
    return {n: np.ascontiguousarray(v) for n, v in A.items()}


def kernel(**inputs):
    import concourse.bacc as bacc
    from concourse.bass_utils import run_bass_kernel_spmd

    nc = bacc.Bacc("TRN2", target_bir_lowering=False, num_devices=1)
    arrays = layout(inputs)
    A = {n: nc.dram_tensor(f"in_{n}", v.shape, mybir.dt.from_np(v.dtype), kind="ExternalInput").ap()
         for n, v in arrays.items()}
    out = nc.dram_tensor("out_0", (NB, C, L), F32, kind="ExternalOutput").ap()
    build(nc, A, out)
    r = run_bass_kernel_spmd(nc, [{f"in_{n}": v for n, v in arrays.items()}], core_ids=[0])
    return np.asarray(r.results[0]["out_0"]).reshape(NB, C, HW, HW)
```

```python
import concourse.bass as bass
from concourse import mybir
from contextlib import ExitStack

import numpy as np

F32 = mybir.dt.float32
I32 = mybir.dt.int32
I16 = mybir.dt.int16
BF16 = mybir.dt.bfloat16
ALU = mybir.AluOpType
ACT = mybir.ActivationFunctionType
AX = mybir.AxisListType

P = 128
NB = 2
C = 256
KC = C // P
HW = 48
L = HW * HW
M = NB * L
T = 384
NT = L // T
BANK = 512

DI = 512
JD = DI // P
DS = 16
DR = 16
NQ = 3
Q = L // NQ


def sems(nc, ctx, *names):
    return [ctx.enter_context(nc.semaphore(n)) for n in names]


def fresh(nc, used):
    with nc.Block() as block:
        @block.sync
        def _(sp):
            for s in used:
                sp.sem_clear(s)


class Core:
    pass


def load_constants(nc, ctx, k, A):
    with ExitStack() as own:
        (loaded,) = sems(nc, own, "loaded")
        with nc.Block() as block:
            @block.sync
            def _(sp):
                n = 0
                for b in range(NB):
                    sp.dma_start(k.X[:, :, b * L:(b + 1) * L],
                                 A["x"][b].rearrange("(k p) n -> p k n", p=P)).then_inc(loaded, 16)
                    n += 16
                for dst, name in ((k.ident, "c_ident"), (k.mean_w, "c_mean"), (k.group_w, "c_group")):
                    sp.dma_start(dst[:], A[name]).then_inc(loaded, 16)
                    n += 16
                sp.wait_ge(loaded, n)
        fresh(nc, [loaded])


def norm_image(nc, k, b, eps):
    DEEP = 3
    TT = T // P
    with ExitStack() as ctx:
        xs = ctx.enter_context(nc.sbuf_tensor(k.name("xs"), [P, DEEP, T], F32))
        sq = ctx.enter_context(nc.sbuf_tensor(k.name("sq"), [P, DEEP, KC, T], F32))
        rstd = ctx.enter_context(nc.sbuf_tensor(k.name("rstd"), [P, DEEP, TT], F32))
        used = sems(nc, ctx, "x_summed", "mean_ready", "centered", "squared", "sq_summed", "var_ready", "rooted",
                    "inverted", "spread", "normalized")
        x_summed, mean_ready, centered, squared, sq_summed, var_ready, rooted, inverted, spread, normalized = used
        with nc.Block() as block:
            @block.gpsimd
            def _(pool):
                for s in range(NT + 2):
                    if s < NT:
                        if s >= DEEP:
                            pool.wait_ge(mean_ready, s - DEEP + 1)
                        at = bass.ds(b * L + s * T, T)
                        pool.tensor_tensor(xs[:, s % DEEP, :], k.X[:, 0, at], k.X[:, 1, at], ALU.add).then_inc(x_summed, 1)
                    if s >= 2:
                        v = s - 2
                        pool.wait_ge(squared, v + 1)
                        pool.tensor_tensor(sq[:, v % DEEP, 0, :], sq[:, v % DEEP, 0, :], sq[:, v % DEEP, 1, :], ALU.add)\
                            .then_inc(sq_summed, 1)

            @block.tensor
            def _(pe):
                for s in range(NT + 2):
                    if s < NT:
                        pe.wait_ge(x_summed, s + 1)
                        if s >= DEEP:
                            pe.wait_ge(centered, s - DEEP + 1)
                        pe.matmul(k.PS[:, s % DEEP, :T], k.mean_w[:], xs[:, s % DEEP, :], start=True, stop=True)\
                          .then_inc(mean_ready, 1)
                    if 1 <= s <= NT:
                        v = s - 1
                        pe.wait_ge(sq_summed, v + 1)
                        if v >= DEEP:
                            pe.wait_ge(normalized, v - DEEP + 1)
                        for t in range(TT):
                            mm = pe.matmul(k.PS[:, DEEP + v % DEEP, t:t + 1], sq[:, v % DEEP, 0, t * P:(t + 1) * P],
                                           k.mean_w[:, 0:1], start=True, stop=True)
                        mm.then_inc(var_ready, 1)
                    if s >= 2:
                        v = s - 2
                        pe.wait_ge(inverted, v + 1)
                        for t in range(TT):
                            mm = pe.matmul(k.PS[:, DEEP + v % DEEP, P + t * P:2 * P + t * P],
                                           rstd[:, v % DEEP, t:t + 1].broadcast_to([P, P]), k.ident[:],
                                           start=True, stop=True)
                        mm.then_inc(spread, 1)

            @block.vector
            def _(dve):
                for s in range(NT + 2):
                    if s < NT:
                        dve.wait_ge(mean_ready, s + 1)
                        mean = k.PS[:, s % DEEP, :T].rearrange("p (o t) -> p o t", o=1).broadcast_to([P, KC, T])
                        dve.tensor_tensor(k.N[:, :, s * T:(s + 1) * T], k.X[:, :, bass.ds(b * L + s * T, T)],
                                          mean, ALU.subtract).then_inc(centered, 1)
                    if 1 <= s <= NT:
                        v = s - 1
                        dve.wait_ge(rooted, v + 1)
                        dve.reciprocal(rstd[:, v % DEEP, :], rstd[:, v % DEEP, :]).then_inc(inverted, 1)
                    if s >= 2:
                        v = s - 2
                        dve.wait_ge(spread, v + 1)
                        root = k.PS[:, DEEP + v % DEEP, P:P + T].rearrange("p (o t) -> p o t", o=1)\
                                .broadcast_to([P, KC, T])
                        n = k.N[:, :, v * T:(v + 1) * T]
                        dve.tensor_tensor(n, n, root, ALU.mult).then_inc(normalized, 1)

            @block.scalar
            def _(act):
                for s in range(NT + 1):
                    if s < NT:
                        act.wait_ge(centered, s + 1)
                        if s >= DEEP:
                            act.wait_ge(var_ready, s - DEEP + 1)
                        act.activation(sq[:, s % DEEP, :, :], k.N[:, :, s * T:(s + 1) * T], ACT.Square)\
                           .then_inc(squared, 1)
                    if s >= 1:
                        v = s - 1
                        act.wait_ge(var_ready, v + 1)
                        if v >= DEEP:
                            act.wait_ge(spread, v - DEEP + 1)
                        act.activation(rstd[:, v % DEEP, :], k.PS[:, DEEP + v % DEEP, 0:TT], ACT.Sqrt, bias=eps[:])\
                           .then_inc(rooted, 1)
        fresh(nc, used)


def mamba(nc, k, A, b):
    with ExitStack() as ctx:
        def sb(name, shape, dt=F32):
            return ctx.enter_context(nc.sbuf_tensor(k.name(name), shape, dt))

        w_in = sb("w_in", [P, KC, DI])
        XS = sb("XS", [P, JD, L])
        Y = sb("Y", [P, JD, L])
        gb = sb("gb", [P, KC, 2])
        pscale = sb("pscale", [P, 1])
        used = sems(nc, ctx, "l0_loaded", "l0_scaled")
        l0_loaded, l0_scaled = used
        pos = Y[:, 0:KC, :]
        with nc.Block() as block:
            @block.sync
            def _(sp):
                sp.dma_start(pos, A["c_pos"]).then_inc(l0_loaded, 16)
                sp.dma_start(gb[:], A["l0_ln"]).then_inc(l0_loaded, 16)
                sp.dma_start(pscale[:], A["L0_conv_pos_scale"].rearrange("(o n) -> o n", o=1)
                             .broadcast_to([P, 1])).then_inc(l0_loaded, 16)
                sp.dma_start(w_in[:], A["l0_w_in"][:, :, 0:DI]).then_inc(l0_loaded, 16)
        norm_image(nc, k, b, k.eps5)
        with nc.Block() as block:
            @block.scalar
            def _(act):
                act.wait_ge(l0_loaded, 64)
                act.activation(k.N[:, 1, :], k.N[:, 1, :], ACT.Identity, bias=gb[:, 1, 1:2], scale=gb[:, 1, 0:1])\
                   .then_inc(l0_scaled, 1)

            @block.vector
            def _(dve):
                dve.wait_ge(l0_loaded, 64)
                dve.tensor_scalar(k.N[:, 0, :], k.N[:, 0, :], gb[:, 0, 0:1], gb[:, 0, 1:2], ALU.mult, ALU.add)
                dve.drain()
                for c in range(KC):
                    if c == 1:
                        dve.wait_ge(l0_scaled, 1)
                    dve.scalar_tensor_tensor(k.N[:, c, :], pos[:, c, :], pscale[:], k.N[:, c, :], ALU.mult, ALU.add)
        fresh(nc, used)
        for rev in range(2):
            with ExitStack() as own:
                mamba_direction(nc, own, k, A, w_in, XS, Y, rev)
        mamba_output(nc, ctx, k, A, b, w_in, Y)


def mamba_direction(nc, ctx, k, A, w_in, XS, Y, rev):
    def sb(name, shape, dt=F32):
        return ctx.enter_context(nc.sbuf_tensor(k.name(name), shape, dt))

    d = "fb"[rev]
    PAD = 3
    region = sb("region", [P, 2 * JD * Q + 64])
    XP2 = region[:, 0:2 * (L + 2 * PAD)].rearrange("p (u t) -> p u t", u=2)
    DT = region[:, 0:JD * Q].rearrange("p (j t) -> p j t", j=JD)
    DU = region[:, JD * Q:2 * JD * Q].rearrange("p (j t) -> p j t", j=JD)
    work = sb("work", [P, 10, Q])
    PJ = work[0:3 * DS, 0:3, :].rearrange("p a t -> p (a t)")
    DA, DBU, G = (work[:, 2 * i:2 * i + 2, :] for i in range(3))
    HS = work[:, 6:6 + JD, :]
    diag = sb("diag", [P, JD, P])
    BB = sb("BB", [P, 2, Q])
    CB = sb("CB", [P, 2, Q])
    dtr = BB[0:DR, 0, :]
    conv_w = sb("conv_w", [P, JD, 4])
    vec = sb("vec", [P, JD, 3])
    alog = sb("alog", [P, JD, DS])
    w_x = sb("w_x", [P, JD, 3 * DS])
    w_dt = sb("w_dt", [DR, DI])
    HC = sb("HC", [P, JD, DS])

    used = sems(nc, ctx, "params", "xi_ready", "xi_copied", "conv_done", "xs_done", "pj_ready", "pj_copied",
                "pj_stored", "padded")
    params, xi_ready, xi_copied, conv_done, xs_done, pj_ready, pj_copied, pj_stored, padded = used
    with nc.Block() as block:
        @block.sync
        def _(sp):
            for dst, name in ((conv_w, "l0_conv_w_"), (vec, "l0_vec_"), (alog, "l0_alog_"), (w_x, "l0_w_x_"),
                              (w_dt, "l0_w_dt_")):
                sp.dma_start(dst[:], A[name + d]).then_inc(params, 16)
            sp.wait_ge(params, 80)
            sp.wait_ge(pj_copied, NT)
            sp.dma_start(k.proj_dram, PJ).then_inc(pj_stored, 16)
            sp.wait_ge(pj_stored, 16)

        @block.tensor
        def _(pe):
            for s in range(JD + 2):
                if s < JD:
                    for c in range(NT):
                        n = s * NT + c
                        if n >= 2:
                            pe.wait_ge(xi_copied, n - 1)
                        for i in range(KC):
                            mm = pe.matmul(k.PS[:, n % 2, :T], w_in[:, i, s * P:(s + 1) * P],
                                           k.N[:, i, c * T:(c + 1) * T], start=(i == 0), stop=(i == KC - 1))
                        mm.then_inc(xi_ready, 1)
                if s >= 2:
                    j = s - 2
                    if j == 0:
                        pe.wait_ge(params, 80)
                    pe.wait_ge(xs_done, j + 1)
                    for c in range(NT):
                        mm = pe.matmul(k.PS[0:3 * DS, 2 + c, :T], w_x[:, j, :], XS[:, j, c * T:(c + 1) * T],
                                       start=(j == 0), stop=(j == JD - 1))
                        if j == JD - 1:
                            mm.then_inc(pj_ready, 1)

        @block.scalar
        def _(act):
            act.wait_ge(params, 80)
            for s in range(JD + 2):
                if s < JD:
                    if s >= 2:
                        act.wait_ge(conv_done, s - 1)
                    for c in range(NT):
                        act.wait_ge(xi_ready, s * NT + c + 1)
                        act.activation(XP2[:, s % 2, PAD + c * T:PAD + (c + 1) * T], k.PS[:, (s * NT + c) % 2, :T],
                                       ACT.Copy).then_inc(xi_copied, 1)
                if s >= 2:
                    j = s - 2
                    act.wait_ge(conv_done, j + 1)
                    act.activation(XS[:, j, :], XS[:, j, :], ACT.Silu, bias=vec[:, j, 0:1]).then_inc(xs_done, 1)
            for c in range(NT):
                act.wait_ge(pj_ready, c + 1)
                act.activation(PJ[:, c * T:(c + 1) * T], k.PS[0:3 * DS, 2 + c, :T], ACT.Copy).then_inc(pj_copied, 1)
            act.activation(alog[:], alog[:], ACT.Exp)
            act.drain()
            act.mul(alog[:], alog[:], -1.0)

        @block.vector
        def _(dve):
            for u in range(2):
                dve.memset(XP2[:, u, 0:PAD], 0.0)
                dve.memset(XP2[:, u, PAD + L:2 * PAD + L], 0.0)
            dve.memset(HC[:], 0.0)
            dve.drain()
            dve.wait_ge(params, 80)
            for j in range(JD):
                dve.tensor_scalar(diag[:, j, :], k.ident[:], vec[:, j, 2:3], None, ALU.mult)
            for j in range(JD):
                dve.wait_ge(xi_copied, (j + 1) * NT)
                out = XS[:, j, :]
                for t in range(4):
                    at = 2 * PAD - t if rev else t
                    xp = XP2[:, j % 2, at:at + L]
                    if t == 0:
                        dve.tensor_scalar(out, xp, conv_w[:, j, 0:1], None, ALU.mult)
                    else:
                        dve.drain()
                        op = dve.scalar_tensor_tensor(out, xp, conv_w[:, j, t:t + 1], out, ALU.mult, ALU.add)
                op.then_inc(conv_done, 1)
    fresh(nc, used)

    H = Q // 2
    used = sems(nc, ctx, "dtr_in", "dt_ready", "dt_exp", "dt_left", "dt_rest", "dt_log", "dt_done",
                "b_in0", "b_in1", "c_in0", "c_in1", "da_done", "dbu_done", "h_done", "hc_done", "g_done", "acc_done")
    (dtr_in, dt_ready, dt_exp, dt_left, dt_rest, dt_log, dt_done,
     b_in0, b_in1, c_in0, c_in1, da_done, dbu_done, h_done, hc_done, g_done, acc_done) = used
    b_in, c_in = (b_in0, b_in1), (c_in0, c_in1)
    with nc.Fori(0, NQ) as i:
        t0 = (NQ - 1) * Q - i * Q if rev else i * Q
        piece = bass.ds(t0, Q)
        E, U, LN = work[:, 0:JD, :], work[:, JD:JD + 2, :], work[:, JD + 2:JD + 4, :]
        with nc.Block() as block:
            @block.sync
            def _(sp):
                sp.dma_start(dtr, k.proj_dram[0:DR, piece]).then_inc(dtr_in, 16)
                sp.wait_ge(dtr_in, 16)

            @block.tensor
            def _(pe):
                pe.wait_ge(dtr_in, 16)
                for j in range(JD):
                    for h in range(2):
                        mm = pe.matmul(k.PS[:, 2 * j + h, :H], w_dt[:, j * P:(j + 1) * P], dtr[:, h * H:(h + 1) * H],
                                       start=True, stop=True)
                    mm.then_inc(dt_ready, 1)

            @block.scalar
            def _(act):
                def halves(ap):
                    return ap.rearrange("p (h t) -> p h t", h=2)

                for j in range(JD):
                    act.wait_ge(dt_ready, j + 1)
                    x = k.PS[:, 2 * j:2 * j + 2, :H]
                    act.activation(halves(E[:, j, :]), x, ACT.Abs, bias=vec[:, j, 1:2])
                    act.activation(halves(DT[:, j, :]), x, ACT.Relu, bias=vec[:, j, 1:2])
                    act.drain()
                    act.activation(E[:, j, :], E[:, j, :], ACT.Exp, scale=-1.0).then_inc(dt_exp, 1)
                act.drain()
                for j in range(JD):
                    if j >= 2:
                        act.wait_ge(dt_done, j - 1)
                    act.activation(LN[:, j % 2, :], E[:, j, :], ACT.Ln, bias=1.0).then_inc(dt_log, 1)

            @block.vector
            def _(dve):
                for j in range(JD):
                    dve.wait_ge(dt_exp, j + 1)
                    if j >= 2:
                        dve.wait_ge(dt_rest, j - 1)
                    dve.tensor_scalar(U[:, j % 2, :], E[:, j, :], 1.0, 1.0, ALU.add, ALU.subtract)
                    dve.drain()
                    dve.tensor_tensor(U[:, j % 2, :], E[:, j, :], U[:, j % 2, :], ALU.subtract).then_inc(dt_left, 1)
                for j in range(JD):
                    dve.wait_ge(dt_rest, j + 1)
                    dve.wait_ge(dt_log, j + 1)
                    dve.tensor_tensor(DT[:, j, :], DT[:, j, :], LN[:, j % 2, :], ALU.add).then_inc(dt_done, 1)
                    dve.drain()
                    if j % 2:
                        dve.tensor_tensor(DU[:, j, :], DT[:, j, :], XS[:, j, piece], ALU.mult)

            @block.gpsimd
            def _(pool):
                for j in range(JD):
                    pool.wait_ge(dt_left, j + 1)
                    pool.tensor_tensor(DT[:, j, :], DT[:, j, :], U[:, j % 2, :], ALU.add).then_inc(dt_rest, 1)
                for j in range(0, JD, 2):
                    pool.wait_ge(dt_done, j + 1)
                    pool.tensor_tensor(DU[:, j, :], DT[:, j, :], XS[:, j, piece], ALU.mult)

        def flow(ap):
            return ap[:, ::-1] if rev else ap

        STEPS = DS * JD
        last = 0 if rev else Q - 1
        with nc.Block() as block:
            @block.sync
            def _(sp):
                for n in range(DS):
                    if n >= 2:
                        sp.wait_ge(dbu_done, (n - 1) * JD)
                        sp.wait_ge(g_done, (n - 1) * JD)
                    for row, dst, s in ((DR, BB, b_in[n % 2]), (DR + DS, CB, c_in[n % 2])):
                        sp.dma_start(dst[:, n % 2, :], k.proj_dram[row + n:row + n + 1, piece].broadcast_to([P, Q]))\
                          .then_inc(s, 16)

            @block.scalar
            def _(act):
                for s in range(STEPS + 2):
                    n, j = divmod(s, JD)
                    if s >= 2:
                        act.wait_ge(h_done, s - 1)
                    if s < STEPS:
                        act.activation(DA[:, j % 2, :], DT[:, j, :], ACT.Exp, scale=alog[:, j, n:n + 1])\
                           .then_inc(da_done, 1)
                    if s >= 2:
                        n, j = divmod(s - 2, JD)
                        act.activation(HC[:, j, n:n + 1], HS[:, j, last:last + 1], ACT.Copy).then_inc(hc_done, 1)

            @block.gpsimd
            def _(pool):
                for s in range(STEPS):
                    n, j = divmod(s, JD)
                    if j == 0:
                        pool.wait_ge(b_in[n % 2], 16 * (n // 2 + 1))
                    if s >= 2:
                        pool.wait_ge(h_done, s - 1)
                    pool.tensor_tensor(DBU[:, j % 2, :], DU[:, j, :], BB[:, n % 2, :], ALU.mult).then_inc(dbu_done, 1)

            @block.vector
            def _(dve):
                for s in range(STEPS + 1):
                    n, j = divmod(s, JD)
                    if s < STEPS:
                        dve.wait_ge(da_done, s + 1)
                        dve.wait_ge(dbu_done, s + 1)
                        if s >= JD:
                            dve.wait_ge(hc_done, s - JD + 1)
                        dve.tensor_tensor_scan(flow(HS[:, j, :]), flow(DA[:, j % 2, :]), flow(DBU[:, j % 2, :]),
                                               HC[:, j, n:n + 1], ALU.mult, ALU.add).then_inc(h_done, 1)
                    if s >= 1:
                        n, j = divmod(s - 1, JD)
                        if j == 0:
                            dve.wait_ge(c_in[n % 2], 16 * (n // 2 + 1))
                        dve.wait_ge(h_done, s)
                        if s >= 3:
                            dve.wait_ge(acc_done, s - 2)
                        dve.tensor_tensor(G[:, j % 2, :], HS[:, j, :], CB[:, n % 2, :], ALU.mult).then_inc(g_done, 1)

            @block.tensor
            def _(pe):
                for j in range(JD):
                    for h in range(2):
                        at = bass.ds(t0 + h * H, H)
                        pe.matmul(k.PS[:, 2 * j + h, :H], diag[:, j, :], XS[:, j, at], start=True, stop=False)
                        if rev:
                            pe.matmul(k.PS[:, 2 * j + h, :H], k.ident[:], Y[:, j, at], start=False, stop=False)
                for s in range(STEPS):
                    n, j = divmod(s, JD)
                    pe.wait_ge(g_done, s + 1)
                    for h in range(2):
                        mm = pe.matmul(k.PS[:, 2 * j + h, :H], k.ident[:], G[:, j % 2, h * H:(h + 1) * H],
                                       start=False, stop=(n == DS - 1))
                    mm.then_inc(acc_done, 1)
        with nc.Block() as block:
            @block.vector
            def _(dve):
                for j in range(0, JD, 2):
                    dve.tensor_copy(Y[:, j, piece].rearrange("p (h t) -> p h t", h=2), k.PS[:, 2 * j:2 * j + 2, :H])

            @block.scalar
            def _(act):
                for j in range(1, JD, 2):
                    act.activation(Y[:, j, piece].rearrange("p (h t) -> p h t", h=2), k.PS[:, 2 * j:2 * j + 2, :H],
                                   ACT.Copy)
        fresh(nc, used)


def mamba_output(nc, ctx, k, A, b, w_in, Y):
    w_out = ctx.enter_context(nc.sbuf_tensor(k.name("w_out"), [P, JD, C], F32))
    Z = ctx.enter_context(nc.sbuf_tensor(k.name("Z"), [P, 2, T], F32))
    used = sems(nc, ctx, "wz_in", "wo_in", "z_ready", "z_done", "gated", "o_ready", "o_added")
    wz_in, wo_in, z_ready, z_done, gated, o_ready, o_added = used
    with nc.Block() as block:
        @block.sync
        def _(sp):
            sp.dma_start(w_in[:], A["l0_w_in"][:, :, DI:2 * DI]).then_inc(wz_in, 16)
            sp.dma_start(w_out[:], A["l0_w_out"]).then_inc(wo_in, 16)
            sp.wait_ge(wz_in, 16)
            sp.wait_ge(wo_in, 16)

        @block.tensor
        def _(pe):
            pe.wait_ge(wz_in, 16)
            for c in range(NT):
                for j in range(JD):
                    n = c * JD + j
                    if n >= 2:
                        pe.wait_ge(z_done, n - 1)
                    for i in range(KC):
                        mm = pe.matmul(k.PS[:, n % 2, :T], w_in[:, i, j * P:(j + 1) * P],
                                       k.N[:, i, c * T:(c + 1) * T], start=(i == 0), stop=(i == KC - 1))
                    mm.then_inc(z_ready, 1)
                pe.wait_ge(gated, (c + 1) * JD)
                if c == 0:
                    pe.wait_ge(wo_in, 16)
                else:
                    pe.wait_ge(o_added, c)
                for m in range(KC):
                    for j in range(JD):
                        mm = pe.matmul(k.PS[:, 2 + m, :T], w_out[:, j, m * P:(m + 1) * P], Y[:, j, c * T:(c + 1) * T],
                                       start=(j == 0), stop=(j == JD - 1))
                mm.then_inc(o_ready, 1)

        @block.scalar
        def _(act):
            for n in range(NT * JD):
                act.wait_ge(z_ready, n + 1)
                if n >= 2:
                    act.wait_ge(gated, n - 1)
                act.activation(Z[:, n % 2, :], k.PS[:, n % 2, :T], ACT.Silu).then_inc(z_done, 1)

        @block.vector
        def _(dve):
            for c in range(NT):
                for j in range(JD):
                    n = c * JD + j
                    dve.wait_ge(z_done, n + 1)
                    dve.tensor_tensor(Y[:, j, c * T:(c + 1) * T], Y[:, j, c * T:(c + 1) * T], Z[:, n % 2, :], ALU.mult)\
                       .then_inc(gated, 1)
                dve.wait_ge(o_ready, c + 1)
                x = k.X[:, :, bass.ds(b * L + c * T, T)]
                dve.tensor_tensor(x, x, k.PS[:, 2:2 + KC, :T], ALU.add).then_inc(o_added, 1)
    fresh(nc, used)


NHEAD = 8
CM = 2048
NM = CM // P
LT = L // P
ROWS = T // HW
TAPS = 3


def two_layer(nc, ctx, k, b, src, w1, b1, w2, gate=None, first=None, last=None,
              beside=None, last_act=None, last_pool=None):
    H = ctx.enter_context(nc.sbuf_tensor(k.name("H"), [P, NM, T], F32))
    used = sems(nc, ctx, "hid_ready", "hid_done", "hid_gated", "hid_used", "sum_ready", "sum_used", "sum_added")
    hid_ready, hid_done, hid_gated, hid_used, sum_ready, sum_used, sum_added = used
    feed = hid_gated if gate is not None else hid_done
    credit = 0 if gate is not None else 3
    with nc.Block() as block:
        @block.tensor
        def _(pe):
            pe.sem_inc(sum_ready, 1)
            with pe.Fori(0, NT) as c:
                for s in range(NM + 2):
                    if s < NM:
                        pe.wait_ge(hid_done, c * NM + s + 1)
                        pe.sem_inc(k.turns, 1)
                        for i in range(KC):
                            mm = pe.matmul(k.PS[:, (s % 3), :T], w1(i, s), src(i, c),
                                           start=(i == 0), stop=(i == KC - 1))
                        mm.then_inc(hid_ready, 1)
                    if s >= 2:
                        m = s - 2
                        pe.wait_ge(feed, c * NM + m + 1 + credit)
                        pe.sem_inc(k.turns, 1)
                        if m == 0:
                            pe.wait_ge(sum_used, c + 1)
                            pe.sem_inc(k.turns, 1)
                            if first is not None:
                                first(pe, c)
                        for o in range(KC):
                            mm = pe.matmul(k.PS[:, 4 + o, :T], w2(m, o), H[:, m, :],
                                           start=(m == 0 and first is None), stop=(m == NM - 1))
                        mm.then_inc(hid_used if m < NM - 1 else sum_ready, 1)

        @block.scalar
        def _(act):
            act.sem_inc(hid_done, 3)
            with act.Fori(0, NT) as c:
                act.wait_ge(sum_ready, c + 1)
                act.sem_inc(k.turns, 1)
                for m in range(NM):
                    act.wait_ge(hid_ready, c * NM + m + 1)
                    act.sem_inc(k.turns, 1)
                    act.activation(H[:, m, :], k.PS[:, m % 3, :T], ACT.Gelu, bias=b1(m)).then_inc(hid_done, 1)
                if beside is not None:
                    act.wait_ge(sum_ready, c + 2)
                    act.sem_inc(k.turns, 1)
                    act.wait_ge(sum_added, c + 1)
                    act.sem_inc(k.turns, 1)
                    last_act(act, c).then_inc(sum_used, 1)

        if beside is not None:
            @block.gpsimd
            def _(pool):
                pool.sem_inc(sum_added, 1)
                with pool.Fori(0, NT) as c:
                    pool.wait_ge(sum_used, c + 2)
                    pool.sem_inc(k.turns, 1)
                    last_pool(pool, c).then_inc(sum_added, 1)

            @block.sync
            def _(sp):
                beside.move(sp)

        @block.vector
        def _(dve):
            if beside is not None:
                dve.sem_inc(sum_used, 1)
                beside.pack(dve)
                return
            dve.sem_inc(sum_used, 1)
            with dve.Fori(0, NT) as c:
                if gate is not None:
                    for m in range(NM):
                        dve.wait_ge(hid_done, c * NM + m + 1 + 3)
                        dve.sem_inc(k.turns, 1)
                        dve.tensor_tensor(H[:, m, :], H[:, m, :], gate(m, c), ALU.mult).then_inc(hid_gated, 1)
                dve.wait_ge(sum_ready, c + 2)
                dve.sem_inc(k.turns, 1)
                last(dve, c).then_inc(sum_used, 1)
    fresh(nc, used)


def linear_attention_block(nc, k, A, b):
    with ExitStack() as ctx:
        def sb(name, shape, dt=F32):
            return ctx.enter_context(nc.sbuf_tensor(k.name(name), shape, dt))

        vec = sb("vec1", [P, KC, 12])
        alpha = sb("alpha", [P, 2])
        SB = sb("SB", [P, KC, 2, 2])
        TT = sb("TT", [P, KC, L])
        sq = sb("sq1", [P, KC, 4])
        (BQ, DWB, BPROJ, BN, BFC2) = (0, 1, 2, 3, 11)
        w1 = sb("w_fc1", [P, KC, CM])
        w2 = sb("w_fc2", [P, NM, C])
        b1 = sb("b_fc1", [P, NM])
        (fc_loaded,) = sems(nc, ctx, "fc_loaded")

        with ExitStack() as own:
            def sbo(name, shape, dt=F32):
                return own.enter_context(nc.sbuf_tensor(k.name(name), shape, dt))

            w_qkv = sbo("w_qkv", [P, KC, 3 * C])
            w_pr = sbo("w_pr", [P, KC, C])
            bkv = sbo("bkv", [P, 2 * C])
            dw = sbo("dw", [P, KC, TAPS * TAPS])
            hmask = sbo("hmask", [P, P])
            QT = sbo("QT", [P, KC, L])
            KV = sbo("KV", [P, LT, 2 * C])
            CTX = sbo("CTX", [P, KC, P])
            IMG = sbo("IMG", [P, KC, HW + 2, HW + 2])
            stats = sbo("stats", [P, KC, NT, 6])
            mv = sbo("mv", [P, KC, 2])
            g = sbo("g", [P, KC, 4])
            used = sems(nc, own, "l1_loaded", "mv_done", "mg_ready", "vg_done", "root_done")
            l1_loaded, mv_done, mg_ready, vg_done, root_done = used
            with nc.Block() as block:
                @block.sync
                def _(sp):
                    n = 0
                    for dst, name in ((vec, "l1_vec"), (w_qkv, "l1_w_qkv"), (w_pr, "l1_w_proj"), (dw, "l1_dw"),
                                      (hmask, "c_head")):
                        sp.dma_start(dst[:], A[name]).then_inc(l1_loaded, 16)
                        n += 16
                    for dst, src in ((bkv[:], A["l1_bkv"].broadcast_to([P, 2 * C])),
                                     (alpha[:], A["l1_alpha"].broadcast_to([P, 2]))):
                        sp.dma_start(dst, src).then_inc(l1_loaded, 16)
                        n += 16
                    assert n == 112
                    for dst, name in ((w1, "l1_w_fc1"), (w2, "l1_w_fc2"), (b1, "l1_b_fc1")):
                        sp.dma_start(dst[:], A[name]).then_inc(fc_loaded, 16)
                    sp.wait_ge(l1_loaded, n)

                @block.vector
                def _(dve):
                    for i in range(KC):
                        for c in range(NT):
                            dve.bn_stats(stats[:, i, c, :], k.X[:, i, bass.ds(b * L + c * T, T)])
                    dve.drain()
                    for i in range(KC):
                        dve.bn_aggr(mv[:, i, :], stats[:, i, :, :].rearrange("p c s -> p (c s)"))
                    dve.drain()
                    dve.tensor_tensor(g[:, :, 0], mv[:, :, 0], mv[:, :, 0], ALU.mult)
                    dve.drain()
                    dve.tensor_tensor(mv[:, :, 1], mv[:, :, 1], g[:, :, 0], ALU.add).then_inc(mv_done, 1)
                    dve.wait_ge(mg_ready, 1)
                    gm = k.PS[:, 0, 0:2 * KC].rearrange("p (i s) -> p i s", i=KC)
                    dve.tensor_copy(g[:, :, 0:2], gm)
                    dve.drain()
                    dve.tensor_tensor(g[:, :, 2], g[:, :, 0], g[:, :, 0], ALU.mult)
                    dve.drain()
                    dve.tensor_tensor(g[:, :, 2], g[:, :, 1], g[:, :, 2], ALU.subtract).then_inc(vg_done, 1)
                    dve.wait_ge(root_done, 1)
                    dve.reciprocal(g[:, :, 3], g[:, :, 3])
                    dve.reciprocal(sq[:], sq[:])
                    dve.drain()
                    for i in range(KC):
                        dve.tensor_scalar(k.N[:, i, :], k.X[:, i, bass.ds(b * L, L)], g[:, i, 0:1], g[:, i, 3:4],
                                          ALU.subtract, ALU.mult)
                    for w in range(2):
                        bn = BN + 4 * w
                        dve.tensor_tensor(SB[:, :, w, 0], vec[:, :, bn], sq[:, :, w], ALU.mult)
                        dve.drain()
                        dve.tensor_tensor(SB[:, :, w, 1], vec[:, :, bn + 2], SB[:, :, w, 0], ALU.mult)
                        dve.drain()
                        dve.tensor_tensor(SB[:, :, w, 1], vec[:, :, bn + 1], SB[:, :, w, 1], ALU.subtract)
                        dve.tensor_scalar(SB[:, :, w, 0], SB[:, :, w, 0], alpha[:, w:w + 1], None, ALU.add)

                @block.tensor
                def _(pe):
                    pe.wait_ge(mv_done, 1)
                    pe.matmul(k.PS[:, 0, 0:2 * KC], k.group_w[:], mv[:].rearrange("p i s -> p (i s)"),
                              start=True, stop=True).then_inc(mg_ready, 1)

                @block.scalar
                def _(act):
                    act.wait_ge(l1_loaded, 112)
                    for w in range(2):
                        act.activation(sq[:, :, w], vec[:, :, BN + 4 * w + 3], ACT.Sqrt, bias=k.eps5[:])
                        act.activation(sq[:, :, 2 + w], vec[:, :, BN + 4 * w + 3], ACT.Sqrt, bias=k.eps5[:])
                    act.wait_ge(vg_done, 1)
                    act.activation(g[:, :, 3], g[:, :, 2], ACT.Sqrt, bias=k.eps5[:]).then_inc(root_done, 1)
            fresh(nc, used)

            used = sems(nc, own, "q_ready", "q_done", "kv_ready", "kv_added", "kv_done", "ctx_ready", "ctx_done",
                        "img_ready", "img_done", "img_zero", "conv1_done", "pr_ready", "tt_done")
            (q_ready, q_done, kv_ready, kv_added, kv_done, ctx_ready, ctx_done,
             img_ready, img_done, img_zero, conv1_done, pr_ready, tt_done) = used
            with nc.Block() as block:
                @block.tensor
                def _(pe):
                    for n in range(KC * NT):
                        m, c = n // NT, n % NT
                        if n >= 2:
                            pe.wait_ge(q_done, n - 1)
                        for i in range(KC):
                            mm = pe.matmul(k.PS[:, n % 2, :T], w_qkv[:, i, m * P:(m + 1) * P],
                                           k.N[:, i, c * T:(c + 1) * T], start=(i == 0), stop=(i == KC - 1))
                        mm.then_inc(q_ready, 1)
                    for t in range(LT + 1):
                        if t < LT:
                            if t >= 2:
                                pe.wait_ge(kv_added, t - 1)
                            for i in range(KC):
                                mm = pe.matmul(k.PS[:, 2 + t % 2, :], k.N[:, i, t * P:(t + 1) * P], w_qkv[:, i, C:3 * C],
                                               start=(i == 0), stop=(i == KC - 1))
                            mm.then_inc(kv_ready, 1)
                        if t >= 1:
                            pe.wait_ge(kv_done, t)
                            for i in range(KC):
                                mm = pe.matmul(k.PS[:, 4 + i, 0:P], KV[:, t - 1, i * P:(i + 1) * P],
                                               KV[:, t - 1, C + i * P:C + (i + 1) * P], start=(t == 1), stop=(t == LT))
                    mm.then_inc(ctx_ready, 1)
                    pe.wait_ge(ctx_done, 1)
                    pe.wait_ge(q_done, KC * NT)
                    for n in range(KC * NT):
                        i, c = n // NT, n % NT
                        if n >= 2:
                            pe.wait_ge(img_done, n - 1)
                        pe.matmul(k.PS[:, 6 + n % 2, :T], CTX[:, i, :], QT[:, i, c * T:(c + 1) * T],
                                  start=True, stop=True).then_inc(img_ready, 1)
                    pe.wait_ge(conv1_done, KC)
                    for n in range(KC * NT):
                        m, c = n // NT, n % NT
                        if n >= 2:
                            pe.wait_ge(tt_done, n - 1)
                        for i in range(KC):
                            mm = pe.matmul(k.PS[:, n % 2, :T], w_pr[:, i, m * P:(m + 1) * P],
                                           QT[:, i, c * T:(c + 1) * T], start=(i == 0), stop=(i == KC - 1))
                        mm.then_inc(pr_ready, 1)

                @block.scalar
                def _(act):
                    for n in range(KC * NT):
                        m, c = n // NT, n % NT
                        act.wait_ge(q_ready, n + 1)
                        act.activation(QT[:, m, c * T:(c + 1) * T], k.PS[:, n % 2, :T], ACT.Relu,
                                       bias=vec[:, m, BQ:BQ + 1]).then_inc(q_done, 1)
                    for t in range(LT):
                        act.wait_ge(kv_added, t + 1)
                        act.activation(KV[:, t, 0:C], KV[:, t, 0:C], ACT.Relu).then_inc(kv_done, 1)
                    act.wait_ge(img_zero, 1)
                    for n in range(KC * NT):
                        i, c = n // NT, n % NT
                        act.wait_ge(img_ready, n + 1)
                        act.activation(IMG[:, i, 1 + c * ROWS:1 + (c + 1) * ROWS, 1:1 + HW],
                                       k.PS[:, 6 + n % 2, :T].rearrange("p (r w) -> p r w", w=HW), ACT.Copy)\
                           .then_inc(img_done, 1)

                @block.gpsimd
                def _(pool):
                    pool.memset(IMG[:], 0.0).then_inc(img_zero, 1)

                @block.vector
                def _(dve):
                    for t in range(LT):
                        dve.wait_ge(kv_ready, t + 1)
                        dve.tensor_tensor(KV[:, t, :], k.PS[:, 2 + t % 2, :], bkv[:], ALU.add).then_inc(kv_added, 1)
                    dve.wait_ge(ctx_ready, 1)
                    for i in range(KC):
                        op = dve.tensor_tensor(CTX[:, i, :], k.PS[:, 4 + i, 0:P], hmask[:], ALU.mult)
                    op.then_inc(ctx_done, 1)
                    for i in range(KC):
                        dve.wait_ge(img_done, (i + 1) * NT)
                        acc = QT[:, i, :].rearrange("p (r w) -> p r w", w=HW)
                        for t in range(TAPS * TAPS):
                            y, x = t // TAPS, t % TAPS
                            win = IMG[:, i, y:y + HW, x:x + HW]
                            if t == 0:
                                dve.tensor_scalar(acc, win, dw[:, i, 0:1], vec[:, i, DWB:DWB + 1], ALU.mult, ALU.add)
                            else:
                                dve.drain()
                                op = dve.scalar_tensor_tensor(acc, win, dw[:, i, t:t + 1], acc, ALU.mult, ALU.add)
                        op.then_inc(conv1_done, 1)
                    for n in range(KC * NT):
                        m, c = n // NT, n % NT
                        dve.wait_ge(pr_ready, n + 1)
                        tt = TT[:, m, c * T:(c + 1) * T]
                        dve.scalar_tensor_tensor(tt, k.PS[:, n % 2, :T], vec[:, m, BPROJ:BPROJ + 1],
                                                 k.N[:, m, c * T:(c + 1) * T], ALU.add, ALU.add).then_inc(tt_done, 1)
                    dve.drain()
                    for m in range(KC):
                        dve.tensor_scalar(TT[:, m, :], TT[:, m, :], SB[:, m, 0, 0:1], SB[:, m, 0, 1:2], ALU.mult, ALU.add)
            fresh(nc, used)

        FF = sb("FF", [P, KC, L])
        EV = sb("EV", [P, KC, T])
        lists = EdgeLists(nc, ctx, k, A["edges"], b)
        with nc.Block() as block:
            @block.scalar
            def _(act):
                act.wait_ge(fc_loaded, 48)
                for o in range(KC):
                    act.activation(SB[:, o, 1, 1:2], vec[:, o, BFC2:BFC2 + 1], ACT.Identity, bias=SB[:, o, 1, 1:2],
                                   scale=SB[:, o, 1, 0:1])
                act.drain()
                for o in range(KC):
                    act.activation(FF[:, o, :], TT[:, o, :], ACT.Identity, bias=SB[:, o, 1, 1:2], scale=SB[:, o, 1, 0:1])
        fresh(nc, [fc_loaded])

        def empty(act, c):
            for o in range(KC):
                op = act.activation(EV[:, o, :], k.PS[:, 4 + o, :T], ACT.Copy, scale=SB[:, o, 1, 0:1])
            return op

        def add(pool, c):
            x = k.X[:, :, bass.ds(b * L + c * T, T)]
            pool.tensor_tensor(x, x, FF[:, :, bass.ds(c * T, T)], ALU.add)
            pool.drain()
            return pool.tensor_tensor(x, x, EV[:], ALU.add)

        two_layer(nc, ctx, k, b, lambda i, c: TT[:, i, bass.ds(c * T, T)], lambda i, m: w1[:, i, m * P:(m + 1) * P], lambda m: b1[:, m:m + 1],
                  lambda m, o: w2[:, m, o * P:(o + 1) * P], beside=lists, last_act=empty, last_pool=add)
        fresh(nc, lists.used)
H3 = 3 * C
FB = H3 // P
NH = 3
S = L // 3
ST = S // P
S2 = S // 2


def softmax_attention(nc, k, A, b):
    norm_image(nc, k, b, k.eps5)
    with ExitStack() as ctx:
        def sb(name, shape, dt=F32):
            return ctx.enter_context(nc.sbuf_tensor(k.name(name), shape, dt))

        w_e = sb("w_e", [P, FB, C + 1])
        b_e = sb("b_e", [P, FB])
        WW = sb("WW", [P, KC, C + 1])
        WO = sb("WO", [P, KC, C])
        c_o = sb("c_o", [P, KC])
        w_o = sb("w_o2", [P, FB, C])
        b_o = sb("b_o2", [P, KC])
        XV = sb("XV", [P, ST, C])
        R = sb("R", [P, KC, S])
        PR = sb("PR", [P, 2, S])
        PT = sb("PT", [P, ST, S])
        mx = sb("mx", [P, 2, 4])
        used = sems(nc, ctx, "l2_loaded", "xv_ready", "xv_done")
        l2_loaded, xv_ready, xv_done = used
        with nc.Block() as block:
            @block.sync
            def _(sp):
                sp.dma_start(w_o[:], A["l2_w_out"]).then_inc(l2_loaded, 16)
                sp.dma_start(b_o[:], A["l2_b_out"]).then_inc(l2_loaded, 16)
                sp.wait_ge(l2_loaded, 32)

            @block.tensor
            def _(pe):
                for t in range(ST):
                    if t >= 2:
                        pe.wait_ge(xv_done, t - 1)
                    for i in range(KC):
                        mm = pe.transpose(k.PS[:, t % 2, i * P:(i + 1) * P], k.N[:, i, 2 * S + t * P:2 * S + (t + 1) * P],
                                          k.ident[:])
                    mm.then_inc(xv_ready, 1)

            @block.vector
            def _(dve):
                for t in range(ST):
                    dve.wait_ge(xv_ready, t + 1)
                    dve.tensor_copy(XV[:, t, :], k.PS[:, t % 2, 0:C]).then_inc(xv_done, 1)
        fresh(nc, used)

        used = sems(nc, ctx, "head_loaded", "e_placed", "ww_ready", "ww_done", "r_ready", "r_done", "s_ready", "max_done",
                    "exp_done", "p_done", "pt_ready", "pt_done", "av_ready", "av_done", "out_ready")
        (head_loaded, e_placed, ww_ready, ww_done, r_ready, r_done, s_ready, max_done,
         exp_done, p_done, pt_ready, pt_done, av_ready, av_done, out_ready) = used
        with nc.Fori(0, NH) as h:
            with nc.Block() as block:
                @block.sync
                def _(sp):
                    sp.dma_start(w_e[:, :, 0:C], A["l2_w_e"][bass.ds(h, 1)].rearrange("o p i n -> (o p) i n")).then_inc(head_loaded, 16)
                    sp.dma_start(b_e[:], A["l2_b_e"][bass.ds(h, 1)].rearrange("o p i -> (o p) i")).then_inc(head_loaded, 16)
                    sp.wait_ge(head_loaded, 32)

                @block.tensor
                def _(pe):
                    pe.wait_ge(head_loaded, 32)
                    pe.wait_ge(e_placed, 1)
                    for i in range(KC):
                        for f in range(FB):
                            pe.matmul(k.PS[:, i, 0:C + 1], w_e[:, f, i * P:(i + 1) * P], w_e[:, f, :],
                                      start=(f == 0), stop=(f == FB - 1))
                        for f in range(FB):
                            pe.matmul(k.PS[:, 2 + i, 0:C], w_e[:, f, i * P:(i + 1) * P], w_o[:, f, :],
                                      start=(f == 0), stop=(f == FB - 1))
                        for f in range(FB):
                            mm = pe.matmul(k.PS[:, 6, i:i + 1], w_o[:, f, i * P:(i + 1) * P], w_e[:, f, C:C + 1],
                                           start=(f == 0), stop=(f == FB - 1))
                    mm.then_inc(ww_ready, 1)
                    pe.wait_ge(ww_done, 1)
                    for n in range(KC * 2):
                        o, c = n // 2, n % 2
                        for i in range(KC):
                            mm = pe.matmul(k.PS[:, 4 + n, :S2], WW[:, i, o * P:(o + 1) * P],
                                           k.N[:, i, c * S2:(c + 1) * S2], start=(i == 0), stop=(i == KC - 1))
                        mm.then_inc(r_ready, 1)
                    pe.wait_ge(r_done, KC * 2)
                    for t in range(ST + 1):
                        if t < ST:
                            if t >= 2:
                                pe.wait_ge(exp_done, t - 1)
                            for c in range(2):
                                for i in range(KC):
                                    mm = pe.matmul(k.PS[:, 2 * (t % 2) + c, :S2], R[:, i, t * P:(t + 1) * P],
                                                   k.N[:, i, S + c * S2:S + (c + 1) * S2],
                                                   start=(i == 0), stop=(i == KC - 1))
                            mm.then_inc(s_ready, 1)
                        if t >= 1:
                            v = t - 1
                            pe.wait_ge(p_done, v + 1)
                            for g in range(2):
                                if v >= 1:
                                    pe.wait_ge(pt_done, 2 * (v - 1) + g + 1)
                                for a in range(3):
                                    kt = 3 * g + a
                                    mm = pe.transpose(k.PS[:, 4 + g, a * P:(a + 1) * P], PR[:, v % 2, kt * P:(kt + 1) * P],
                                                      k.ident[:])
                                mm.then_inc(pt_ready, 1)
                    pe.wait_ge(pt_done, 2 * ST)
                    for n in range(KC * 2):
                        o, c = n // 2, n % 2
                        for kt in range(ST):
                            mm = pe.matmul(k.PS[:, n, :S2], XV[:, kt, o * P:(o + 1) * P],
                                           PT[:, kt, c * S2:(c + 1) * S2], start=(kt == 0), stop=(kt == ST - 1))
                        mm.then_inc(av_ready, 1)
                    pe.wait_ge(av_done, KC * 2)
                    for n in range(KC * 2):
                        o, c = n // 2, n % 2
                        for i in range(KC):
                            mm = pe.matmul(k.PS[:, 4 + n, :S2], WO[:, i, o * P:(o + 1) * P],
                                           R[:, i, c * S2:(c + 1) * S2], start=(i == 0), stop=(i == KC - 1))
                        mm.then_inc(out_ready, 1)

                @block.scalar
                def _(act):
                    for t in range(ST):
                        act.wait_ge(max_done, t + 1)
                        act.activation(PR[:, t % 2, :].rearrange("p (c n) -> p c n", c=2),
                                       k.PS[:, 2 * (t % 2):2 * (t % 2) + 2, :S2], ACT.Exp, scale=C ** -0.5,
                                       bias=mx[:, t % 2, 1:2], accum_out=mx[:, t % 2, 2:3]).then_inc(exp_done, 1)
                        for g in range(2):
                            act.wait_ge(pt_ready, 2 * t + g + 1)
                            act.activation(PT[:, 3 * g:3 * g + 3, t * P:(t + 1) * P],
                                           k.PS[:, 4 + g, 0:3 * P].rearrange("p (a n) -> p a n", a=3), ACT.Copy)\
                               .then_inc(pt_done, 1)

                @block.vector
                def _(dve):
                    dve.wait_ge(head_loaded, 32)
                    dve.tensor_copy(w_e[:, :, C], b_e[:]).then_inc(e_placed, 1)
                    dve.wait_ge(ww_ready, 1)
                    dve.tensor_copy(WW[:], k.PS[:, 0:KC, 0:C + 1])
                    dve.tensor_copy(WO[:], k.PS[:, 2:2 + KC, 0:C])
                    dve.tensor_tensor(c_o[:], b_o[:], k.PS[:, 6, 0:KC], ALU.add)
                    dve.drain().then_inc(ww_done, 1)
                    for n in range(KC * 2):
                        o, c = n // 2, n % 2
                        dve.wait_ge(r_ready, n + 1)
                        dve.tensor_scalar(R[:, o, c * S2:(c + 1) * S2], k.PS[:, 4 + n, :S2], WW[:, o, C:C + 1], None,
                                          ALU.add).then_inc(r_done, 1)
                    for t in range(ST):
                        m = mx[:, t % 2, :]
                        dve.wait_ge(s_ready, t + 1)
                        dve.tensor_reduce(m[:, 0:1], k.PS[:, 2 * (t % 2):2 * (t % 2) + 2, :S2], AX.XY, ALU.max)
                        dve.drain()
                        dve.tensor_scalar(m[:, 1:2], m[:, 0:1], -(C ** -0.5), None, ALU.mult).then_inc(max_done, 1)
                        dve.wait_ge(exp_done, t + 1)
                        dve.reciprocal(m[:, 3:4], m[:, 2:3])
                        dve.drain()
                        dve.tensor_scalar(PR[:, t % 2, :], PR[:, t % 2, :], m[:, 3:4], None, ALU.mult).then_inc(p_done, 1)
                    for n in range(KC * 2):
                        o, c = n // 2, n % 2
                        dve.wait_ge(av_ready, n + 1)
                        dve.tensor_copy(R[:, o, c * S2:(c + 1) * S2], k.PS[:, n, :S2]).then_inc(av_done, 1)
                    for n in range(KC * 2):
                        o, c = n // 2, n % 2
                        dve.wait_ge(out_ready, n + 1)
                        n_in = k.N[:, o, bass.ds(h * S + c * S2, S2)]
                        y = PR[:, 0, (n % 2) * S2:(n % 2 + 1) * S2]
                        dve.scalar_tensor_tensor(y, k.PS[:, 4 + n, :S2], c_o[:, o:o + 1], n_in, ALU.add, ALU.add)
                        dve.drain()
                        x = k.X[:, o, bass.ds(b * L + h * S + c * S2, S2)]
                        dve.tensor_tensor(x, x, y, ALU.add)
            fresh(nc, used)


E2 = 4
HE = E2 * E2
F2 = 2 * C
TM = M // P
EDGES = 1048576
EC = EDGES // P
EH = EC // 2
SHIFT_BITS = 13
ROW = E2 + HE
TOP2 = 2
WINDOW = 60.0
GC = 8
HC_ = 16
NU = 2
BW = 1024
BH = BW // NU
NBLK = EC // BW
HI = TM // 2
SLOPE = 0.2


def front(dve, V, D, D2, MV, width):
    cur, nxt = D, D2
    bits = width.bit_length() - 1
    for s in range(bits):
        w = width - (1 << s)
        dve.tensor_scalar(MV[:], cur[:], 1 << s, None, ALU.bitwise_and)
        dve.drain()
        if s < bits - 1:
            dve.scalar_tensor_tensor(nxt[:], MV[:], 0.0, cur[:], ALU.is_equal, ALU.mult)
            dve.drain()
            dve.copy_predicated(nxt[:, 0:w], MV[:, 1 << s:width], cur[:, 1 << s:width])
        dve.copy_predicated(V[:, 0:w], MV[:, 1 << s:width], V[:, 1 << s:width])
        dve.drain()
        cur, nxt = nxt, cur


class EdgeLists:

    def __init__(self, nc, ctx, k, edges, h):
        def sb(name, shape, dt=I32):
            return ctx.enter_context(nc.sbuf_tensor(k.name(name), shape, dt))

        self.k, self.edges, self.h = k, edges, h
        self.V, self.DSTS = sb("V", [P, EH]), sb("dsts", [P, EH])
        self.D, self.D2, self.MV = (sb(n, [P, EH], I16) for n in ("D", "D2", "MV"))
        self.used = sems(nc, ctx, "edges_in", "packed", "edges_out")
        self.edges_in, self.packed, self.edges_out = self.used

    def move(self, sp):
        for dst, w in ((self.V, 0), (self.DSTS, 1)):
            src = self.edges[w].rearrange("(p c) -> p c", p=P)[:, bass.ds(self.h * EH, EH)]
            sp.dma_start(dst[:], src).then_inc(self.edges_in, 16)
        sp.wait_ge(self.packed, 1)
        sp.dma_start(self.k.edges_dram[:, bass.ds(self.h * EH, EH)], self.V[:]).then_inc(self.edges_out, 16)
        sp.wait_ge(self.edges_out, 16)

    def pack(self, dve):
        V, DSTS, D, D2, MV = self.V, self.DSTS, self.D, self.D2, self.MV
        dve.wait_ge(self.edges_in, 32)
        dve.tensor_scalar(MV[:], DSTS[:], float(M), None, ALU.is_ge)
        dve.tensor_scalar(V[:], V[:], float(M - 1), None, ALU.min)
        dve.drain()
        dve.tensor_tensor_scan(D[:], MV[:], MV[:], 0.0, ALU.add, ALU.max)
        dve.tensor_scalar(DSTS[:], DSTS[:], SHIFT_BITS, None, ALU.arith_shift_left)
        dve.drain()
        dve.tensor_tensor(V[:], V[:], DSTS[:], ALU.bitwise_or)
        dve.tensor_scalar(self.k.cnt[:, bass.ds(self.h, 1)], D[:, EH - 1:EH], -1.0, float(EH), ALU.mult, ALU.add)
        dve.drain()
        dve.scalar_tensor_tensor(D[:], MV[:], 0.0, D[:], ALU.is_equal, ALU.mult)
        dve.drain()
        front(dve, V, D, D2, MV, EH)
        dve.sem_inc(self.packed, 1)


def split_block(nc, k, blk, held, g):
    with ExitStack() as ctx:
        def sb(name, shape, dt=I32):
            return ctx.enter_context(nc.sbuf_tensor(k.name(name), shape, dt))

        VB = sb("VB", [P, BW])
        S_, T_, X_ = (sb(n, [P, BW]) for n in ("S_", "T_", "X_"))
        LIVE, LAST, LOF, HIF, CH_ = (sb(n, [P, BW], F32) for n in ("LIVE", "LAST", "LOF", "HIFb", "CHb"))
        LOB, HIB = (sb(n, [P, BW], BF16) for n in ("LOB", "HIB"))
        OLB = sb("OLB", [P, NU, P, HC_], BF16)
        OHB = sb("OHB", [P, NU, TM, HC_], BF16)
        D, D2, MV = (sb(n, [P, BW], I16) for n in ("Db", "D2b", "MVb"))
        IDX = sb("IDX", [P, 2, BW])
        DIG = sb("DIG", [P, 2, BW], F32)
        lim = sb("lim", [P, 3], F32)
        used = sems(nc, ctx, "block_in", "hot_done", "hot_used", "count_done", "count_row", "lists_done", "lists_out")
        block_in, hot_done, hot_used, count_done, count_row, lists_done, lists_out = used

        def digits(dve, V, lo, hi):
            dve.tensor_scalar(T_[:], V[:], SHIFT_BITS, None, ALU.arith_shift_right)
            dve.drain()
            dve.tensor_scalar(X_[:], T_[:], P - 1, None, ALU.bitwise_and)
            dve.drain()
            dve.tensor_copy(lo, X_[:])
            dve.drain()
            dve.tensor_scalar(X_[:], T_[:], 7, None, ALU.arith_shift_right)
            dve.drain()
            dve.tensor_copy(hi, X_[:])
            dve.drain()

        with nc.Block() as block:
            @block.sync
            def _(sp):
                with sp.If(held > 0):
                    for h in range(NU):
                        sp.dma_start(VB[:, h * BH:(h + 1) * BH], k.edges_dram[:, bass.ds(blk * BH + h * EH, BH)])\
                          .then_inc(block_in, 16)
                    sp.wait_ge(lists_done, 1)
                    for w in range(2):
                        sp.dma_start(k.idx_dram[w][:, bass.ds(blk * BW, BW)], IDX[:, w, :]).then_inc(lists_out, 16)
                        sp.dma_start(k.dig_dram[w][:, bass.ds(blk * BW, BW)], DIG[:, w, :]).then_inc(lists_out, 16)
                    sp.wait_ge(lists_out, 64)

            @block.vector
            def _(dve):
                with dve.If(held > 0):
                    dve.wait_ge(block_in, 16 * NU)
                    dve.tensor_copy(lim[:, 0:NU], g.left[:])
                    dve.tensor_scalar(S_[:], VB[:], (1 << SHIFT_BITS) - 1, None, ALU.bitwise_and)
                    dve.drain()
                    for h in range(NU):
                        dve.tensor_scalar(LIVE[:, h * BH:(h + 1) * BH], g.iota_b[:, 0:BH], lim[:, h:h + 1], None, ALU.is_lt)
                    dve.tensor_scalar(g.left[:], g.left[:], -float(BH), None, ALU.add)
                    dve.tensor_copy(CH_[:], S_[:])
                    dve.drain()
                    dve.scalar_tensor_tensor(LAST[:], CH_[:], float(M - 1), LIVE[:], ALU.is_equal, ALU.mult)
                    dve.drain()
                    dve.tensor_tensor(LIVE[:], LIVE[:], LAST[:], ALU.subtract)
                    digits(dve, VB, LOF[:], HIF[:])
                    dve.scalar_tensor_tensor(HIF[:], HIF[:], 1.0, LAST[:], ALU.add, ALU.mult)
                    dve.tensor_copy(LOB[:], LOF[:])
                    dve.drain()
                    dve.tensor_scalar(HIB[:], HIF[:], -1.0, None, ALU.add)
                    dve.drain()
                    with dve.Fori(0, BH // HC_) as i:
                        with dve.If(held > i * HC_):
                            for u in range(NU):
                                at = bass.ds(i * HC_ + u * BH, HC_)
                                dve.wait_ge(hot_used, i * NU + u + 1)
                                dve.sem_inc(k.turns, 1)
                                lo = LOB[:, at].rearrange("p (o c) -> p o c", o=1).broadcast_to([P, P, HC_])
                                hi = HIB[:, at].rearrange("p (o c) -> p o c", o=1).broadcast_to([P, TM, HC_])
                                dve.tensor_tensor(OLB[:, u, :, :], g.iota_h[:], lo, ALU.is_equal)
                                dve.tensor_tensor(OHB[:, u, :, :], g.iota_h[:, 0:TM, :], hi, ALU.is_equal).then_inc(hot_done, 1)
                    dve.tensor_scalar(MV[:], LIVE[:], -1.0, 1.0, ALU.mult, ALU.add)
                    dve.drain()
                    dve.tensor_tensor_scan(D[:], MV[:], MV[:], 0.0, ALU.add, ALU.max)
                    dve.drain()
                    dve.tensor_scalar(lim[:, NU:NU + 1], D[:, BW - 1:BW], -1.0, float(BW), ALU.mult, ALU.add).then_inc(count_done, 1)
                    dve.scalar_tensor_tensor(D2[:], MV[:], 0.0, D[:], ALU.is_equal, ALU.mult)
                    dve.drain()
                    front(dve, VB, D2, D, MV, BW)
                    dve.tensor_scalar(IDX[:, 0, :], VB[:], (1 << SHIFT_BITS) - 1, None, ALU.bitwise_and)
                    dve.tensor_scalar(IDX[:, 1, :], VB[:], SHIFT_BITS, None, ALU.arith_shift_right)
                    dve.tensor_scalar(LIVE[:], g.iota_b[:], lim[:, NU:NU + 1], None, ALU.is_lt)
                    digits(dve, VB, DIG[:, 0, :], HIF[:])
                    dve.tensor_scalar(IDX[:, 1, :], IDX[:, 1, :], float(M - 1), None, ALU.min)
                    dve.scalar_tensor_tensor(HIF[:], HIF[:], 1.0, LIVE[:], ALU.add, ALU.mult)
                    dve.drain()
                    dve.tensor_scalar(DIG[:, 1, :], HIF[:], -1.0, None, ALU.add)
                    dve.wait_ge(count_row, 1)
                    dve.tensor_reduce(g.most[:, 0:1], k.PS[0:1, 1, 0:P], AX.X, ALU.max)
                    dve.drain()
                    dve.tensor_copy(g.most_b[:, bass.ds(blk, 1)], g.most[:])
                    dve.tensor_tensor(g.HIST[:], g.HIST[:], k.PS[:, 0, 0:TM], ALU.add).then_inc(lists_done, 1)

            @block.tensor
            def _(pe):
                with pe.If(held > 0):
                    pe.sem_inc(hot_used, NU)
                    pe.matmul(k.PS[:, 0, 0:TM], k.zeros[:, 0:P], k.zeros[:, 0:TM], start=True, stop=False)
                    with pe.Fori(0, BH // HC_) as i:
                        with pe.If(held > i * HC_):
                            for u in range(NU):
                                pe.wait_ge(hot_done, i * NU + u + 1)
                                pe.sem_inc(k.turns, 1)
                                for c in range(HC_):
                                    mm = pe.matmul(k.PS[:, 0, 0:TM], OLB[:, u, :, c], OHB[:, u, :, c], start=False, stop=False)
                                mm.then_inc(hot_used, 1)
                    pe.matmul(k.PS[:, 0, 0:TM], k.zeros[:, 0:P], k.zeros[:, 0:TM], start=False, stop=True)
                    pe.wait_ge(count_done, 1)
                    pe.matmul(k.PS[0:1, 1, 0:P], lim[:, NU:NU + 1], k.ident[:], start=True, stop=True).then_inc(count_row, 1)
        fresh(nc, used)


def split_edges(nc, k, A, g):
    with ExitStack() as own:
        g.iota_b = own.enter_context(nc.sbuf_tensor("iota_b", [P, BW], F32))
        g.iota_h = own.enter_context(nc.sbuf_tensor("iota_h", [P, P, HC_], BF16))
        g.left = own.enter_context(nc.sbuf_tensor("left", [P, NU], F32))
        g.ahead = own.enter_context(nc.sbuf_tensor("ahead", [1, NBLK], F32))
        used = sems(nc, own, "iota_in", "cnt_row")
        iota_in, cnt_row = used
        with nc.Block() as block:
            @block.sync
            def _(sp):
                sp.dma_start(g.iota_b[:], A["c_iota"].broadcast_to([P, BW])).then_inc(iota_in, 16)

            @block.tensor
            def _(pe):
                for h in range(NU):
                    mm = pe.matmul(k.PS[0:1, 0, h * P:(h + 1) * P], k.cnt[:, h:h + 1], k.ident[:], start=True, stop=True)
                mm.then_inc(cnt_row, 1)

            @block.vector
            def _(dve):
                dve.memset(g.HIST[:], 0.0)
                dve.tensor_copy(g.left[:], k.cnt[:])
                dve.wait_ge(cnt_row, 1)
                dve.tensor_reduce(g.most[:], k.PS[0:1, 0, 0:NU * P], AX.X, ALU.max)
                dve.wait_ge(iota_in, 16)
                dve.drain()
                dve.tensor_copy(g.iota_h[:], g.iota_b[:, 0:P].rearrange("p (n o) -> p n o", o=1).broadcast_to([P, P, HC_]))
                dve.tensor_scalar(g.ahead[:], g.iota_b[0:1, 0:NBLK], -float(BH), g.most[:], ALU.mult, ALU.add)
                dve.drain()
                dve.tensor_scalar(g.ahead[:], g.ahead[:], 0.0, float(BH), ALU.max, ALU.min)
                dve.drain()
                dve.tensor_copy(g.most_b[:], g.ahead[:])
        fresh(nc, used)
        with nc.Fori(0, NBLK) as blk:
            held = nc.values_load(g.most_b[0:1, bass.ds(blk, 1)], min_val=0, max_val=BH)
            split_block(nc, k, blk, held, g)


def graph_features(nc, k, A, b, g):
    norm_image(nc, k, b, k.eps5)
    with ExitStack() as ctx:
        tmp = ctx.enter_context(nc.sbuf_tensor(k.name("tmp_h"), [P, 2, LT, HE], F32))
        used = sems(nc, ctx, "h_ready")
        with nc.Block() as block:
            @block.tensor
            def _(pe):
                for t in range(LT):
                    for i in range(KC):
                        mm = pe.matmul(k.PS[:, 0, t * HE:(t + 1) * HE], k.N[:, i, t * P:(t + 1) * P], g.w_gat[:, i, :],
                                       start=(i == 0), stop=(i == KC - 1))
                mm.then_inc(used[0], 1)

            @block.scalar
            def _(act):
                act.activation(g.NN[:, :, bass.ds(b * L, L)], k.N[:], ACT.Copy)

            @block.vector
            def _(dve):
                dve.wait_ge(used[0], 1)
                h = k.PS[:, 0, 0:LT * HE].rearrange("p (t f) -> p t f", f=HE)
                dve.tensor_copy(g.GS[:, bass.ds(b * LT, LT), E2:ROW], h)
                for w in range(2):
                    att = g.att[:, w, :].rearrange("p (o f) -> p o f", o=1).broadcast_to([P, LT, HE])
                    dve.tensor_tensor(tmp[:, w, :, :], h, att, ALU.mult)
                dve.drain()
                for w in range(2):
                    dst = (g.GS if w == 0 else g.GD)[:, bass.ds(b * LT, LT), 0:E2]
                    dve.tensor_reduce(dst, tmp[:, w, :, :].rearrange("p t (h e) -> p t h e", e=E2), AX.X, ALU.add)
        fresh(nc, used)


def graph_mixture(nc, k, A):
    with ExitStack() as top:
        g = Core()

        def keep(name, shape, dt=F32):
            return top.enter_context(nc.sbuf_tensor(k.name(name), shape, dt))

        g.most = keep("most", [1, 1])
        g.most_b = keep("most_b", [1, NBLK], I32)
        g.HIST = keep("HIST", [P, TM])
        g.NN = keep("NN", [P, KC, M])
        g.w1 = keep("w1g", [P, KC, E2 * F2])
        g.w2 = keep("w2g", [P, NM, C])
        g.b1 = keep("b1g", [P, NM])
        g.b2 = keep("b2g", [E2, C])
        (g.w_loaded,) = sems(nc, top, "w_loaded")
        with nc.Block() as block:
            @block.sync
            def _(sp):
                for dst, name in ((g.w1, "l2_w1"), (g.w2, "l2_w2"), (g.b1, "l2_b1"), (g.b2, "l2_b2")):
                    sp.dma_start(dst[:], A[name]).then_inc(g.w_loaded, 16)
        split_edges(nc, k, A, g)
        with ExitStack() as own:
            def sbo(name, shape, dt=F32):
                return own.enter_context(nc.sbuf_tensor(k.name(name), shape, dt))

            g.GS = sbo("GS", [P, TM, ROW])
            g.GD = sbo("GD", [P, TM, 2 * E2])
            g.w_gat = sbo("w_gat", [P, KC, HE])
            g.att = sbo("att", [P, 2, HE])
            g.rows = sbo("g_rows", [P, 3, HE])
            g.iota = sbo("g_iota", [P, P])
            g.SELF = sbo("SELF", [P, TM, E2])
            used = sems(nc, own, "g_loaded")
            with nc.Block() as block:
                @block.sync
                def _(sp):
                    sp.dma_start(g.w_gat[:], A["l2_w_gat"]).then_inc(used[0], 16)
                    sp.dma_start(g.att[:], A["l2_att"].broadcast_to([P, 2, HE])).then_inc(used[0], 16)
                    sp.dma_start(g.rows[:], A["l2_g_rows"].broadcast_to([P, 3, HE])).then_inc(used[0], 16)
                    sp.dma_start(g.iota[:], A["c_iota"][:, 0:P].broadcast_to([P, P])).then_inc(used[0], 16)
                    sp.wait_ge(used[0], 64)
            fresh(nc, used)
            with nc.Fori(0, NB) as b:
                graph_features(nc, k, A, b, g)
            graph_tables(nc, k, g)
            edge_sums(nc, k, g)
            gates(nc, k, g)
        with nc.Fori(0, NB) as b:
            gated_experts(nc, k, A, b, g)


def graph_tables(nc, k, g):
    with ExitStack() as ctx:
        def sb(name, shape, dt=F32):
            return ctx.enter_context(nc.sbuf_tensor(k.name(name), shape, dt))

        pm = sb("pm", [P, 2, E2])
        U = sb("U", [P, TM, E2])
        used = sems(nc, ctx, "part_max", "all_max", "table_done", "self_done", "tables_out")
        part_max, all_max, table_done, self_done, tables_out = used

        def leaky(dve, x):
            dve.scalar_tensor_tensor(x, x, SLOPE, x, ALU.mult, ALU.max)

        with nc.Block() as block:
            @block.vector
            def _(dve):
                dve.tensor_reduce(pm[:, 0, :], g.GS[:, :, 0:E2].rearrange("p t h -> p h t"), AX.X, ALU.max)\
                   .then_inc(part_max, 1)
                dve.tensor_tensor(g.SELF[:], g.GS[:, :, 0:E2], g.GD[:, :, 0:E2], ALU.add)
                dve.drain()
                leaky(dve, g.SELF[:])
                dve.wait_ge(all_max, 1)
                dve.tensor_tensor(U[:], g.GD[:, :, 0:E2],
                                  pm[:, 1, :].rearrange("p (o h) -> p o h", o=1).broadcast_to([P, TM, E2]), ALU.add)
                dve.drain()
                leaky(dve, U[:])
                dve.drain()
                dve.scalar_tensor_tensor(U[:], U[:], -WINDOW, g.SELF[:], ALU.add, ALU.max)
                dve.drain()
                dve.tensor_scalar(g.GD[:, :, E2:2 * E2], U[:], -1.0, None, ALU.mult)
                dve.tensor_tensor(g.SELF[:], g.SELF[:], U[:], ALU.subtract).then_inc(table_done, 1)

            @block.gpsimd
            def _(pool):
                pool.wait_ge(part_max, 1)
                pool.partition_all_reduce(pm[:, 1, :], pm[:, 0, :], P, bass.bass_isa.ReduceOp.max).then_inc(all_max, 1)

            @block.scalar
            def _(act):
                act.wait_ge(table_done, 1)
                act.activation(g.SELF[:], g.SELF[:], ACT.Exp).then_inc(self_done, 1)

            @block.sync
            def _(sp):
                sp.wait_ge(table_done, 1)
                sp.dma_start(k.src_dram.rearrange("(t p) f -> p t f", p=P), g.GS[:]).then_inc(tables_out, 16)
                sp.dma_start(k.dst_dram.rearrange("(t p) f -> p t f", p=P), g.GD[:]).then_inc(tables_out, 16)
                sp.wait_ge(tables_out, 32)
        fresh(nc, used)


def edge_sums(nc, k, g):
    def zeroes(start):
        with nc.Block() as block:
            @block.tensor
            def _(pe):
                for n in range(2):
                    pe.matmul(k.PS[:, 4 + n, 0:HI * ROW], k.zeros[:, 0:P], k.zeros[:, 0:HI * ROW], start=start, stop=not start)

    zeroes(True)
    with nc.Fori(0, NBLK) as blk:
        longest = nc.values_load(g.most_b[0:1, bass.ds(blk, 1)], min_val=0, max_val=BW)
        with nc.If(longest > 0):
            block_sums(nc, k, g, blk, longest)
    zeroes(False)


def block_sums(nc, k, g, blk, longest):
    with ExitStack() as ctx:
        def sb(name, shape, dt=F32):
            return ctx.enter_context(nc.sbuf_tensor(k.name(name), shape, dt))

        IX = sb("IX", [P, NU, 2, GC], I32)
        DG = sb("DG", [P, NU, 2, GC])
        RS = sb("RS", [P, NU, GC * ROW])
        RD = sb("RD", [P, NU, GC * 2 * E2])
        W = sb("Wt", [P, NU, GC, E2])
        VL = sb("VL", [P, NU, GC, ROW])
        OL = sb("OL", [P, NU, GC, P])
        OH = sb("OHI", [P, NU, GC, TM])
        R = sb("Rr", [P, NU, GC, TM, ROW])
        used = sems(nc, ctx, "ix_in0", "ix_in1", "dg_in0", "dg_in1", "e_sum", "e_exp", "r_done", "added")
        ix_in0, ix_in1, dg_in0, dg_in1, e_sum, e_exp, r_done, added = used
        ix_in, dg_in = (ix_in0, ix_in1), (dg_in0, dg_in1)
        STEP = NU * GC
        rs_in, rd_in = k.rs_in, k.rd_in

        def hot(ap, n):
            return ap.rearrange("p (c o) -> p c o", o=1).broadcast_to([P, GC, n])

        with nc.Block() as block:
            @block.sync
            def _(sp):
                with sp.Fori(0, BW // STEP) as i:
                    with sp.If(longest > i * STEP):
                        for u in range(NU):
                            sp.wait_ge(r_done, i * NU + u + 1)
                            sp.sem_inc(k.turns, 1)
                            for w in range(2):
                                at = bass.ds(blk * BW + i * STEP + u * GC, GC)
                                sp.dma_start(IX[:, u, w, :], k.idx_dram[w][:, at]).then_inc(ix_in[u], 16)
                                sp.dma_start(DG[:, u, w, :], k.dig_dram[w][:, at]).then_inc(dg_in[u], 16)

            @block.gpsimd
            def _(pool):
                with pool.Fori(0, BW // STEP) as i:
                    with pool.If(longest > i * STEP):
                        for u in range(NU):
                            pool.wait_ge(ix_in[u], i * 32 + 32)
                            pool.sem_inc(k.turns, 1)
                            for c in range(GC):
                                pool.indirect_dma_start(
                                    out=RS[:, u, c * ROW:(c + 1) * ROW], out_offset=None, in_=k.src_dram,
                                    in_offset=bass.IndirectOffsetOnAxis(ap=IX[:, u, 0, c:c + 1], axis=0),
                                    bounds_check=M - 1, oob_is_err=False).then_inc(rs_in[u], 16)
                                pool.indirect_dma_start(
                                    out=RD[:, u, c * 2 * E2:(c + 1) * 2 * E2], out_offset=None, in_=k.dst_dram,
                                    in_offset=bass.IndirectOffsetOnAxis(ap=IX[:, u, 1, c:c + 1], axis=0),
                                    bounds_check=M - 1, oob_is_err=False).then_inc(rd_in[u], 16)

            def weigh(dve, i, u):
                rs = RS[:, u, :].rearrange("p (c f) -> p c f", f=ROW)
                rd = RD[:, u, :].rearrange("p (c f) -> p c f", f=2 * E2)
                w = W[:, u, :, :]
                dve.wait_ge(dg_in[u], i * 32 + 32)
                dve.sem_inc(k.turns, 1)
                dve.wait_ge(added, i * NU + u + 1)
                dve.sem_inc(k.turns, 1)
                dve.tensor_tensor(OL[:, u, :, :], g.iota[:].rearrange("p (o n) -> p o n", o=1).broadcast_to([P, GC, P]),
                                  hot(DG[:, u, 0, :], P), ALU.is_equal)
                dve.tensor_tensor(OH[:, u, :, :], g.iota[:, 0:TM].rearrange("p (o n) -> p o n", o=1)
                                  .broadcast_to([P, GC, TM]), hot(DG[:, u, 1, :], TM), ALU.is_equal)
                dve.wait_ge(rs_in[u], i * (16 * GC) + 16 * GC)
                dve.sem_inc(k.turns, 1)
                dve.wait_ge(rd_in[u], i * (16 * GC) + 16 * GC)
                dve.sem_inc(k.turns, 1)
                dve.tensor_tensor(w, rs[:, :, 0:E2], rd[:, :, 0:E2], ALU.add)
                dve.drain()
                dve.scalar_tensor_tensor(w, w, SLOPE, w, ALU.mult, ALU.max)
                dve.drain()
                dve.tensor_tensor(w, w, rd[:, :, E2:2 * E2], ALU.add).then_inc(e_sum, 1)
                dve.wait_ge(e_exp, i * NU + u + 1)
                dve.sem_inc(k.turns, 1)
                vl = VL[:, u, :, :]
                dve.tensor_copy(vl[:, :, 0:E2], w)
                for c in range(GC):
                    dve.tensor_tensor(vl[:, c, E2:ROW].rearrange("p (h e) -> p h e", e=E2),
                                      rs[:, c, E2:ROW].rearrange("p (h e) -> p h e", e=E2),
                                      w[:, c, :].rearrange("p (h o) -> p h o", o=1).broadcast_to([P, E2, E2]), ALU.mult)
                dve.drain()
                for c in range(GC):
                    op = dve.tensor_tensor(R[:, u, c, :, :],
                                           OH[:, u, c, :].rearrange("p (t o) -> p t o", o=1).broadcast_to([P, TM, ROW]),
                                           vl[:, c, :].rearrange("p (o f) -> p o f", o=1).broadcast_to([P, TM, ROW]),
                                           ALU.mult)
                op.then_inc(r_done, 1)

            @block.vector
            def _(dve):
                dve.sem_inc(r_done, NU)
                with dve.Fori(0, BW // STEP) as i:
                    with dve.If(longest > i * STEP):
                        for u in range(NU):
                            weigh(dve, i, u)

            @block.scalar
            def _(act):
                with act.Fori(0, BW // STEP) as i:
                    with act.If(longest > i * STEP):
                        for u in range(NU):
                            act.wait_ge(e_sum, i * NU + u + 1)
                            act.sem_inc(k.turns, 1)
                            act.activation(W[:, u, :, :], W[:, u, :, :], ACT.Exp).then_inc(e_exp, 1)

            @block.tensor
            def _(pe):
                pe.sem_inc(added, NU)
                with pe.Fori(0, BW // STEP) as i:
                    with pe.If(longest > i * STEP):
                        for u in range(NU):
                            pe.wait_ge(r_done, i * NU + u + 1 + NU)
                            pe.sem_inc(k.turns, 1)
                            for c in range(GC):
                                for n in range(2):
                                    mm = pe.matmul(k.PS[:, 4 + n, 0:HI * ROW], OL[:, u, c, :],
                                                   R[:, u, c, n * HI:(n + 1) * HI, :].rearrange("p t f -> p (t f)"),
                                                   start=False, stop=False)
                            mm.then_inc(added, 1)
        fresh(nc, used)
        with nc.Block() as block:
            @block.gpsimd
            def _(pool):
                for s in k.rs_in + k.rd_in:
                    pool.dma_reset(range(s.num, s.num + 1))
                    pool.sem_clear(s)


def gates(nc, k, g):
    with ExitStack() as ctx:
        def sb(name, shape, dt=F32):
            return ctx.enter_context(nc.sbuf_tensor(k.name(name), shape, dt))

        AG = sb("AG", [P, TM, ROW])
        Y = sb("Yg", [P, TM, HE])
        SQ = sb("SQg", [P, TM, HE])
        st = sb("stg", [P, 4, TM])
        SC = sb("SCg", [P, TM, E2])
        RK = sb("RKg", [P, TM, E2])
        GE = sb("GEg", [P, E2, TM])
        GR = sb("GRg", [2 * TM, 2, P])
        LR = sb("LRg", [P, ROW])
        LW = sb("LWg", [P, TM, E2])
        used = sems(nc, ctx, "lr_in", "lw_sum", "lw_exp", "g_var", "g_root", "g_diff", "g_exp", "ge_done", "gt_ready", "gt_done", "gates_out")
        lr_in, lw_sum, lw_exp, g_var, g_root, g_diff, g_exp, ge_done, gt_ready, gt_done, gates_out = used

        def over(ap, n):
            return ap.rearrange("p (t o) -> p t o", o=1).broadcast_to([P, TM, n])

        def row(i):
            return g.rows[:, i, :].rearrange("p (o f) -> p o f", o=1).broadcast_to([P, TM, HE])

        with nc.Block() as block:
            @block.vector
            def _(dve):
                for n in range(2):
                    dve.tensor_copy(AG[:, n * HI:(n + 1) * HI, :],
                                    k.PS[:, 4 + n, 0:HI * ROW].rearrange("p (t f) -> p t f", f=ROW))
                for h in range(E2):
                    dve.tensor_tensor(Y[:, :, h * E2:(h + 1) * E2], g.GS[:, :, E2 + h * E2:E2 + (h + 1) * E2],
                                      g.SELF[:, :, h:h + 1].broadcast_to([P, TM, E2]), ALU.mult)
                dve.drain()
                dve.tensor_tensor(AG[:, :, 0:E2], AG[:, :, 0:E2], g.SELF[:], ALU.add)
                dve.tensor_tensor(AG[:, :, E2:ROW], AG[:, :, E2:ROW], Y[:], ALU.add)
                dve.wait_ge(lr_in, 16)
                dve.tensor_tensor(LW[:], g.GD[:, :, 0:E2], LR[:, 0:E2].rearrange("p (o h) -> p o h", o=1)
                                  .broadcast_to([P, TM, E2]), ALU.add)
                dve.drain()
                dve.scalar_tensor_tensor(LW[:], LW[:], SLOPE, LW[:], ALU.mult, ALU.max)
                dve.drain()
                dve.tensor_tensor(LW[:], LW[:], g.GD[:, :, E2:2 * E2], ALU.add).then_inc(lw_sum, 1)
                dve.wait_ge(lw_exp, 1)
                dve.tensor_tensor(LW[:], LW[:], over(g.HIST[:], E2), ALU.mult)
                dve.drain()
                dve.tensor_tensor(AG[:, :, 0:E2], AG[:, :, 0:E2], LW[:], ALU.add)
                for h in range(E2):
                    for e in range(E2):
                        f = E2 + h * E2 + e
                        dve.scalar_tensor_tensor(AG[:, :, f], LW[:, :, h], LR[:, f:f + 1], AG[:, :, f], ALU.mult, ALU.add)
                dve.drain()
                dve.reciprocal(AG[:, :, 0:E2], AG[:, :, 0:E2])
                dve.drain()
                for h in range(E2):
                    dve.tensor_tensor(Y[:, :, h * E2:(h + 1) * E2], AG[:, :, E2 + h * E2:E2 + (h + 1) * E2],
                                      AG[:, :, h:h + 1].broadcast_to([P, TM, E2]), ALU.mult)
                dve.drain()
                dve.tensor_tensor(Y[:], Y[:], row(0), ALU.add)
                dve.drain()
                mean, var, diff, first = (st[:, i, :] for i in range(4))
                dve.tensor_reduce(mean, Y[:], AX.X, ALU.add)
                dve.drain()
                dve.tensor_scalar(mean, mean, 1.0 / HE, None, ALU.mult)
                dve.drain()
                dve.tensor_tensor(Y[:], Y[:], over(mean, HE), ALU.subtract)
                dve.drain()
                dve.tensor_tensor(SQ[:], Y[:], Y[:], ALU.mult)
                dve.drain()
                dve.tensor_reduce(var, SQ[:], AX.X, ALU.add)
                dve.drain()
                dve.tensor_scalar(var, var, 1.0 / HE, None, ALU.mult).then_inc(g_var, 1)
                dve.wait_ge(g_root, 1)
                dve.reciprocal(var, var)
                dve.drain()
                dve.tensor_tensor(Y[:], Y[:], over(var, HE), ALU.mult)
                dve.drain()
                dve.tensor_tensor(Y[:], Y[:], row(1), ALU.mult)
                dve.drain()
                dve.tensor_tensor(Y[:], Y[:], row(2), ALU.add)
                dve.drain()
                dve.tensor_reduce(SC[:], Y[:].rearrange("p t (h e) -> p t e h", e=E2), AX.X, ALU.add)
                dve.drain()
                dve.tensor_scalar(SC[:], SC[:], 1.0 / E2, None, ALU.mult)
                dve.memset(RK[:], 0.0)
                dve.drain()
                for e in range(E2):
                    for o in range(E2):
                        if o != e:
                            dve.tensor_tensor(diff, SC[:, :, o], SC[:, :, e], ALU.is_ge if o < e else ALU.is_gt)
                            dve.drain()
                            dve.tensor_tensor(RK[:, :, e], RK[:, :, e], diff, ALU.add)
                            dve.drain()
                dve.tensor_reduce(first, SC[:], AX.X, ALU.max)
                dve.tensor_scalar(SQ[:, :, 0:E2], RK[:], 1.0, None, ALU.is_equal)
                dve.tensor_scalar(SQ[:, :, E2:2 * E2], RK[:], 0.0, None, ALU.is_equal)
                dve.drain()
                dve.tensor_tensor(SC[:], SC[:], SQ[:, :, 0:E2], ALU.mult)
                dve.drain()
                dve.tensor_reduce(diff, SC[:], AX.X, ALU.add)
                dve.drain()
                dve.tensor_tensor(diff, diff, first, ALU.subtract).then_inc(g_diff, 1)
                dve.wait_ge(g_exp, 1)
                dve.tensor_scalar(first, diff, 1.0, None, ALU.add)
                dve.drain()
                dve.reciprocal(first, first)
                dve.tensor_tensor(SC[:], SQ[:, :, 0:E2], over(diff, E2), ALU.mult)
                dve.drain()
                dve.tensor_tensor(SC[:], SC[:], SQ[:, :, E2:2 * E2], ALU.add)
                dve.drain()
                dve.tensor_tensor(GE[:].rearrange("p e t -> p t e"), SC[:], over(first, E2), ALU.mult)\
                   .then_inc(ge_done, 1)
                dve.wait_ge(gt_ready, 1)
                dve.tensor_copy(GR[:], k.PS[0:2 * TM, 0:2, 0:P]).then_inc(gt_done, 1)

            @block.scalar
            def _(act):
                act.wait_ge(lw_sum, 1)
                act.activation(LW[:], LW[:], ACT.Exp).then_inc(lw_exp, 1)
                act.wait_ge(g_var, 1)
                act.activation(st[:, 1, :], st[:, 1, :], ACT.Sqrt, bias=k.eps5[:]).then_inc(g_root, 1)
                act.wait_ge(g_diff, 1)
                act.activation(st[:, 2, :], st[:, 2, :], ACT.Exp).then_inc(g_exp, 1)

            @block.tensor
            def _(pe):
                pe.wait_ge(ge_done, 1)
                for n in range(2):
                    mm = pe.transpose(k.PS[0:2 * TM, n, 0:P], GE[:, 2 * n:2 * n + 2, :].rearrange("p e t -> p (e t)"),
                                      k.ident[:])
                mm.then_inc(gt_ready, 1)

            @block.sync
            def _(sp):
                sp.dma_start(LR[:], k.src_dram[M - 1:M, :].broadcast_to([P, ROW])).then_inc(lr_in, 16)
                sp.wait_ge(lr_in, 16)
                sp.wait_ge(gt_done, 1)
                for n in range(2):
                    sp.dma_start(k.gate_dram[n * 2 * TM:(n + 1) * 2 * TM, :], GR[:, n, :]).then_inc(gates_out, 16)
                sp.wait_ge(gates_out, 32)
        fresh(nc, used)


def gated_experts(nc, k, A, b, g):
    with ExitStack() as ctx:
        def sb(name, shape, dt=F32):
            return ctx.enter_context(nc.sbuf_tensor(k.name(name), shape, dt))

        w1, w2, b1, b2 = g.w1, g.w2, g.b1, g.b2
        GB = sb("GB", [P, E2, L])
        G4 = sb("G4", [E2, L])
        used = sems(nc, ctx, "gates_in")
        with nc.Block() as block:
            @block.sync
            def _(sp):
                rows = k.gate_dram.rearrange("(e t) p -> e (t p)", e=E2)[:, bass.ds(b * L, L)]
                sp.dma_start(G4[:], rows).then_inc(used[0], 16)
                for e in range(E2):
                    sp.dma_start(GB[:, e, :], rows[e:e + 1, :].broadcast_to([P, L])).then_inc(used[0], 16)
                sp.wait_ge(used[0], 16 * (1 + E2))
                sp.wait_ge(g.w_loaded, 64)
        fresh(nc, used)

        def bias(pe, c):
            for o in range(KC):
                pe.matmul(k.PS[:, 4 + o, :T], b2[:, o * P:(o + 1) * P], G4[:, bass.ds(c * T, T)], start=True, stop=False)

        def add(dve, c):
            x = k.X[:, :, bass.ds(b * L + c * T, T)]
            return dve.tensor_tensor(x, x, k.PS[:, 4:4 + KC, :T], ALU.add)

        two_layer(nc, ctx, k, b, lambda i, c: g.NN[:, i, bass.ds(b * L + c * T, T)], lambda i, m: w1[:, i, m * P:(m + 1) * P], lambda m: b1[:, m:m + 1],
                  lambda m, o: w2[:, m, o * P:(o + 1) * P],
                  gate=lambda m, c: GB[:, m // E2, bass.ds(c * T, T)], first=bias, last=add)




def transposed_image(nc, k, dst):
    with ExitStack() as own:
        used = sems(nc, own, "t_ready", "t_done")
        t_ready, t_done = used
        with nc.Block() as block:
            @block.tensor
            def _(pe):
                for t in range(LT):
                    if t >= 4:
                        pe.wait_ge(t_done, t - 3)
                    for i in range(KC):
                        mm = pe.transpose(k.PS[:, t % 4, i * P:(i + 1) * P], k.N[:, i, t * P:(t + 1) * P], k.ident[:])
                    mm.then_inc(t_ready, 1)

            @block.vector
            def _(dve):
                for t in range(LT):
                    dve.wait_ge(t_ready, t + 1)
                    dve.tensor_copy(dst[:, t, :], k.PS[:, t % 4, 0:C]).then_inc(t_done, 1)
        fresh(nc, used)


def sigmoid_attention(nc, k, A, b):
    norm_image(nc, k, b, k.eps5)
    with ExitStack() as ctx:
        def sb(name, shape, dt=F32):
            return ctx.enter_context(nc.sbuf_tensor(k.name(name), shape, dt))

        w_q = sb("w_q", [P, KC, C])
        QT = sb("QT3", [P, KC, L])
        XT = sb("XT3", [P, LT, C])
        NA = 3
        AT = sb("AT", [P, NA, T])
        transposed_image(nc, k, XT)
        used = sems(nc, ctx, "l3_loaded", "q3_ready", "q3_done")
        l3_loaded, q3_ready, q3_done = used
        with nc.Block() as block:
            @block.sync
            def _(sp):
                sp.dma_start(w_q[:], A["l3_w_q"]).then_inc(l3_loaded, 16)
                sp.wait_ge(l3_loaded, 16)

            @block.tensor
            def _(pe):
                pe.wait_ge(l3_loaded, 16)
                for n in range(KC * NT):
                    m, c = n // NT, n % NT
                    if n >= 4:
                        pe.wait_ge(q3_done, n - 3)
                    for i in range(KC):
                        mm = pe.matmul(k.PS[:, n % 4, :T], w_q[:, i, m * P:(m + 1) * P], k.N[:, i, c * T:(c + 1) * T],
                                       start=(i == 0), stop=(i == KC - 1))
                    mm.then_inc(q3_ready, 1)

            @block.scalar
            def _(act):
                for n in range(KC * NT):
                    m, c = n // NT, n % NT
                    act.wait_ge(q3_ready, n + 1)
                    act.activation(QT[:, m, c * T:(c + 1) * T], k.PS[:, n % 4, :T], ACT.Copy).then_inc(q3_done, 1)
        fresh(nc, used)

        used = sems(nc, ctx, "sc_ready", "att_done", "att_used", "val_ready", "val_used")
        sc_ready, att_done, att_used, val_ready, val_used = used
        with nc.Block() as block:
            @block.tensor
            def _(pe):
                pe.sem_inc(att_used, NA)
                with pe.Fori(0, NT) as c:
                    for s in range(LT + 2):
                        if s < LT:
                            pe.wait_ge(att_done, c * LT + s + 1)
                            pe.sem_inc(k.turns, 1)
                            for i in range(KC):
                                mm = pe.matmul(k.PS[:, s % NA, :T], k.N[:, i, s * P:(s + 1) * P],
                                               QT[:, i, bass.ds(c * T, T)], start=(i == 0), stop=(i == KC - 1))
                            mm.then_inc(sc_ready, 1)
                        if s >= 2:
                            m = s - 2
                            pe.wait_ge(att_done, c * LT + m + 1 + NA)
                            pe.sem_inc(k.turns, 1)
                            if m == 0:
                                pe.wait_ge(val_used, c + 1)
                                pe.sem_inc(k.turns, 1)
                            for o in range(KC):
                                mm = pe.matmul(k.PS[:, 4 + o, :T], XT[:, m, o * P:(o + 1) * P], AT[:, m % NA, :],
                                               start=(m == 0), stop=(m == LT - 1))
                            mm.then_inc(att_used, 1)
                    pe.drain().then_inc(val_ready, 1)

            @block.scalar
            def _(act):
                act.sem_inc(att_done, NA)
                with act.Fori(0, NT) as c:
                    for m in range(LT):
                        act.wait_ge(sc_ready, c * LT + m + 1)
                        act.sem_inc(k.turns, 1)
                        act.wait_ge(att_used, c * LT + m + 1)
                        act.sem_inc(k.turns, 1)
                        act.activation(AT[:, m % NA, :], k.PS[:, m % NA, :T], ACT.Sigmoid).then_inc(att_done, 1)

            @block.vector
            def _(dve):
                dve.sem_inc(val_used, 1)
                with dve.Fori(0, NT) as c:
                    dve.wait_ge(val_ready, c + 1)
                    dve.sem_inc(k.turns, 1)
                    x = k.X[:, :, bass.ds(b * L + c * T, T)]
                    dve.tensor_tensor(x, x, k.PS[:, 4:4 + KC, :T], ALU.add).then_inc(val_used, 1)
        fresh(nc, used)


NE = 8
F = 4 * C
FBE = F // P
CAP = (5 * M // 4 + NE - 1) // NE
RT = 120
NR = CAP // RT
CH = CAP // 2
END = float(NE * CAP + 1)
NO_SLOT = 8192.0
ZN = 9
ZW = NE * CAP * C // (P * ZN)


def clear_buffer(nc, k, zero):
    with nc.Block() as block:
        @block.vector
        def _(dve):
            dve.memset(zero[:], 0.0).then_inc(k.zeroed, 1)

        @block.sync
        def _(sp):
            sp.wait_ge(k.zeroed, 1)
            for i in range(ZN):
                sp.dma_start(k.buf_dram.rearrange("(i p r) c -> i p (r c)", i=ZN, p=P)[i], zero[:])\
                  .then_inc(k.buf_clear, 16)


def route_image(nc, k, A, b, st):
    norm_image(nc, k, b, k.eps5)
    with ExitStack() as ctx:
        def sb(name, shape, dt=F32):
            return ctx.enter_context(nc.sbuf_tensor(k.name(name), shape, dt))

        XT = sb("XT5", [P, LT, C])
        transposed_image(nc, k, XT)
        LG = sb("LG", [P, LT, NE])
        OH = sb("OH", [P, LT, NE])
        POS = sb("POS", [P, LT, NE])
        red = sb("red", [P, 6, LT])
        SI = sb("SI", [P, LT], I32)
        used = sems(nc, ctx, "lg_ready", "lg_shifted", "lg_exp", "oh_done", "count_ready", "slot_done")
        lg_ready, lg_shifted, lg_exp, oh_done, count_ready, slot_done = used

        def wide(ap):
            return ap.rearrange("p (t o) -> p t o", o=1).broadcast_to([P, LT, NE])

        with nc.Block() as block:
            @block.tensor
            def _(pe):
                for t in range(LT):
                    for i in range(KC):
                        mm = pe.matmul(k.PS[:, 0, t * NE:(t + 1) * NE], k.N[:, i, t * P:(t + 1) * P], st.gate_w[:, i, :],
                                       start=(i == 0), stop=(i == KC - 1))
                mm.then_inc(lg_ready, 1)
                pe.wait_ge(oh_done, 1)
                oh = OH[:].rearrange("p t e -> p (t e)")
                pe.matmul(k.PS[:, 1, 0:LT * NE], st.tri[:], oh, start=True, stop=True)
                pe.matmul(k.PS[:, 2, 0:LT * NE], st.ones[:], oh, start=True, stop=True).then_inc(count_ready, 1)

            @block.scalar
            def _(act):
                act.wait_ge(lg_shifted, 1)
                act.activation(LG[:], LG[:], ACT.Exp).then_inc(lg_exp, 1)

            @block.vector
            def _(dve):
                mx, total, prb, pos, base, kept = (red[:, i, :] for i in range(6))
                dve.wait_ge(lg_ready, 1)
                logits = k.PS[:, 0, 0:LT * NE].rearrange("p (t e) -> p t e", e=NE)
                dve.tensor_tensor(LG[:], logits,
                                  st.gate_b[:].rearrange("p (o e) -> p o e", o=1).broadcast_to([P, LT, NE]), ALU.add)
                dve.drain()
                dve.tensor_reduce(mx, LG[:], AX.X, ALU.max)
                dve.drain()
                dve.tensor_tensor(LG[:], LG[:], wide(mx), ALU.subtract).then_inc(lg_shifted, 1)
                dve.wait_ge(lg_exp, 1)
                dve.tensor_reduce(total, LG[:], AX.X, ALU.add)
                dve.drain()
                dve.reciprocal(total, total)
                dve.drain()
                dve.tensor_tensor(LG[:], LG[:], wide(total), ALU.mult)
                dve.drain()
                dve.tensor_reduce(prb, LG[:], AX.X, ALU.max)
                dve.drain()
                dve.tensor_tensor(OH[:], LG[:], wide(prb), ALU.is_equal)
                dve.drain()
                key = st.key[:].rearrange("p (o e) -> p o e", o=1).broadcast_to([P, LT, NE])
                dve.tensor_tensor(POS[:], OH[:], key, ALU.mult)
                dve.drain()
                dve.tensor_reduce(base, POS[:], AX.X, ALU.max)
                dve.drain()
                dve.tensor_tensor(OH[:], POS[:], wide(base), ALU.is_equal).then_inc(oh_done, 1)
                dve.drain()
                dve.tensor_scalar(base, base, -1.0, END, ALU.mult, ALU.add)
                dve.wait_ge(count_ready, 1)
                tot = k.PS[:, 2, 0:LT * NE].rearrange("p (t e) -> p t e", e=NE)
                for e in range(NE):
                    dve.tensor_tensor_scan(st.PF[:, 1:LT + 1, e], tot[:, :, e], OH[:, :, e], st.PF[:, 0, e:e + 1],
                                           ALU.add, ALU.max)
                dve.drain()
                dve.tensor_tensor(POS[:], k.PS[:, 1, 0:LT * NE].rearrange("p (t e) -> p t e", e=NE),
                                  st.PF[:, 0:LT, :], ALU.add)
                dve.drain()
                dve.tensor_copy(st.PF[:, 0, :], st.PF[:, LT, :])
                dve.tensor_tensor(POS[:], POS[:], OH[:], ALU.mult)
                dve.drain()
                dve.tensor_reduce(pos, POS[:], AX.X, ALU.add)
                dve.drain()
                dve.tensor_scalar(pos, pos, -1.0, None, ALU.add)
                dve.drain()
                dve.tensor_scalar(kept, pos, float(CAP), None, ALU.is_lt)
                dve.drain()
                dve.tensor_tensor(st.WT[:, bass.ds(b * LT, LT)], prb, kept, ALU.mult)
                dve.tensor_scalar(kept, kept, -NO_SLOT, NO_SLOT, ALU.mult, ALU.add)
                dve.tensor_scalar(total, pos, float(CAP - 1), None, ALU.min)
                dve.drain()
                dve.tensor_tensor(kept, kept, pos, ALU.add)
                dve.tensor_tensor(st.GI[:, bass.ds(b * LT, LT)], total, base, ALU.add)
                dve.drain()
                dve.tensor_tensor(SI[:], kept, base, ALU.add).then_inc(slot_done, 1)

            @block.gpsimd
            def _(pool):
                pool.wait_ge(slot_done, 1)
                for t in range(LT):
                    pool.indirect_dma_start(
                        out=k.buf_dram, out_offset=bass.IndirectOffsetOnAxis(ap=SI[:, t:t + 1], axis=0),
                        in_=XT[:, t, :], in_offset=None, bounds_check=NE * CAP - 1, oob_is_err=False)\
                        .then_inc(k.row_sent, 16)
                pool.wait_ge(k.row_sent, (b + 1) * (16 * LT))
                pool.sem_inc(k.turns, 1)
        fresh(nc, used)


def capacity_mixture(nc, k, A):
    with ExitStack() as top:
        st = Core()

        def keep(name, shape, dt=F32):
            return top.enter_context(nc.sbuf_tensor(k.name(name), shape, dt))

        st.gate_w = keep("gate_w", [P, KC, NE])
        st.gate_b = keep("gate_b", [P, NE])
        st.key = keep("key", [P, NE])
        st.tri = keep("tri", [P, P])
        st.ones = keep("ones", [P, P])
        st.PF = keep("PF", [P, LT + 1, NE])
        st.GI = keep("GI", [P, NB * LT], I32)
        st.WT = keep("WT", [P, NB * LT])
        used = sems(nc, top, "gate_in")
        with nc.Block() as block:
            @block.vector
            def _(dve):
                dve.memset(st.PF[:, 0, :], 0.0)
                dve.memset(st.ones[:], 1.0)

            @block.sync
            def _(sp):
                sp.dma_start(st.gate_w[:], A["l3_gate_w"]).then_inc(used[0], 16)
                sp.dma_start(st.tri[:], A["c_tri"]).then_inc(used[0], 16)
                sp.dma_start(st.gate_b[:], A["l3_gate_b"].broadcast_to([P, NE])).then_inc(used[0], 16)
                sp.dma_start(st.key[:], A["c_key"].broadcast_to([P, NE])).then_inc(used[0], 16)
                sp.wait_ge(used[0], 64)
                sp.wait_ge(k.buf_clear, 16 * ZN)
        fresh(nc, used)
        with nc.Fori(0, NB) as b:
            route_image(nc, k, A, b, st)
        with ExitStack() as own:
            experts(nc, own, k, A)
        combine(nc, k, st)


def experts(nc, ctx, k, A):
    def sb(name, shape, dt=F32):
        return ctx.enter_context(nc.sbuf_tensor(k.name(name), shape, dt))

    w1 = sb("ew1", [P, 2, KC, F])
    w2 = sb("ew2", [P, 2, FBE, C])
    b1 = sb("eb1", [P, 2, FBE])
    b2 = sb("eb2", [P, 2, C])
    XR = sb("XR", [RT, 2, NR, C])
    XB = sb("XB", [P, KC, CAP])
    H = sb("HE", [P, FBE, CAP])
    YB = sb("YB", [RT, 2, NR, C])
    used = sems(nc, ctx, "e_loaded0", "e_loaded1", "rows_in0", "rows_in1", "x_ready", "x_done", "h5_ready", "h5_done",
                "y_ready", "y_done", "y_sent0", "y_sent1", "e_done")
    (e_loaded0, e_loaded1, rows_in0, rows_in1, x_ready, x_done, h5_ready, h5_done,
     y_ready, y_done, y_sent0, y_sent1, e_done) = used
    e_loaded, rows_in, y_sent = (e_loaded0, e_loaded1), (rows_in0, rows_in1), (y_sent0, y_sent1)
    NH = FBE * 2
    with nc.Block() as block:
        @block.sync
        def _(sp):
            with sp.Fori(0, NE // 2) as i:
                for u in range(2):
                    e = i * 2 + u
                    sp.wait_ge(e_done, i * 2 + u + 1)
                    sp.sem_inc(k.turns, 1)
                    sp.dma_start(XR[:, u, :, :], k.buf_dram[bass.ds(e * CAP, CAP), :].rearrange("(t p) c -> p t c", p=RT))\
                      .then_inc(rows_in[u], 16)
                    sp.dma_start(w1[:, u, :, :], A["l3_w1"][bass.ds(e, 1)].rearrange("o p i n -> (o p) i n"))\
                      .then_inc(e_loaded[u], 16)
                    sp.dma_start(w2[:, u, :, :], A["l3_w2"][bass.ds(e, 1)].rearrange("o p i n -> (o p) i n"))\
                      .then_inc(e_loaded[u], 16)
                    sp.dma_start(b1[:, u, :], A["l3_b1"][bass.ds(e, 1)].rearrange("o p i -> (o p) i"))\
                      .then_inc(e_loaded[u], 16)
                    sp.dma_start(b2[:, u, :], A["l3_b2"][bass.ds(e, 1), :].broadcast_to([P, C]))\
                      .then_inc(e_loaded[u], 16)

        @block.tensor
        def _(pe):
            with pe.Fori(0, NE // 2) as i:
                for u in range(2):
                    pe.wait_ge(rows_in[u], i * 16 + 16)
                    pe.sem_inc(k.turns, 1)
                    for t in range(NR):
                        if t >= 2:
                            pe.wait_ge(x_done, i * (2 * NR) + u * NR + t - 1)
                            pe.sem_inc(k.turns, 1)
                        for c in range(KC):
                            mm = pe.transpose(k.PS[:, t % 2, c * RT:(c + 1) * RT], XR[:, u, t, c * P:(c + 1) * P],
                                              k.ident[0:RT, 0:RT])
                        mm.then_inc(x_ready, 1)
                    pe.wait_ge(x_done, i * (2 * NR) + u * NR + NR)
                    pe.sem_inc(k.turns, 1)
                    pe.wait_ge(e_loaded[u], i * 64 + 64)
                    pe.sem_inc(k.turns, 1)
                    for n in range(NH):
                        f, c = n // 2, n % 2
                        if n >= 3:
                            pe.wait_ge(h5_done, i * (2 * NH) + u * NH + n - 2)
                            pe.sem_inc(k.turns, 1)
                        for o in range(KC):
                            mm = pe.matmul(k.PS[:, 2 + n % 3, :CH], w1[:, u, o, f * P:(f + 1) * P],
                                           XB[:, o, c * CH:(c + 1) * CH], start=(o == 0), stop=(o == KC - 1))
                        mm.then_inc(h5_ready, 1)
                    pe.wait_ge(h5_done, i * (2 * NH) + u * NH + NH)
                    pe.sem_inc(k.turns, 1)
                    for t in range(NR):
                        pe.wait_ge(y_done, i * (2 * NR) + u * NR + t + 1)
                        pe.sem_inc(k.turns, 1)
                        for f in range(FBE):
                            mm = pe.matmul(k.PS[0:RT, 6 + t % 2, :C], H[:, f, t * RT:(t + 1) * RT], w2[:, u, f, :],
                                           start=(f == 0), stop=(f == FBE - 1))
                        mm.then_inc(y_ready, 1)

        @block.scalar
        def _(act):
            for u in range(2):
                act.sem_inc(y_sent[u], 1)
            with act.Fori(0, NE // 2) as i:
                for u in range(2):
                    act.wait_ge(e_loaded[u], i * 64 + 64)
                    act.sem_inc(k.turns, 1)
                    for n in range(NH):
                        f, c = n // 2, n % 2
                        act.wait_ge(h5_ready, i * (2 * NH) + u * NH + n + 1)
                        act.sem_inc(k.turns, 1)
                        act.activation(H[:, f, c * CH:(c + 1) * CH], k.PS[:, 2 + n % 3, :CH], ACT.Relu,
                                       bias=b1[:, u, f:f + 1]).then_inc(h5_done, 1)
                    for t in range(NR):
                        act.wait_ge(y_done, i * (2 * NR) + u * NR + t + 1 + 2)
                        act.sem_inc(k.turns, 1)
                        act.dma_start(k.y_dram[bass.ds((i * 2 + u) * CAP + t * RT, RT), :], YB[:, u, t, :])\
                           .then_inc(y_sent[u], 16)
            for u in range(2):
                act.wait_ge(y_sent[u], 16 * NR * (NE // 2) + 1)

        @block.vector
        def _(dve):
            dve.sem_inc(y_done, 2)
            dve.sem_inc(e_done, 2)
            with dve.Fori(0, NE // 2) as i:
                for u in range(2):
                    for t in range(NR):
                        dve.wait_ge(x_ready, i * (2 * NR) + u * NR + t + 1)
                        dve.sem_inc(k.turns, 1)
                        dve.tensor_copy(XB[:, :, t * RT:(t + 1) * RT],
                                        k.PS[:, t % 2, 0:KC * RT].rearrange("p (i r) -> p i r", i=KC)).then_inc(x_done, 1)
                    dve.wait_ge(e_loaded[u], i * 64 + 64)
                    dve.sem_inc(k.turns, 1)
                    dve.wait_ge(y_sent[u], i * (16 * NR) + 1)
                    dve.sem_inc(k.turns, 1)
                    for t in range(NR):
                        dve.wait_ge(y_ready, i * (2 * NR) + u * NR + t + 1)
                        dve.sem_inc(k.turns, 1)
                        dve.tensor_tensor(YB[:, u, t, :], k.PS[0:RT, 6 + t % 2, :C], b2[0:RT, u, :], ALU.add)\
                           .then_inc(y_done, 1)
                    dve.drain().then_inc(e_done, 1)
    fresh(nc, used)


FMAX = float(np.finfo(np.float32).max)
GT = 4
NG = TM // GT


def combine(nc, k, st):
    with ExitStack() as ctx:
        def sb(name, shape, dt=F32):
            return ctx.enter_context(nc.sbuf_tensor(k.name(name), shape, dt))

        YG = sb("YG", [P, TM, C])
        OK = sb("OK", [P, 2, GT, C])
        MK = sb("MK", [P, 2, GT, C], I32)
        CL = sb("CL", [P, GT, C])
        AB = sb("AB", [P, 2, GT, C])
        used = sems(nc, ctx, "y_weighed", "y_clean", "yt_ready", "yt_added")
        y_weighed, y_clean, yt_ready, yt_added = used

        def add(dve, n):
            dve.wait_ge(yt_ready, n + 1)
            x = k.X[:, :, n * GT * P:(n + 1) * GT * P].rearrange("p i (t n) -> p t i n", n=P)
            y = k.PS[:, 2 * (n % 2):2 * (n % 2) + 2, :].rearrange("p b (t i n) -> p (b t) i n", i=KC, n=P)
            for h in range(KC):
                op = dve.tensor_tensor(x[:, :, h, :], x[:, :, h, :], y[:, :, h, :], ALU.add)
            op.then_inc(yt_added, 1)

        with nc.Block() as block:
            @block.gpsimd
            def _(pool):
                for n in range(NG):
                    for t in range(n * GT, (n + 1) * GT):
                        pool.indirect_dma_start(
                            out=YG[:, t, :], out_offset=None, in_=k.y_dram,
                            in_offset=bass.IndirectOffsetOnAxis(ap=st.GI[:, t:t + 1], axis=0),
                            bounds_check=NE * CAP - 1, oob_is_err=False).then_inc(k.row_in[n], 16)

            @block.scalar
            def _(act):
                for n in range(NG):
                    act.wait_ge(k.row_in[n], 16 * GT)
                    for t in range(n * GT, (n + 1) * GT):
                        act.activation(YG[:, t, :], YG[:, t, :], ACT.Copy, scale=st.WT[:, t:t + 1])
                    if n >= 2:
                        act.wait_ge(y_clean, n - 1)
                    act.drain()
                    act.activation(AB[:, n % 2, :, :], YG[:, n * GT:(n + 1) * GT, :], ACT.Abs).then_inc(y_weighed, 1)

            @block.vector
            def _(dve):
                for n in range(NG):
                    y, ok = YG[:, n * GT:(n + 1) * GT, :], OK[:, n % 2, :, :]
                    if n >= 2:
                        dve.wait_ge(yt_ready, n - 1)
                    dve.memset(ok, 0.0)
                    dve.wait_ge(y_weighed, n + 1)
                    dve.tensor_tensor(MK[:, 0, :, :], y, y, ALU.is_equal)
                    dve.tensor_scalar(MK[:, 1, :, :], AB[:, n % 2, :, :], FMAX, None, ALU.is_gt)
                    dve.tensor_scalar(CL[:], y, 1e4, -1e4, ALU.min, ALU.max)
                    dve.drain()
                    dve.copy_predicated(ok, MK[:, 0, :, :], y)
                    dve.drain()
                    dve.copy_predicated(ok, MK[:, 1, :, :], CL[:]).then_inc(y_clean, 1)
                    dve.drain()
                    if n >= 1:
                        add(dve, n - 1)
                add(dve, NG - 1)

            @block.tensor
            def _(pe):
                for n in range(NG):
                    pe.wait_ge(y_clean, n + 1)
                    if n >= 2:
                        pe.wait_ge(yt_added, n - 1)
                    for t in range(GT):
                        for i in range(KC):
                            at = (t % 2) * C + i * P
                            mm = pe.transpose(k.PS[:, 2 * (n % 2) + t // 2, at:at + P],
                                              OK[:, n % 2, t, i * P:(i + 1) * P], k.ident[:])
                    mm.then_inc(yt_ready, 1)
        fresh(nc, used)


def build(nc, A, out, start=0, upto=99):
    with ExitStack() as ctx:
        k = Core()
        k.serial = 0

        def name(n):
            k.serial += 1
            return f"{n}_{k.serial}"

        k.name = name
        k.X = ctx.enter_context(nc.sbuf_tensor("X", [P, KC, M], F32))
        k.N = ctx.enter_context(nc.sbuf_tensor("N", [P, KC, L], F32))
        k.ident = ctx.enter_context(nc.sbuf_tensor("ident", [P, P], F32))
        k.mean_w = ctx.enter_context(nc.sbuf_tensor("mean_w", [P, P], F32))
        k.group_w = ctx.enter_context(nc.sbuf_tensor("group_w", [P, P], F32))
        k.zeros = ctx.enter_context(nc.sbuf_tensor("zeros", [1, BANK], BF16))
        k.eps5 = ctx.enter_context(nc.sbuf_tensor("eps5", [P, 1], F32))
        k.cnt = ctx.enter_context(nc.sbuf_tensor("cnt", [P, NU], F32))
        k.PS = ctx.enter_context(nc.psum_tensor("PS", [P, 8, BANK], F32))
        k.proj_dram = nc.dram_tensor("proj_dram", [DR + 2 * DS, L], F32, kind="Internal").ap()
        k.edges_dram = nc.dram_tensor("edges_dram", [P, EC], I32, kind="Internal").ap()
        k.idx_dram = nc.dram_tensor("idx_dram", [2, P, EC], I32, kind="Internal").ap()
        k.dig_dram = nc.dram_tensor("dig_dram", [2, P, EC], F32, kind="Internal").ap()
        k.src_dram = nc.dram_tensor("src_dram", [M, ROW], F32, kind="Internal").ap()
        k.dst_dram = nc.dram_tensor("dst_dram", [M, 2 * E2], F32, kind="Internal").ap()
        k.gate_dram = nc.dram_tensor("gate_dram", [E2 * TM, P], F32, kind="Internal").ap()
        k.buf_dram = nc.dram_tensor("buf_dram", [NE * CAP, C], F32, kind="Internal").ap()
        k.y_dram = nc.dram_tensor("y_dram", [NE * CAP, C], F32, kind="Internal").ap()
        k.row_sent = ctx.enter_context(nc.semaphore("row_sent"))
        k.row_in = [ctx.enter_context(nc.semaphore(f"row_in{n}")) for n in range(NG)]
        k.zeroed = ctx.enter_context(nc.semaphore("zeroed"))
        k.buf_clear = ctx.enter_context(nc.semaphore("buf_clear"))
        k.turns = ctx.enter_context(nc.semaphore("turns"))
        k.rs_in = [ctx.enter_context(nc.semaphore(f"rs_in{u}")) for u in range(NU)]
        k.rd_in = [ctx.enter_context(nc.semaphore(f"rd_in{u}")) for u in range(NU)]
        with nc.Block() as block:
            @block.vector
            def _(dve):
                dve.memset(k.zeros[:], 0.0)
                dve.memset(k.eps5[:], 1e-5)
        load_constants(nc, ctx, k, A)
        if start <= 0 <= upto:
            with nc.Fori(0, NB) as b:
                mamba(nc, k, A, b)
        if start <= 1 <= upto:
            with nc.Fori(0, NB) as b:
                linear_attention_block(nc, k, A, b)
        if start <= 2 <= upto:
            with nc.Fori(0, NB) as b:
                softmax_attention(nc, k, A, b)
        if start <= 3 <= upto:
            graph_mixture(nc, k, A)
        zero = ctx.enter_context(nc.sbuf_tensor("zero", [P, ZW], F32))
        clear_buffer(nc, k, zero)
        if start <= 4 <= upto:
            with nc.Fori(0, NB) as b:
                sigmoid_attention(nc, k, A, b)
        if start <= 5 <= upto:
            capacity_mixture(nc, k, A)
        with ExitStack() as own:
            (stored,) = sems(nc, own, "stored")
            with nc.Block() as block:
                @block.sync
                def _(sp):
                    for b in range(NB):
                        sp.dma_start(out[b].rearrange("(k p) n -> p k n", p=P), k.X[:, :, b * L:(b + 1) * L])\
                          .then_inc(stored, 16)
                    sp.wait_ge(stored, 16 * NB)


def layout(inputs):
    a = {n: np.asarray(v) for n, v in inputs.items()}
    A = {"x": a["x"].reshape(NB, C, L)}

    def cols(w, kc):
        return w.reshape(kc, P, -1).transpose(1, 0, 2)

    A["c_ident"] = np.eye(P, dtype=np.float32)
    A["c_mean"] = np.full((P, P), 1.0 / C, np.float32)
    A["c_group"] = np.kron(np.eye(P // 8), np.full((8, 8), 1.0 / 8)).astype(np.float32)
    inv = (np.float32(1.0) / np.power(np.float32(10000.0), np.arange(0, C, 2, dtype=np.float32) / np.float32(C)))
    ang = (np.arange(L, dtype=np.float32)[:, None] * inv.astype(np.float32)[None, :]).astype(np.float32)
    pos = np.concatenate([np.sin(ang.astype(np.float64)), np.cos(ang.astype(np.float64))], -1).astype(np.float32)
    A["c_pos"] = cols(pos.T, KC)
    A["l0_ln"] = np.stack([a["L0_conv_ln_g"], a["L0_conv_ln_b"]], -1).reshape(KC, P, 2).transpose(1, 0, 2)
    A["L0_conv_pos_scale"] = a["L0_conv_pos_scale"]
    A["l0_w_in"] = cols(a["L0_conv_in_proj_w"].T, KC)
    A["l0_w_out"] = cols(a["L0_conv_out_proj_w"].T, JD)
    for d in "fb":
        A["l0_conv_w_" + d] = cols(a["L0_conv_conv_w_" + d], JD)
        A["l0_vec_" + d] = cols(np.stack([a["L0_conv_conv_b_" + d], a["L0_conv_dtproj_b_" + d], a["L0_conv_D_" + d]], -1), JD)
        A["l0_alog_" + d] = cols(a["L0_conv_A_log_" + d], JD)
        A["l0_w_x_" + d] = cols(a["L0_conv_xproj_w_" + d].T, JD)
        A["l0_w_dt_" + d] = a["L0_conv_dtproj_w_" + d].T
    A["c_head"] = np.kron(np.eye(P // 32), np.full((32, 32), 32.0 ** -0.5)).astype(np.float32)
    A["l1_vec"] = np.stack([a["L1_conv_bqkv"][:C], a["L1_conv_dw_b"], a["L1_conv_bproj"]]
                           + [a[f"L1_conv_bn{w}_{s}"] for w in "12" for s in "gbmv"] + [a["L1_conv_bfc2"]], -1)\
        .reshape(KC, P, 12).transpose(1, 0, 2)
    A["l1_bkv"] = a["L1_conv_bqkv"][C:].reshape(1, 2 * C)
    A["l1_alpha"] = np.stack([a["L1_conv_alpha1"], a["L1_conv_alpha2"]], -1).reshape(1, 2)
    A["l1_w_qkv"] = cols(a["L1_conv_Wqkv"], KC)
    A["l1_w_proj"] = cols(a["L1_conv_Wproj"], KC)
    A["l1_dw"] = cols(a["L1_conv_dw_w"].reshape(C, TAPS * TAPS), KC)
    A["l1_w_fc1"] = cols(a["L1_conv_Wfc1"], KC)
    A["l1_w_fc2"] = cols(a["L1_conv_Wfc2"], NM)
    A["l1_b_fc1"] = a["L1_conv_bfc1"].reshape(NM, P).T
    A["l2_w_e"] = a["L2_attn_W_embed"].reshape(NH, FB, P, C).transpose(0, 2, 1, 3)
    A["l2_b_e"] = a["L2_attn_b_embed"].reshape(NH, FB, P).transpose(0, 2, 1)
    A["l2_w_out"] = cols(a["L2_attn_W_out"].T, FB)
    A["l2_b_out"] = a["L2_attn_b_out"].reshape(KC, P).T
    A["edges"] = a["L2_ffn_edge_index"]
    A["l2_w_gat"] = cols(a["L2_ffn_W_gat"], KC)
    A["l2_att"] = np.stack([a["L2_ffn_att_src"], a["L2_ffn_att_dst"]]).reshape(1, 2, HE)
    A["l2_g_rows"] = np.stack([a["L2_ffn_b_gat"], a["L2_ffn_ln_gamma"], a["L2_ffn_ln_beta"]]).reshape(1, 3, HE)
    A["c_iota"] = np.arange(BW, dtype=np.float32).reshape(1, BW)
    A["l2_w1"] = cols(a["L2_ffn_W1"].transpose(1, 0, 2).reshape(C, E2 * F2), KC)
    A["l2_w2"] = cols(a["L2_ffn_W2"].reshape(E2 * F2, C), NM)
    A["l2_b1"] = a["L2_ffn_b1"].reshape(NM, P).T
    A["l2_b2"] = a["L2_ffn_b2"]
    A["l3_w_q"] = cols(a["L3_attn_q_weight"], KC)
    A["c_tri"] = np.triu(np.ones((P, P), np.float32))
    A["c_key"] = (END - np.arange(NE, dtype=np.float32) * CAP).astype(np.float32).reshape(1, NE)
    A["l3_gate_w"] = cols(a["L3_ffn_gate_w"], KC)
    A["l3_gate_b"] = a["L3_ffn_gate_b"].reshape(1, NE)
    A["l3_w1"] = a["L3_ffn_w1"].reshape(NE, KC, P, F).transpose(0, 2, 1, 3)
    A["l3_w2"] = a["L3_ffn_w2"].reshape(NE, FBE, P, C).transpose(0, 2, 1, 3)
    A["l3_b1"] = a["L3_ffn_b1"].reshape(NE, FBE, P).transpose(0, 2, 1)
    A["l3_b2"] = a["L3_ffn_b2"]
    return {n: np.ascontiguousarray(v) for n, v in A.items()}


def kernel(**inputs):
    import concourse.bacc as bacc
    from concourse.bass_utils import run_bass_kernel_spmd

    nc = bacc.Bacc("TRN2", target_bir_lowering=False, num_devices=1)
    arrays = layout(inputs)
    A = {n: nc.dram_tensor(f"in_{n}", v.shape, mybir.dt.from_np(v.dtype), kind="ExternalInput").ap()
         for n, v in arrays.items()}
    out = nc.dram_tensor("out_0", (NB, C, L), F32, kind="ExternalOutput").ap()
    build(nc, A, out)
    r = run_bass_kernel_spmd(nc, [{f"in_{n}": v for n, v in arrays.items()}], core_ids=[0])
    return np.asarray(r.results[0]["out_0"]).reshape(NB, C, HW, HW)
```
